# Optimizing a Trainium2 kernel written in Bass

```python
import numpy as np
import jax
import jax.numpy as jnp

def _softmax(x, axis=-1):
    return jax.nn.softmax(x, axis=axis)

def _gelu(x):
    return jax.nn.gelu(x, approximate=True)

def _silu(x):
    return jax.nn.silu(x)

def _sigmoid(x):
    return jax.nn.sigmoid(x)

def _layernorm(x, axis=-1, eps=1e-05):
    m = jnp.mean(x, axis=axis, keepdims=True)
    v = jnp.var(x, axis=axis, keepdims=True)
    return (x - m) / jnp.sqrt(v + eps)

def _scatter_add(tgt, idx, src, axis=0):
    return tgt.at[idx].add(src)

def _segment_sum(src, seg, n):
    return jax.ops.segment_sum(src, seg, n)
kernel_name = 'mk_seq_postln_d2_jaxref_r8_de2fbe'

def setup_inputs(seed: int=0):
    np.random.seed(seed)
    _w = jnp.asarray

    def _L0_attn_setup():
        import jax, jax.numpy as jnp
        import numpy as np
        EMBED_DIM = 128
        NUM_HEADS = 16
        HEAD_DIM = EMBED_DIM // NUM_HEADS
        ALPHA = 1.0
        key = jax.random.key(seed)
        ks = jax.random.split(key, 9)
        B, T, D = (2, 256, EMBED_DIM)
        s = 1.0 / np.sqrt(D)
        return {'x': jax.random.normal(ks[0], (B, T, D), dtype=jnp.float32), 'Wq': jax.random.uniform(ks[1], (D, D), jnp.float32, -s, s), 'bq': jax.random.uniform(ks[2], (D,), jnp.float32, -s, s), 'Wk': jax.random.uniform(ks[3], (D, D), jnp.float32, -s, s), 'bk': jax.random.uniform(ks[4], (D,), jnp.float32, -s, s), 'Wv': jax.random.uniform(ks[5], (D, D), jnp.float32, -s, s), 'bv': jax.random.uniform(ks[6], (D,), jnp.float32, -s, s), 'Wo': jax.random.uniform(ks[7], (D, D), jnp.float32, -s, s), 'bo': jax.random.uniform(ks[8], (D,), jnp.float32, -s, s)}
    _L0_attn_in = _L0_attn_setup()

    def _L0_ffn_setup():
        import jax, jax.numpy as jnp
        import numpy as np
        E = 8
        D = 128
        F = 512
        S, B = (256, 2)
        LN_EPS = 1e-05

        def _moe_forward(input_features, centroids, ln_g, ln_b, W1, b1, W2, b2):
            s, b, d = input_features.shape
            x = jnp.swapaxes(input_features, 0, 1).reshape(-1, d)
            logits = x.astype(jnp.float32) @ centroids.astype(jnp.float32).T
            assign = jnp.argmax(logits, axis=-1)
            onehot = jax.nn.one_hot(assign, E, dtype=x.dtype)
            disp = jnp.einsum('te,td->etd', onehot, x)
            mu = disp.mean(-1, keepdims=True)
            var = disp.var(-1, keepdims=True)
            xn = (disp - mu) * jax.lax.rsqrt(var + LN_EPS)
            xn = xn * ln_g[:, None, :] + ln_b[:, None, :]
            h = jax.nn.relu(jnp.einsum('etd,edf->etf', xn, W1) + b1[:, None, :])
            y = jnp.einsum('etf,efd->etd', h, W2) + b2[:, None, :]
            y = disp + y
            out = jnp.einsum('te,etd->td', onehot, y)
            return jnp.swapaxes(out.reshape(b, s, d), 0, 1)
        key = jax.random.key(seed)
        ks = jax.random.split(key, 8)
        scale_in = 1.0 / np.sqrt(D)
        scale_ff = 1.0 / np.sqrt(F)
        return {'input_features': jax.random.normal(ks[0], (S, B, D), dtype=jnp.float32), 'centroids': jax.random.normal(ks[1], (E, D), dtype=jnp.float32) * scale_in, 'ln_g': jnp.ones((E, D), dtype=jnp.float32), 'ln_b': jnp.zeros((E, D), dtype=jnp.float32), 'W1': jax.random.normal(ks[2], (E, D, F), dtype=jnp.float32) * scale_in, 'b1': jax.random.normal(ks[3], (E, F), dtype=jnp.float32) * 0.01, 'W2': jax.random.normal(ks[4], (E, F, D), dtype=jnp.float32) * scale_ff, 'b2': jax.random.normal(ks[5], (E, D), dtype=jnp.float32) * 0.01}
    _L0_ffn_in = _L0_ffn_setup()

    def _L1_attn_setup():
        import jax, jax.numpy as jnp
        import numpy as np
        import math
        N_HEAD = 16
        HEAD_DIM = 64
        N_EMBD = 128
        EPS_RMS = 1e-05
        U_L2_EPS = 1e-06

        def _get_alibi_slopes(n_heads):

            def pow2(n):
                start = 2 ** (-2 ** (-(math.log2(n) - 3)))
                return [start * start ** i for i in range(n)]
            if math.log2(n_heads).is_integer():
                return pow2(n_heads)
            c = 2 ** math.floor(math.log2(n_heads))
            s = pow2(c)
            extra = _get_alibi_slopes(2 * c)
            return s + extra[0::2][:n_heads - c]

        def _rmsnorm(x, w):
            var = jnp.mean(jnp.square(x), axis=-1, keepdims=True)
            return x * jax.lax.rsqrt(var + EPS_RMS) * w
        key = jax.random.key(seed)
        ks = jax.random.split(key, 9)
        B, T = (2, 256)
        H, D, C = (N_HEAD, HEAD_DIM, N_EMBD)
        x = jax.random.normal(ks[0], (B, T, C), dtype=jnp.float32)
        sc = 1.0 / math.sqrt(C)
        Wq = jax.random.normal(ks[1], (C, H * D), dtype=jnp.float32) * sc
        Wk = jax.random.normal(ks[2], (C, H * D), dtype=jnp.float32) * sc
        Wv = jax.random.normal(ks[3], (C, H * D), dtype=jnp.float32) * sc
        Wproj = jax.random.normal(ks[4], (H * D, C), dtype=jnp.float32) * (0.5 / math.sqrt(C) / math.sqrt(12))
        q_rms_w = jnp.ones((D,), dtype=jnp.float32)
        k_rms_w = jnp.ones((D,), dtype=jnp.float32)
        omega = jnp.full((H,), math.log(math.expm1(1.0)), dtype=jnp.float32)
        u = jax.random.normal(ks[5], (H, D), dtype=jnp.float32) * (1.0 / math.sqrt(D))
        return {'x': x, 'Wq': Wq, 'Wk': Wk, 'Wv': Wv, 'Wproj': Wproj, 'q_rms_w': q_rms_w, 'k_rms_w': k_rms_w, 'omega': omega, 'u': u}
    _L1_attn_in = _L1_attn_setup()

    def _L1_ffn_setup():
        import jax, jax.numpy as jnp
        import numpy as np
        D_IN, D_HID = (128, 512)

        def _ternary(key, shape):
            return jax.random.randint(key, shape, -1, 2).astype(jnp.float32)

        def _tlin(x, w, s):
            return jnp.einsum('bsi,oi->bso', x, w) * s
        key = jax.random.key(seed)
        ks = jax.random.split(key, 12)
        inv = lambda fan: 1.0 / np.sqrt(fan).astype(np.float32)
        return {'x': jax.random.normal(ks[0], (4, 256, D_IN), dtype=jnp.float32), 'w1_w': _ternary(ks[1], (D_HID, D_IN)), 'w1_s': jax.random.uniform(ks[2], (D_HID,), dtype=jnp.float32) * inv(D_IN), 'w2_w': _ternary(ks[3], (D_HID, D_IN)), 'w2_s': jax.random.uniform(ks[4], (D_HID,), dtype=jnp.float32) * inv(D_IN), 'h1_w': _ternary(ks[5], (D_HID, D_HID)), 'h1_s': jax.random.uniform(ks[6], (D_HID,), dtype=jnp.float32) * inv(D_HID), 'h2_w': _ternary(ks[7], (D_HID, D_HID)), 'h2_s': jax.random.uniform(ks[8], (D_HID,), dtype=jnp.float32) * inv(D_HID), 'w3_w': _ternary(ks[9], (D_IN, D_HID)), 'w3_s': jax.random.uniform(ks[10], (D_IN,), dtype=jnp.float32) * inv(D_HID)}
    _L1_ffn_in = _L1_ffn_setup()
    _d = {'L0_attn_x': _L0_attn_in['x'], 'L0_attn_Wq': _L0_attn_in['Wq'], 'L0_attn_bq': _L0_attn_in['bq'], 'L0_attn_Wk': _L0_attn_in['Wk'], 'L0_attn_bk': _L0_attn_in['bk'], 'L0_attn_Wv': _L0_attn_in['Wv'], 'L0_attn_bv': _L0_attn_in['bv'], 'L0_attn_Wo': _L0_attn_in['Wo'], 'L0_attn_bo': _L0_attn_in['bo'], 'L0_ffn_centroids': _L0_ffn_in['centroids'], 'L0_ffn_ln_g': _L0_ffn_in['ln_g'], 'L0_ffn_ln_b': _L0_ffn_in['ln_b'], 'L0_ffn_W1': _L0_ffn_in['W1'], 'L0_ffn_b1': _L0_ffn_in['b1'], 'L0_ffn_W2': _L0_ffn_in['W2'], 'L0_ffn_b2': _L0_ffn_in['b2'], 'L1_attn_Wq': _L1_attn_in['Wq'], 'L1_attn_Wk': _L1_attn_in['Wk'], 'L1_attn_Wv': _L1_attn_in['Wv'], 'L1_attn_Wproj': _L1_attn_in['Wproj'], 'L1_attn_q_rms_w': _L1_attn_in['q_rms_w'], 'L1_attn_k_rms_w': _L1_attn_in['k_rms_w'], 'L1_attn_omega': _L1_attn_in['omega'], 'L1_attn_u': _L1_attn_in['u'], 'L1_ffn_w1_w': _L1_ffn_in['w1_w'], 'L1_ffn_w1_s': _L1_ffn_in['w1_s'], 'L1_ffn_w2_w': _L1_ffn_in['w2_w'], 'L1_ffn_w2_s': _L1_ffn_in['w2_s'], 'L1_ffn_h1_w': _L1_ffn_in['h1_w'], 'L1_ffn_h1_s': _L1_ffn_in['h1_s'], 'L1_ffn_h2_w': _L1_ffn_in['h2_w'], 'L1_ffn_h2_s': _L1_ffn_in['h2_s'], 'L1_ffn_w3_w': _L1_ffn_in['w3_w'], 'L1_ffn_w3_s': _L1_ffn_in['w3_s']}
    _x0 = _d['L0_attn_x']
    _d['L0_attn_x'] = jax.random.normal(jax.random.fold_in(jax.random.key(seed), 1), (4, 1024, 128), dtype=_x0.dtype)
    del _x0
    return _d

def reference(L0_attn_x, L0_attn_Wq, L0_attn_bq, L0_attn_Wk, L0_attn_bk, L0_attn_Wv, L0_attn_bv, L0_attn_Wo, L0_attn_bo, L0_ffn_centroids, L0_ffn_ln_g, L0_ffn_ln_b, L0_ffn_W1, L0_ffn_b1, L0_ffn_W2, L0_ffn_b2, L1_attn_Wq, L1_attn_Wk, L1_attn_Wv, L1_attn_Wproj, L1_attn_q_rms_w, L1_attn_k_rms_w, L1_attn_omega, L1_attn_u, L1_ffn_w1_w, L1_ffn_w1_s, L1_ffn_w2_w, L1_ffn_w2_s, L1_ffn_h1_w, L1_ffn_h1_s, L1_ffn_h2_w, L1_ffn_h2_s, L1_ffn_w3_w, L1_ffn_w3_s):

    def _L0_attn_ref(x, Wq, bq, Wk, bk, Wv, bv, Wo, bo):
        import jax, jax.numpy as jnp
        import numpy as np
        EMBED_DIM = 128
        NUM_HEADS = 16
        HEAD_DIM = EMBED_DIM // NUM_HEADS
        ALPHA = 1.0
        B, T, D = x.shape
        H, hd = (NUM_HEADS, HEAD_DIM)

        def proj(W, b):
            return (x @ W.T + b).reshape(B, T, H, hd).transpose(0, 2, 1, 3)
        Q = proj(Wq, bq)
        K = proj(Wk, bk)
        V = proj(Wv, bv)
        scores = jnp.einsum('bhid,bhjd->bhij', Q, K) / jnp.sqrt(jnp.float32(hd))
        ti = jnp.arange(T)
        delta = ti[:, None] - ti[None, :]
        causal = delta < 0
        deltaf = delta.astype(jnp.float32)
        decay = jnp.where(causal, 0.0, -jnp.abs(deltaf) ** ALPHA)
        scores = jnp.where(causal[None, None], -jnp.inf, scores) + decay[None, None]
        attn = jax.nn.softmax(scores, axis=-1)
        out = jnp.einsum('bhij,bhjd->bhid', attn, V)
        out = out.transpose(0, 2, 1, 3).reshape(B, T, D)
        return out @ Wo.T + bo

    def _L0_ffn_ref(input_features, centroids, ln_g, ln_b, W1, b1, W2, b2):
        import jax, jax.numpy as jnp
        import numpy as np
        E = 8
        D = 128
        F = 512
        S, B = (256, 2)
        LN_EPS = 1e-05

        def _moe_forward(input_features, centroids, ln_g, ln_b, W1, b1, W2, b2):
            s, b, d = input_features.shape
            x = jnp.swapaxes(input_features, 0, 1).reshape(-1, d)
            logits = x.astype(jnp.float32) @ centroids.astype(jnp.float32).T
            assign = jnp.argmax(logits, axis=-1)
            onehot = jax.nn.one_hot(assign, E, dtype=x.dtype)
            disp = jnp.einsum('te,td->etd', onehot, x)
            mu = disp.mean(-1, keepdims=True)
            var = disp.var(-1, keepdims=True)
            xn = (disp - mu) * jax.lax.rsqrt(var + LN_EPS)
            xn = xn * ln_g[:, None, :] + ln_b[:, None, :]
            h = jax.nn.relu(jnp.einsum('etd,edf->etf', xn, W1) + b1[:, None, :])
            y = jnp.einsum('etf,efd->etd', h, W2) + b2[:, None, :]
            y = disp + y
            out = jnp.einsum('te,etd->td', onehot, y)
            return jnp.swapaxes(out.reshape(b, s, d), 0, 1)
        return _moe_forward(input_features, centroids, ln_g, ln_b, W1, b1, W2, b2)

    def _L1_attn_ref(x, Wq, Wk, Wv, Wproj, q_rms_w, k_rms_w, omega, u):
        import jax, jax.numpy as jnp
        import numpy as np
        import math
        N_HEAD = 16
        HEAD_DIM = 64
        N_EMBD = 128
        EPS_RMS = 1e-05
        U_L2_EPS = 1e-06

        def _get_alibi_slopes(n_heads):

            def pow2(n):
                start = 2 ** (-2 ** (-(math.log2(n) - 3)))
                return [start * start ** i for i in range(n)]
            if math.log2(n_heads).is_integer():
                return pow2(n_heads)
            c = 2 ** math.floor(math.log2(n_heads))
            s = pow2(c)
            extra = _get_alibi_slopes(2 * c)
            return s + extra[0::2][:n_heads - c]

        def _rmsnorm(x, w):
            var = jnp.mean(jnp.square(x), axis=-1, keepdims=True)
            return x * jax.lax.rsqrt(var + EPS_RMS) * w
        B, T, C = x.shape
        H, D = (N_HEAD, HEAD_DIM)
        q = (x @ Wq).reshape(B, T, H, D)
        k = (x @ Wk).reshape(B, T, H, D)
        v = (x @ Wv).reshape(B, T, H, D)
        q = _rmsnorm(q, q_rms_w)
        k = _rmsnorm(k, k_rms_w)
        slopes = jnp.asarray(_get_alibi_slopes(H), dtype=jnp.float32)
        omega_eff = jax.nn.softplus(omega) * slopes
        u_n = u / jnp.maximum(jnp.linalg.norm(u, axis=-1, keepdims=True), U_L2_EPS)
        gate_logits = jnp.einsum('bthd,hd->bht', k, u_n) / math.sqrt(D)
        gate = jax.nn.softplus(gate_logits)
        idx = jnp.arange(T)
        dist = jnp.maximum(idx[:, None] - idx[None, :], 0).astype(jnp.float32)
        bias = -dist[None, None] * omega_eff[None, :, None, None] * gate[:, :, None, :]
        causal = idx[:, None] >= idx[None, :]
        bias = jnp.where(causal[None, None], bias, -jnp.inf)
        scale = 1.0 / math.sqrt(D)
        scores = jnp.einsum('bihd,bjhd->bhij', q, k) * scale + bias
        attn = jax.nn.softmax(scores, axis=-1)
        y = jnp.einsum('bhij,bjhd->bihd', attn, v).reshape(B, T, H * D)
        return y @ Wproj

    def _L1_ffn_ref(x, w1_w, w1_s, w2_w, w2_s, h1_w, h1_s, h2_w, h2_s, w3_w, w3_s):
        import jax, jax.numpy as jnp
        import numpy as np
        D_IN, D_HID = (128, 512)

        def _ternary(key, shape):
            return jax.random.randint(key, shape, -1, 2).astype(jnp.float32)

        def _tlin(x, w, s):
            return jnp.einsum('bsi,oi->bso', x, w) * s
        h = jax.nn.silu(_tlin(x, w1_w, w1_s)) * _tlin(x, w2_w, w2_s)
        h = jax.nn.gelu(_tlin(h, h1_w, h1_s), approximate=False)
        h = jax.nn.gelu(_tlin(h, h2_w, h2_s), approximate=False)
        return _tlin(h, w3_w, w3_s)
    x = L0_attn_x
    x = _layernorm(x + _L0_attn_ref(x, L0_attn_Wq, L0_attn_bq, L0_attn_Wk, L0_attn_bk, L0_attn_Wv, L0_attn_bv, L0_attn_Wo, L0_attn_bo), axis=-1)
    x = _layernorm(x + _L0_ffn_ref(x, L0_ffn_centroids, L0_ffn_ln_g, L0_ffn_ln_b, L0_ffn_W1, L0_ffn_b1, L0_ffn_W2, L0_ffn_b2), axis=-1)
    x = _layernorm(x + _L1_attn_ref(x, L1_attn_Wq, L1_attn_Wk, L1_attn_Wv, L1_attn_Wproj, L1_attn_q_rms_w, L1_attn_k_rms_w, L1_attn_omega, L1_attn_u), axis=-1)
    x = _layernorm(x + _L1_ffn_ref(x, L1_ffn_w1_w, L1_ffn_w1_s, L1_ffn_w2_w, L1_ffn_w2_s, L1_ffn_h1_w, L1_ffn_h1_s, L1_ffn_h2_w, L1_ffn_h2_s, L1_ffn_w3_w, L1_ffn_w3_s), axis=-1)
    return x

_drawn_inputs = setup_inputs


def setup_inputs(seed=0):
    import zlib

    import numpy as np

    out = dict(_drawn_inputs(seed))
    spreads = {'L0_ffn_ln_g': (1.0, 0.2),
     'L0_ffn_ln_b': (0.0, 0.1),
     'L1_attn_q_rms_w': (1.0, 0.6),
     'L1_attn_k_rms_w': (1.0, 0.6),
     'L1_attn_omega': (0.5413248538970947, 0.6)}
    factors = {'L0_attn_bq': 3.288,
     'L0_attn_bk': 8.0,
     'L0_ffn_b1': 8.0,
     'L0_ffn_b2': 8.0,
     'L1_attn_u': 7.458,
     'L1_ffn_w1_w': 8.0,
     'L1_ffn_w1_s': 8.0,
     'L1_ffn_w2_w': 8.0,
     'L1_ffn_w2_s': 8.0,
     'L1_ffn_h1_w': 8.0,
     'L1_ffn_h1_s': 8.0,
     'L1_ffn_h2_w': 8.0,
     'L1_ffn_h2_s': 8.0,
     'L1_ffn_w3_w': 8.0,
     'L1_ffn_w3_s': 8.0}
    for name, (base, spread) in spreads.items():
        noise = np.random.default_rng([zlib.crc32(name.encode()), seed]).standard_normal(out[name].shape)
        drawn = base * np.exp(spread * noise) if base else spread * noise
        out[name] = jnp.asarray(drawn.astype(out[name].dtype))
    for name, factor in factors.items():
        out[name] = (out[name] * factor).astype(out[name].dtype)
    return out
```

```python
from contextlib import ExitStack

import numpy as np

import concourse.bass as bass
from concourse import mybir
from concourse.alu_op_type import AluOpType as ALU

ACT = mybir.ActivationFunctionType
AX = mybir.AxisListType
F32 = mybir.dt.float32
F32R = mybir.dt.float32r
BF16 = mybir.dt.bfloat16

P = 128
BANK = 512
CHUNK = 512
TILES = CHUNK // P
EPS = 1e-5

POS = 64
MAXROW = 68
MASKED = -1e30


class Lane:

    def __init__(self, nc, engine, name, per):
        self.sem, self.engine, self.per, self.base, self.n = nc.alloc_semaphore(name), engine, per, per, 0
        if per:
            engine.sem_inc(self.sem, per)

    def begin(self, it):
        self.base, self.n = it * self.per + self.per, 0

    def did(self, instruction, k=1):
        instruction.then_inc(self.sem, k)
        self.n += k
        return self.n

    def need(self, engine, number):
        engine.wait_ge(self.sem, self.base + number)



def settle(*lanes):
    found, said = [x.n for x in lanes], [x.per for x in lanes]
    assert found == said, (found, said)


def barrier(nc):
    nc.all_engine_barrier()


def sbuf(nc, ctx, name, shape, dt=F32):
    return ctx.enter_context(nc.sbuf_tensor(name, shape, dt))


def attention(nc, ps, const, tag, qh, ql, kh, kl, extra, v_of, y_of, groups, heads, seq):
    NB = 4
    W = seq
    IT = seq // P
    HC = seq // BANK
    two = ql is not None and heads == 2
    wide = P // heads
    R = 4 * heads if heads > 2 else 12
    units = [(c, j) for c in range(HC) for j in range((c + 1) * BANK // P)]
    U = len(units) * heads
    assert U % R == 0 and HC == 2 and groups % NB == 0
    n_load = len(qh) + len(kh) + 1 + len(extra) + (len(ql) + len(kl) if two else 0)

    with ExitStack() as ctx:
        QA = [sbuf(nc, ctx, f"{tag}QA{b}", [P, heads, W], F32R) for b in range(NB)]
        KA = [sbuf(nc, ctx, f"{tag}KA{b}", [P, heads, W], F32R) for b in range(NB)]
        QB = [sbuf(nc, ctx, f"{tag}QB{b}", [P, heads, W], F32R) for b in range(NB)] if two else None
        KB = [sbuf(nc, ctx, f"{tag}KB{b}", [P, heads, W], F32R) for b in range(NB)] if two else None
        V = [sbuf(nc, ctx, f"{tag}V{b}", [P, IT, P]) for b in range(NB)]
        prob = sbuf(nc, ctx, f"{tag}prob", [P, R, BANK])
        mx = sbuf(nc, ctx, f"{tag}mx", [P, heads * IT])
        negT = sbuf(nc, ctx, f"{tag}negT", [heads * IT, NB, P], F32R)
        den = sbuf(nc, ctx, f"{tag}den", [P, BANK])
        rec = sbuf(nc, ctx, f"{tag}rec", [P, TILES * heads])
        recw = sbuf(nc, ctx, f"{tag}recw", [P, TILES * heads, wide])
        recb = sbuf(nc, ctx, f"{tag}recb", [P, BANK])
        oT = sbuf(nc, ctx, f"{tag}oT", [P, HC, BANK])
        S1 = [ps[:, 0:2, :], ps[:, 2:4, :]]
        S2 = [ps[:, 4, :], ps[:, 5, :]]
        O = ps[:, 6, :]
        D = ps[:, 7, :]

        ld = [nc.alloc_semaphore(f"{tag}_loaded{b}") for b in range(NB)]
        s1_full = nc.alloc_semaphore(f"{tag}_s1_full")
        s1_free = nc.alloc_semaphore(f"{tag}_s1_free")
        t_full = nc.alloc_semaphore(f"{tag}_t_full")
        neg_full = nc.alloc_semaphore(f"{tag}_neg_full")
        row_full = [nc.alloc_semaphore(f"{tag}_row_full{b}") for b in range(NB)]
        s2_full = nc.alloc_semaphore(f"{tag}_s2_full")
        p_full = nc.alloc_semaphore(f"{tag}_p_full")
        p_free = nc.alloc_semaphore(f"{tag}_p_free")
        d_copied = nc.alloc_semaphore(f"{tag}_d_copied")
        d_turned = nc.alloc_semaphore(f"{tag}_d_turned")
        r_full = nc.alloc_semaphore(f"{tag}_r_full")
        rb_full = nc.alloc_semaphore(f"{tag}_rb_full")
        rb_copied = nc.alloc_semaphore(f"{tag}_rb_copied")
        o_done = nc.alloc_semaphore(f"{tag}_o_done")
        stored = [nc.alloc_semaphore(f"{tag}_stored{c}") for c in range(HC)]
        setup = nc.alloc_semaphore(f"{tag}_setup")

        nc.vector.sem_inc(s1_free, 2)
        nc.scalar.sem_inc(p_full, 2)
        nc.tensor.sem_inc(p_free, R)
        nc.vector.sem_inc(o_done, 1)
        for c in range(HC):
            nc.vector.sem_inc(stored[c], 16)
        n = 0
        for b in range(NB):
            for buf, rows in ((QA, const["qpos"]), (KA, const["kpos"])):
                if not two:
                    nc.vector.memset(buf[b][0:POS, :, :].bitcast(F32), 0.0).then_inc(setup, 1)
                    n += 1
                for h in range(heads):
                    nc.vector.tensor_copy(buf[b][POS:P, h, :], rows[POS:P, :]).then_inc(setup, 1)
                    n += 1
        nc.sync.wait_ge(setup, n)
        nc.tensor.wait_ge(setup, n)

        def load(g, b):
            parts = [(QA, r, s) for r, s in qh] + [(KA, r, s) for r, s in kh] + [(KA if k else QA, r, s) for k, r, s in extra]
            if two:
                parts += [(QB, r, s) for r, s in ql] + [(KB, r, s) for r, s in kl]
            for buf, (r0, r1), src in parts:
                nc.sync.dma_start(buf[b][r0:r1, :, :].bitcast(F32), src(g)).then_inc(ld[b], 16)
            nc.sync.dma_start(V[b][:, :, :], v_of(g)).then_inc(ld[b], 16)

        def loaded(engine, r, b):
            engine.wait_ge(ld[b], (r + 1) * 16 * n_load)

        def maxima(g, r, b, h, t):
            k = h * IT + t
            n = g * (heads * IT) + k
            if k == 0:
                loaded(nc.tensor, r, b)
                nc.tensor.wait_ge(neg_full, g + 1)
            nc.tensor.wait_ge(s1_free, n + 1)
            s = S1[k % 2]
            lhs = QA[b][:, h, t * P:(t + 1) * P]
            cols = (t + 1) * P
            for j0 in range(0, cols, BANK):
                j1 = min(cols, j0 + BANK)
                last = j1 == cols
                nc.tensor.matmul(s[:, j0 // BANK, 0:j1 - j0], lhs, KA[b][:, h, j0:j1], start=True, stop=not last)
            d0 = t * P % BANK
            nc.tensor.matmul(s[:, t * P // BANK, d0:d0 + P], const["identb"][:, :], const["mask_ij"][:, :],
                             start=False, stop=True).then_inc(s1_full, 1)
            nc.vector.wait_ge(s1_full, n + 1)
            flat = s.rearrange("p a n -> p (a n)")[:, 0:cols]
            nc.vector.tensor_reduce(mx[:, k:k + 1], flat, axis=AX.X, op=ALU.max).then_inc(s1_free, 1)

        def turn_maxima(g, b):
            nc.tensor.wait_ge(s1_free, (g + 1) * (heads * IT) + 2)
            nc.tensor.transpose(S1[0][0:heads * IT, 0, 0:P], mx[:, :], const["ident"][:, :]).then_inc(t_full, 1)
            nc.vector.wait_ge(t_full, g + 1)
            nc.vector.tensor_scalar(negT[:, b, :], S1[0][0:heads * IT, 0, 0:P], -1.0, None, ALU.mult).then_inc(neg_full, 1)
            nc.sync.wait_ge(neg_full, g + 2)
            nc.sync.dma_start(QA[b][MAXROW:MAXROW + 1, :, :].bitcast(F32), negT[:, b, :].bitcast(F32)).then_inc(row_full[b], 16)

        def exponentials(g, r, b, u, h):
            c, j = units[u]
            k = u * heads + h
            n = g * U + k
            if k == 0:
                nc.tensor.wait_ge(row_full[b], (r + 1) * 16)
            off = max(0, j * P - c * BANK)
            i0, i1 = c * BANK + off, (c + 1) * BANK
            s = S2[k % 2][:, off:BANK]
            diag = j * P >= c * BANK
            nc.tensor.wait_ge(p_full, n + 1)
            last = nc.tensor.matmul(s, KA[b][:, h, j * P:(j + 1) * P], QA[b][:, h, i0:i1], start=True,
                                    stop=not (two or diag))
            if two:
                last = nc.tensor.matmul(s, KB[b][:, h, j * P:(j + 1) * P], QB[b][:, h, i0:i1], start=False, stop=not diag)
            if diag:
                last = nc.tensor.matmul(S2[k % 2][:, off:off + P], const["identb"][:, :], const["mask_ji"][:, :],
                                        start=False, stop=True)
            last.then_inc(s2_full, 1)
            nc.scalar.wait_ge(s2_full, n + 1)
            nc.scalar.wait_ge(p_free, n + 1)
            nc.scalar.activation(prob[:, k % R, off:BANK], s, ACT.Exp).then_inc(p_full, 1)

        def values(g, b, u):
            c, j = units[u]
            off = max(0, j * P - c * BANK)
            first, final = j == 0, u + 1 == len(units) or units[u + 1][0] != c
            if first:
                nc.tensor.wait_ge(o_done, g * HC + c + 1)
            nc.tensor.wait_ge(p_full, g * U + (u + 1) * heads + 2)
            for h in range(heads):
                k = u * heads + h
                last = nc.tensor.matmul(O[h * wide:(h + 1) * wide, off:BANK], V[b][:, j, h * wide:(h + 1) * wide],
                                        prob[:, k % R, off:BANK], start=first, stop=final)
            if two:
                for m in range(2):
                    for h in range(heads):
                        k = u * heads + h
                        lo, hi = max(off, m * 256), (m + 1) * 256
                        if lo < hi:
                            q = 32 * (h + 2 * m)
                            last = nc.tensor.matmul(D[q:q + 32, lo - m * 256:hi - m * 256], const["ones"][:, 0:32],
                                                    prob[:, k % R, lo:hi], start=first,
                                                    stop=final or (m == 0 and units[u][1] * P - c * BANK == P))
            last.then_inc(p_free, heads)

        def copy_den(g, c):
            done = sum(1 for x in units if x[0] <= c) * heads
            nc.scalar.wait_ge(p_free, g * U + done + R)
            if two:
                nc.scalar.activation(den[:, 0:256], D[:, 0:256], ACT.Copy).then_inc(d_copied, 1)
            else:
                nc.scalar.activation(den[:, :], O, ACT.Copy).then_inc(d_copied, 1)

        def turn_den(g, c):
            nc.tensor.wait_ge(d_copied, g * HC + c + 1)
            for t in range(TILES):
                if two:
                    lhs, rhs = den[:, (t % 2) * P:(t % 2 + 1) * P], const["pick"][:, t // 2 * heads:(t // 2 + 1) * heads]
                else:
                    lhs, rhs = den[:, t * P:(t + 1) * P], const["pick"][:, 0:heads]
                last = nc.tensor.matmul(D[:, t * heads:(t + 1) * heads], lhs, rhs, start=True, stop=True)
            last.then_inc(d_turned, 1)
            nc.vector.wait_ge(d_turned, g * HC + c + 1)
            nc.vector.reciprocal(rec[:, :], D[:, 0:TILES * heads]).then_inc(r_full, 1)
            nc.vector.wait_ge(r_full, (g * HC + c) * 2 + 1)
            nc.vector.tensor_copy(recw[:, :, :], rec[:, :].unsqueeze(2).to_broadcast([P, TILES * heads, wide])).then_inc(r_full, 1)

        def spread(g, c):
            nc.tensor.wait_ge(r_full, (g * HC + c) * 2 + 2)
            for t in range(TILES):
                lhs = recw[:, t * heads:(t + 1) * heads, :].rearrange("p h w -> p (h w)")
                last = nc.tensor.matmul(D[:, t * P:(t + 1) * P], lhs, const["ident"][:, :], start=True, stop=True)
            last.then_inc(rb_full, 1)
            nc.scalar.wait_ge(rb_full, g * HC + c + 1)
            nc.scalar.activation(recb[:, :], D, ACT.Copy).then_inc(rb_copied, 1)

        def normalise(g, c):
            nc.vector.wait_ge(rb_copied, g * HC + c + 1)
            nc.vector.wait_ge(stored[c], (g + 1) * 16)
            nc.vector.tensor_tensor(oT[:, c, :], O, recb[:, :], ALU.mult).then_inc(o_done, 1)
            nc.sync.wait_ge(o_done, g * HC + c + 2)
            nc.sync.dma_start(y_of(g, c), oT[:, c, :]).then_inc(stored[c], 16)

        def step(g, r, b, r2, b2, ahead):
            todo = [(maxima, h, t) for h in range(heads) for t in range(IT)] if ahead else []
            total, given = len(todo), [0]
            weight = [0.0]
            every = len(units) * heads + 6

            def fill(w):
                weight[0] += w
                while todo and given[0] < total * weight[0] / every:
                    _, h, t = todo.pop(0)
                    maxima(g + 2, r2, b2, h, t)
                    given[0] += 1

            def exps(u):
                for h in range(heads):
                    exponentials(g, r, b, u, h)
                    fill(1)

            seam = sum(1 for x in units if x[0] == 0)
            for u in range(len(units)):
                exps(u)
                if u == seam:
                    values(g, b, u - 1)
                    copy_den(g, 0)
                elif u == seam + 1:
                    turn_den(g, 0)
                elif u == seam + 2:
                    spread(g, 0)
                    normalise(g, 0)
                elif u == seam + 3:
                    for x in range(seam, u):
                        values(g, b, x)
                elif u:
                    values(g, b, u - 1)
            fill(1)
            values(g, b, len(units) - 1)
            copy_den(g, 1)
            fill(2)
            turn_den(g, 1)
            fill(1)
            spread(g, 1)
            fill(every)
            normalise(g, 1)
            if ahead:
                turn_maxima(g + 2, b2)

        def load_when_free(g, b):
            nc.sync.wait_ge(p_free, (g - NB + 1) * U + R)
            load(g, b)

        nc.vector.sem_inc(neg_full, 1)
        for b in range(NB):
            load(b, b)
        for b in range(2):
            for h in range(heads):
                for t in range(IT):
                    maxima(b, 0, b, h, t)
            turn_maxima(b, b)
        body = groups // NB
        with nc.Fori(0, body - 1) as it:
            for b in range(NB):
                g = it * NB + b
                step(g, it, b, it + (b + 2) // NB, (b + 2) % NB, True)
                load_when_free(g + NB, b)
        for b in range(NB):
            g = (body - 1) * NB + b
            step(g, body - 1, b, body - 1, (b + 2) % NB, b < 2)
        for c in range(HC):
            nc.sync.wait_ge(stored[c], 16 * (groups + 1))
        barrier(nc)


def layernorm(nc, V, A, x, out, stats, mv, rstd, eps, spare, after):
    V.need(nc.vector, after)
    for t in range(TILES):
        V.did(nc.vector.bn_stats(stats[:, t, :], x[:, t, :]))
    V.need(nc.vector, V.n)
    nc.vector.memset(spare[:, 0:1], 0.0)
    for t in range(TILES):
        V.did(nc.vector.bn_aggr(mv[:, t, :], stats[:, t, :]))
    V.need(nc.scalar, V.n)
    A.did(nc.scalar.activation(rstd[:, :], mv[:, :, 1], ACT.Sqrt, bias=eps[:, 0:1]))
    A.need(nc.vector, A.n)
    V.did(nc.vector.reciprocal(rstd[:, :], rstd[:, :]))
    V.need(nc.vector, V.n)
    for t in range(TILES):
        V.did(nc.vector.tensor_scalar(out[:, t, :], x[:, t, :], mv[:, t, 0:1], rstd[:, t:t + 1],
                                      ALU.subtract, ALU.mult))
    return V.n


def turn(nc, T, A, src, bank, dst, ident):
    for t in range(TILES):
        last = nc.tensor.transpose(bank[:, t * P:(t + 1) * P], src[:, t, :], ident)
    n = T.did(last)
    T.need(nc.scalar, n)
    return A.did(nc.scalar.activation(dst[:, :], bank, ACT.Copy))


def project0(nc, ps, const, ins, scr, tokens, heads):
    scale = float(1.0 / np.sqrt(np.float32(P // heads)))
    PER = {"T": 7, "V": 8, "A": 3}
    with ExitStack() as ctx:
        wq, wk = sbuf(nc, ctx, "p0wq", [P, P]), sbuf(nc, ctx, "p0wk", [P, P])
        wv, bv = sbuf(nc, ctx, "p0wv", [P, BANK]), sbuf(nc, ctx, "p0bv", [P, BANK])
        bq, bk = sbuf(nc, ctx, "p0bq", [P, 1]), sbuf(nc, ctx, "p0bk", [P, 1])
        x = sbuf(nc, ctx, "p0x", [P, TILES, P])
        xT = sbuf(nc, ctx, "p0xT", [P, CHUNK])
        full = sbuf(nc, ctx, "p0full", [P, 2, CHUNK])
        high = sbuf(nc, ctx, "p0high", [P, 2, CHUNK], F32R)
        low = sbuf(nc, ctx, "p0low", [P, 2, CHUNK], F32R)
        v = sbuf(nc, ctx, "p0v", [P, TILES, BANK])
        w_in, x_in, out = (nc.alloc_semaphore(f"p0_{s}") for s in ("w_in", "x_in", "out"))
        T, V, A = Lane(nc, nc.tensor, "p0_T", PER["T"]), Lane(nc, nc.vector, "p0_V", PER["V"]), Lane(nc, nc.scalar, "p0_A", PER["A"])
        for d, s in ((wq, ins["wq0"]), (wk, ins["wk0"]), (wv, ins["wv0"]), (bq, ins["bq0"]), (bk, ins["bk0"]),
                     (bv, ins["bv0"].partition_broadcast(P))):
            nc.sync.dma_start(d[:, :], s).then_inc(w_in, 16)
        nc.tensor.wait_ge(w_in, 96)
        nc.vector.wait_ge(w_in, 96)
        nc.sync.sem_inc(out, 16 * 5)
        with nc.Fori(0, tokens // CHUNK) as it:
            for lane in (T, V, A):
                lane.begin(it)
            T.need(nc.sync, 0)
            nc.sync.dma_start(x[:, :, :], ins["x"][bass.ds(it * CHUNK, CHUNK), :].rearrange("(t p) d -> p t d", p=P)).then_inc(x_in, 16)
            nc.tensor.wait_ge(x_in, it * 16 + 16)
            V.need(nc.tensor, 0)
            A.need(nc.tensor, 0)
            xt = turn(nc, T, A, x, ps[:, 0, :], xT, const["ident"][:, :])
            A.need(nc.tensor, xt)
            T.did(nc.tensor.matmul(ps[:, 1, :], wq[:, :], xT[:, :], start=True, stop=True))
            k_at = T.did(nc.tensor.matmul(ps[:, 2, :], wk[:, :], xT[:, :], start=True, stop=True))
            v_at = [T.did(nc.tensor.matmul(ps[:, 3 + t, :], xT[:, t * P:(t + 1) * P], wv[:, :], start=True, stop=True))
                    for t in range(TILES)]
            nc.vector.wait_ge(out, it * 16 * 5 + 16 * 5)
            T.need(nc.vector, k_at)
            V.did(nc.vector.tensor_scalar(full[:, 0, :], ps[:, 1, :], bq[:, 0:1], scale, ALU.add, ALU.mult))
            f = V.did(nc.vector.tensor_scalar(full[:, 1, :], ps[:, 2, :], bk[:, 0:1], None, ALU.add))
            V.need(nc.scalar, f)
            A.did(nc.scalar.activation(high[:, 0, :], full[:, 0, :], ACT.Copy))
            hi = A.did(nc.scalar.activation(high[:, 1, :], full[:, 1, :], ACT.Copy))
            for t in range(TILES):
                T.need(nc.vector, v_at[t])
                V.did(nc.vector.tensor_tensor(v[:, t, :], ps[:, 3 + t, :], bv[:, :], ALU.add))
            A.need(nc.vector, hi)
            for n in range(2):
                V.did(nc.vector.tensor_tensor(low[:, n, :], full[:, n, :], high[:, n, :].bitcast(F32), ALU.subtract))
            V.need(nc.sync, V.n)
            A.need(nc.sync, hi)
            at = bass.ds(it * CHUNK, CHUNK)
            nc.sync.dma_start(scr["v0"][at, :].rearrange("(t p) n -> p t n", p=P), v[:, :, :]).then_inc(out, 16)
            for n, name in enumerate(("q0", "k0")):
                nc.sync.dma_start(scr[name][0, :, at], high[:, n, :].bitcast(F32)).then_inc(out, 16)
                nc.sync.dma_start(scr[name][1, :, at], low[:, n, :].bitcast(F32)).then_inc(out, 16)
        settle(T, V, A)
        nc.sync.wait_ge(out, 16 * 5 * (tokens // CHUNK + 1))
        barrier(nc)


def middle(nc, ps, const, ins, scr, tokens, experts, hidden, heads, dim):
    PER = {"T": 76, "V": 143, "A": 54}
    KC = 4
    FC = hidden // P
    HD = heads * dim
    PAIRS = HD // P
    with ExitStack() as ctx:
        wo = sbuf(nc, ctx, "mwo", [P, KC, P])
        bo = sbuf(nc, ctx, "mbo", [P, P])
        cent = sbuf(nc, ctx, "mcent", [P, experts])
        gT, bT = sbuf(nc, ctx, "mg", [P, experts]), sbuf(nc, ctx, "mb", [P, experts])
        w1 = sbuf(nc, ctx, "mw1", [P, experts, hidden])
        b1 = sbuf(nc, ctx, "mb1", [P, experts, FC])
        w2 = sbuf(nc, ctx, "mw2", [P, experts, FC, P])
        b2 = sbuf(nc, ctx, "mb2", [experts, P])
        wq, wk, wv = (sbuf(nc, ctx, f"m{n}", [P, HD]) for n in ("wq", "wk", "wv"))
        wqn, wkn = sbuf(nc, ctx, "mwqn", [P, 1]), sbuf(nc, ctx, "mwkn", [P, 1])
        u, kw = sbuf(nc, ctx, "mu", [heads, dim]), sbuf(nc, ctx, "mkw", [heads, dim])
        usq, us = sbuf(nc, ctx, "musq", [heads, dim]), sbuf(nc, ctx, "mus", [heads, 1])
        G = sbuf(nc, ctx, "mG", [P, heads])
        om, om1, slopes = (sbuf(nc, ctx, f"m{n}", [P, heads]) for n in ("om", "om1", "slopes"))
        iota = sbuf(nc, ctx, "miota", [P, TILES, experts])
        eps, spare = sbuf(nc, ctx, "meps", [P, 1]), sbuf(nc, ctx, "mspare", [P, 1])

        y, x = sbuf(nc, ctx, "my", [P, KC, CHUNK]), sbuf(nc, ctx, "mx0", [P, TILES, P])
        jpos = sbuf(nc, ctx, "mjpos", [P, TILES])
        r1 = sbuf(nc, ctx, "mr1", [P, TILES, P])
        x1, xn, acc, x2 = (sbuf(nc, ctx, f"m{n}", [P, TILES, P]) for n in ("x1", "xn", "acc", "x2"))
        xT, xnT, xe = (sbuf(nc, ctx, f"m{n}", [P, CHUNK]) for n in ("xT", "xnT", "xe"))
        stats, mv, rstd = sbuf(nc, ctx, "mst", [P, TILES, 6]), sbuf(nc, ctx, "mmv", [P, TILES, 2]), sbuf(nc, ctx, "mrs", [P, TILES])
        top = sbuf(nc, ctx, "mtop", [P, TILES])
        eq, oh = sbuf(nc, ctx, "meq", [P, TILES, experts]), sbuf(nc, ctx, "moh", [P, TILES, experts])
        ohT = sbuf(nc, ctx, "mohT", [experts, CHUNK])
        h = sbuf(nc, ctx, "mh", [P, FC, CHUNK])
        sq = sbuf(nc, ctx, "msq", [P, 2 * HD])
        ss = sbuf(nc, ctx, "mss", [P, 2 * heads])
        qk = sbuf(nc, ctx, "mqk", [P, 2 * HD])
        v = sbuf(nc, ctx, "mval", [P, HD])
        high, low = sbuf(nc, ctx, "mhi", [P, 2, PAIRS, P], F32R), sbuf(nc, ctx, "mlo", [P, 2, PAIRS, P], F32R)
        z, zabs, g, gj = (sbuf(nc, ctx, f"m{n}", [P, TILES, heads]) for n in ("z", "zabs", "slope", "gj"))
        aug = sbuf(nc, ctx, "maug", [P, TILES, P // heads, heads], F32R)
        augT = sbuf(nc, ctx, "maugT", [4 * heads, CHUNK])

        sem = lambda n: nc.alloc_semaphore(f"m_{n}")
        w_in, c_in, out, out_v, out_qk = sem("w_in"), sem("c_in"), sem("out"), sem("out_v"), sem("out_qk")
        s0, s1 = sem("setup_v"), sem("setup_a")
        weights = [(wo[:, :, :], ins["wo0"]), (bo[:, :], ins["bo0"].partition_broadcast(P)), (cent[:, :], ins["cent"]),
                   (gT[:, :], ins["ln_g"]), (bT[:, :], ins["ln_b"]), (w1[:, :, :], ins["w1"]), (b1[:, :, :], ins["b1"]),
                   (w2[:, :, :, :], ins["w2"]), (b2[:, :], ins["b2"]), (wq[:, :], ins["wq1"]), (wk[:, :], ins["wk1"]),
                   (wv[:, :], ins["wv1"]), (wqn[:, :], ins["qn"]), (wkn[:, :], ins["kn"]), (u[:, :], ins["u"]),
                   (kw[:, :], ins["kn_row"].partition_broadcast(heads)), (om[:, :], ins["omega"].partition_broadcast(P)),
                   (slopes[:, :], ins["slopes"].partition_broadcast(P)),
                   (iota[:, :, :], ins["iota"].partition_broadcast(P))]
        for d, s in weights:
            nc.sync.dma_start(d, s).then_inc(w_in, 16)
        n_w = 16 * len(weights)
        for e in (nc.tensor, nc.vector, nc.scalar):
            e.wait_ge(w_in, n_w)

        dv, ac = [0], [0]

        def dve(ins_):
            dv[0] += 1
            ins_.then_inc(s0, 1)
            nc.vector.wait_ge(s0, dv[0])

        def act(ins_):
            ac[0] += 1
            nc.vector.wait_ge(s1, ac[0])
            return ins_
        dve(nc.vector.memset(eps[:, :], EPS))
        dve(nc.vector.memset(aug[:, :, :, :].bitcast(F32), 0.0))
        dve(nc.vector.tensor_scalar(wqn[:, :], wqn[:, :], float(1.0 / np.sqrt(dim)), None, ALU.mult))
        dve(nc.vector.tensor_tensor(usq[:, :], u[:, :], u[:, :], ALU.mult))
        dve(nc.vector.tensor_reduce(us[:, :], usq[:, :], axis=AX.X, op=ALU.add))
        nc.scalar.wait_ge(s0, dv[0])
        nc.scalar.activation(us[:, :], us[:, :], ACT.Sqrt).then_inc(s1, 1)
        nc.vector.wait_ge(s1, 1)
        dve(nc.vector.tensor_scalar(us[:, :], us[:, :], 1e-6, None, ALU.max))
        dve(nc.vector.reciprocal(us[:, :], us[:, :]))
        dve(nc.vector.scalar_tensor_tensor(usq[:, :], u[:, :], us[:, 0:1], kw[:, :], ALU.mult, ALU.mult))
        nc.sync.wait_ge(s0, dv[0])
        nc.sync.dma_start(scr["ku"], usq[:, :]).then_inc(w_in, 16)
        nc.sync.wait_ge(w_in, n_w + 16)
        nc.sync.dma_start(sq[:, 0:HD], scr["ku"].rearrange("h d -> (h d)").partition_broadcast(P)).then_inc(w_in, 16)
        nc.vector.wait_ge(w_in, n_w + 32)
        dve(nc.vector.tensor_tensor(sq[:, 0:HD], sq[:, 0:HD], wk[:, :], ALU.mult))
        dve(nc.vector.tensor_reduce(G[:, :], sq[:, 0:HD].rearrange("p (h d) -> p h d", d=dim), axis=AX.X, op=ALU.add))
        dve(nc.vector.tensor_scalar(G[:, :], G[:, :], float(1.0 / np.sqrt(dim)), None, ALU.mult))
        dve(nc.vector.scalar_tensor_tensor(om1[:, :], om[:, :], -1.0, om[:, :], ALU.mult, ALU.max))
        nc.scalar.wait_ge(s0, dv[0])
        nc.scalar.activation(om1[:, :], om1[:, :], ACT.Exp, scale=-1.0).then_inc(s1, 1)
        nc.scalar.wait_ge(s1, 2)
        nc.scalar.activation(om1[:, :], om1[:, :], ACT.Ln, bias=1.0).then_inc(s1, 1)
        nc.vector.wait_ge(s1, 3)
        dve(nc.vector.scalar_tensor_tensor(om[:, :], om[:, :], 0.0, om1[:, :], ALU.max, ALU.add))
        dve(nc.vector.tensor_tensor(om[:, :], om[:, :], slopes[:, :], ALU.mult))
        nc.tensor.wait_ge(s0, dv[0])
        nc.scalar.wait_ge(s0, dv[0])

        T, V, A = Lane(nc, nc.tensor, "m_T", PER["T"]), Lane(nc, nc.vector, "m_V", PER["V"]), Lane(nc, nc.scalar, "m_A", PER["A"])
        nc.sync.sem_inc(out, 32)
        nc.sync.sem_inc(out_v, 16)
        nc.sync.sem_inc(out_qk, 64)
        ident = const["ident"][:, :]
        with nc.Fori(0, tokens // CHUNK) as it:
            for lane in (T, V, A):
                lane.begin(it)
            at = bass.ds(it * CHUNK, CHUNK)
            for e in (nc.sync, nc.tensor, nc.vector, nc.scalar):
                for lane in (T, V, A):
                    if lane.engine is not e:
                        lane.need(e, 0)
            nc.sync.dma_start(y[:, :, :], scr["y0"][:, at].rearrange("(k p) n -> p k n", p=P)).then_inc(c_in, 16)
            nc.sync.dma_start(x[:, :, :], ins["x"][at, :].rearrange("(t p) d -> p t d", p=P)).then_inc(c_in, 16)
            nc.sync.dma_start(jpos[:, :], ins["jpos"][bass.ds(it, 1), :, :].rearrange("a p t -> (a p) t")).then_inc(c_in, 16)
            nc.tensor.wait_ge(c_in, it * 48 + 48)
            nc.vector.wait_ge(c_in, it * 48 + 48)
            for t in range(TILES):
                for k in range(KC):
                    last = nc.tensor.matmul(ps[:, 0, t * P:(t + 1) * P], y[:, k, t * P:(t + 1) * P], wo[:, k, :],
                                            start=k == 0, stop=k == KC - 1)
            T.did(last)
            T.need(nc.vector, T.n)
            V.did(nc.vector.tensor_tensor(r1[:, :, :], ps[:, 0, :].rearrange("p (t d) -> p t d", d=P), x[:, :, :], ALU.add))
            V.need(nc.vector, V.n)
            V.did(nc.vector.tensor_tensor(r1[:, :, :], r1[:, :, :], bo[:, :].unsqueeze(1).to_broadcast([P, TILES, P]), ALU.add))
            n1 = layernorm(nc, V, A, r1, x1, stats, mv, rstd, eps, spare, V.n)
            V.need(nc.tensor, n1)
            a = turn(nc, T, A, x1, ps[:, 1, :], xT, ident)
            A.need(nc.tensor, a)
            for t in range(TILES):
                last = nc.tensor.matmul(ps[:, 2, t * experts:(t + 1) * experts], xT[:, t * P:(t + 1) * P], cent[:, :],
                                        start=True, stop=True)
            lg = T.did(last)
            n = layernorm(nc, V, A, x1, xn, stats, mv, rstd, eps, spare, n1)
            V.need(nc.tensor, n)
            nT = turn(nc, T, A, xn, ps[:, 3, :], xnT, ident)
            T.need(nc.vector, lg)
            logits = ps[:, 2, 0:TILES * experts].rearrange("p (t e) -> p t e", e=experts)
            per_tile = [P, TILES, experts]
            V.did(nc.vector.tensor_reduce(top[:, :], logits, axis=AX.X, op=ALU.max))
            V.need(nc.vector, V.n)
            V.did(nc.vector.tensor_tensor(eq[:, :, :], logits, top[:, :].unsqueeze(2).to_broadcast(per_tile), ALU.is_equal))
            V.need(nc.vector, V.n)
            V.did(nc.vector.tensor_tensor(eq[:, :, :], eq[:, :, :], iota[:, :, :], ALU.mult))
            V.need(nc.vector, V.n)
            V.did(nc.vector.tensor_reduce(top[:, :], eq[:, :, :], axis=AX.X, op=ALU.min))
            V.need(nc.vector, V.n)
            o = V.did(nc.vector.tensor_tensor(oh[:, :, :], iota[:, :, :], top[:, :].unsqueeze(2).to_broadcast(per_tile), ALU.is_equal))
            V.need(nc.tensor, o)
            for t in range(TILES):
                last = nc.tensor.transpose(ps[0:experts, 4, t * P:(t + 1) * P], oh[:, t, :], ident)
            T.did(last)
            T.need(nc.scalar, T.n)
            A.did(nc.scalar.activation(ohT[:, :], ps[0:experts, 4, :], ACT.Copy))
            A.need(nc.tensor, A.n)
            for t in range(TILES):
                last = nc.tensor.matmul(ps[:, 6, t * P:(t + 1) * P], ohT[:, t * P:(t + 1) * P], b2[:, :], start=True, stop=True)
            T.did(last)
            T.need(nc.vector, T.n)
            ac_ = V.did(nc.vector.scalar_tensor_tensor(acc[:, :, :], x1[:, :, :], 2.0,
                                                       ps[:, 6, :].rearrange("p (t d) -> p t d", d=P), ALU.mult, ALU.add))
            A.need(nc.vector, nT)
            hb = [0] * FC
            y_at = None
            for e in range(experts):
                if e:
                    T.need(nc.vector, up)
                V.did(nc.vector.tensor_scalar(xe[:, :], xnT[:, :], gT[:, e:e + 1], bT[:, e:e + 1], ALU.mult, ALU.add))
                V.need(nc.tensor, V.n)
                ups = []
                for f in range(FC):
                    if e:
                        (V if f % 2 else A).need(nc.tensor, hb[f])
                    ups.append(T.did(nc.tensor.matmul(ps[:, f, :], w1[:, e, f * P:(f + 1) * P], xe[:, :], start=True, stop=True)))
                up = ups[-1]
                if e:
                    T.need(nc.scalar, y_at)
                    T.need(nc.vector, y_at)
                for f in range(FC):
                    if f % 2:
                        T.need(nc.vector, ups[f])
                        hb[f] = V.did(nc.vector.tensor_scalar(h[:, f, :], ps[:, f, :], b1[:, e, f:f + 1], 0.0, ALU.add, ALU.max))
                    else:
                        T.need(nc.scalar, ups[f])
                        hb[f] = A.did(nc.scalar.activation(h[:, f, :], ps[:, f, :], ACT.Relu, bias=b1[:, e, f:f + 1]))
                V.need(nc.tensor, V.n)
                A.need(nc.tensor, A.n)
                for t in range(TILES):
                    for f in range(FC):
                        last = nc.tensor.matmul(ps[:, 4 + e % 2, t * P:(t + 1) * P], h[:, f, t * P:(t + 1) * P], w2[:, e, f, :],
                                                start=f == 0, stop=f == FC - 1)
                y_at = T.did(last)
                T.need(nc.vector, y_at)
                V.need(nc.vector, ac_)
                for t in range(TILES):
                    ac_ = V.did(nc.vector.scalar_tensor_tensor(acc[:, t, :], ps[:, 4 + e % 2, t * P:(t + 1) * P], oh[:, t, e:e + 1],
                                                               acc[:, t, :], ALU.mult, ALU.add))
            nc.vector.wait_ge(out, it * 32 + 32)
            nc.scalar.wait_ge(out, it * 32 + 32)
            n2 = layernorm(nc, V, A, acc, x2, stats, mv, rstd, eps, spare, ac_)
            V.need(nc.sync, n2)
            nc.sync.dma_start(scr["x2"][at, :].rearrange("(t p) d -> p t d", p=P), x2[:, :, :]).then_inc(out, 16)
            V.need(nc.tensor, n2)
            a = turn(nc, T, A, x2, ps[:, 6, :], xT, ident)
            A.need(nc.tensor, a)
            lows = []
            for t in range(TILES):
                lhs = xT[:, t * P:(t + 1) * P]
                if t:
                    V.need(nc.tensor, qkn)
                    A.need(nc.tensor, sqd)
                for n, w in ((0, wq), (1, wq), (2, wk), (3, wk)):
                    last = nc.tensor.matmul(ps[:, n, :], lhs, w[:, n % 2 * BANK:(n % 2 + 1) * BANK], start=True, stop=True)
                pq = T.did(last)
                if t:
                    A.need(nc.tensor, vc)
                for n in range(2):
                    last = nc.tensor.matmul(ps[:, 4 + n, :], lhs, wv[:, n * BANK:(n + 1) * BANK], start=True, stop=True)
                pv = T.did(last)
                T.need(nc.scalar, pq)
                if t:
                    V.need(nc.scalar, ssd)
                sqd = A.did(nc.scalar.activation(sq[:, :], ps[:, 0:4, :].rearrange("p a n -> p (a n)"), ACT.Square))
                A.need(nc.vector, sqd)
                ssd = V.did(nc.vector.tensor_reduce(ss[:, :], sq[:, :].rearrange("p (h d) -> p h d", d=dim), axis=AX.X, op=ALU.add))
                V.need(nc.scalar, ssd)
                A.did(nc.scalar.activation(ss[:, :], ss[:, :], ACT.Sqrt, scale=1.0 / dim, bias=eps[:, 0:1]))
                A.need(nc.vector, A.n)
                V.did(nc.vector.reciprocal(ss[:, :], ss[:, :]))
                V.need(nc.vector, V.n)
                if t:
                    T.need(nc.vector, tr)
                qkn = V.did(nc.vector.tensor_tensor(qk[:, :].rearrange("p (h d) -> p h d", d=dim),
                                                    ps[:, 0:4, :].rearrange("p a (h d) -> p (a h) d", d=dim),
                                                    ss[:, :].unsqueeze(2).to_broadcast([P, 2 * heads, dim]), ALU.mult))
                T.need(nc.scalar, pv)
                nc.scalar.wait_ge(out_v, (it * TILES + t + 1) * 16)
                vc = A.did(nc.scalar.activation(v[:, :], ps[:, 4:6, :].rearrange("p a n -> p (a n)"), ACT.Copy))
                A.need(nc.sync, vc)
                nc.sync.dma_start(scr["v1"][at, :][t * P:(t + 1) * P, :], v[:, :]).then_inc(out_v, 16)
                A.need(nc.tensor, vc)
                gm = T.did(nc.tensor.matmul(ps[:, 4, 0:heads], lhs, G[:, :], start=True, stop=True))
                T.need(nc.vector, gm)
                zt = V.did(nc.vector.tensor_tensor(z[:, t, :], ps[:, 4, 0:heads], ss[:, heads:2 * heads], ALU.mult))
                V.need(nc.tensor, zt)
                nc.vector.wait_ge(out_qk, (it * TILES + t + 1) * 64)
                nc.scalar.wait_ge(out_qk, (it * TILES + t + 1) * 64)
                for half in range(2 * PAIRS // 4):
                    n, p0 = half * 4 // PAIRS, half * 4 % PAIRS
                    bank = 6 + half % 2
                    if len(lows) >= 2:
                        V.need(nc.tensor, lows[-2])
                    for m in range(4):
                        last = nc.tensor.transpose(ps[:, bank, m * P:(m + 1) * P], qk[:, (half * 4 + m) * P:(half * 4 + m + 1) * P], ident)
                    tr = T.did(last)
                    T.need(nc.scalar, tr)
                    wn = (wqn, wkn)[n]
                    view = ps[:, bank, :].rearrange("p (m i) -> p m i", i=P)
                    A.did(nc.scalar.activation(high[:, n, p0:p0 + 4, :], view, ACT.Copy, scale=wn[:, 0:1]))
                    A.need(nc.vector, A.n)
                    lows.append(V.did(nc.vector.scalar_tensor_tensor(low[:, n, p0:p0 + 4, :], view, wn[:, 0:1],
                                                                     high[:, n, p0:p0 + 4, :].bitcast(F32), ALU.mult, ALU.subtract)))
                V.need(nc.sync, V.n)
                for n, name in enumerate(("q1", "k1")):
                    for part, buf in enumerate((high, low)):
                        nc.sync.dma_start(scr[name][part, :, at][:, t * P:(t + 1) * P].rearrange("(k p) i -> p k i", p=P),
                                          buf[:, n, :, :].bitcast(F32)).then_inc(out_qk, 16)
            V.need(nc.vector, zt)
            V.did(nc.vector.scalar_tensor_tensor(zabs[:, :, :], z[:, :, :], -1.0, z[:, :, :], ALU.mult, ALU.max))
            V.need(nc.scalar, V.n)
            A.did(nc.scalar.activation(zabs[:, :, :], zabs[:, :, :], ACT.Exp, scale=-1.0))
            A.need(nc.scalar, A.n)
            A.did(nc.scalar.activation(zabs[:, :, :], zabs[:, :, :], ACT.Ln, bias=1.0))
            A.need(nc.vector, A.n)
            V.did(nc.vector.scalar_tensor_tensor(g[:, :, :], z[:, :, :], 0.0, zabs[:, :, :], ALU.max, ALU.add))
            V.need(nc.vector, V.n)
            V.did(nc.vector.tensor_tensor(g[:, :, :], g[:, :, :], om[:, :].unsqueeze(1).to_broadcast([P, TILES, heads]), ALU.mult))
            V.need(nc.vector, V.n)
            V.did(nc.vector.tensor_tensor(gj[:, :, :], g[:, :, :], jpos[:, :].unsqueeze(2).to_broadcast([P, TILES, heads]), ALU.mult))
            V.did(nc.vector.tensor_copy(aug[:, :, 0, :], g[:, :, :]))
            V.need(nc.vector, V.n)
            V.did(nc.vector.tensor_copy(aug[:, :, 2, :], gj[:, :, :]))
            V.did(nc.vector.tensor_tensor(aug[:, :, 1, :], g[:, :, :], aug[:, :, 0, :].bitcast(F32), ALU.subtract))
            V.need(nc.vector, V.n)
            V.did(nc.vector.tensor_tensor(aug[:, :, 3, :], gj[:, :, :], aug[:, :, 2, :].bitcast(F32), ALU.subtract))
            V.need(nc.tensor, V.n)
            for t in range(TILES):
                last = nc.tensor.transpose(ps[:, 5, t * P:(t + 1) * P],
                                           aug[:, t, :, :].rearrange("p a h -> p (a h)").bitcast(F32), ident)
            T.did(last)
            T.need(nc.scalar, T.n)
            A.did(nc.scalar.activation(augT[:, :], ps[0:4 * heads, 5, :], ACT.Copy))
            A.need(nc.sync, A.n)
            nc.sync.dma_start(scr["g1"][:, at], augT[:, :]).then_inc(out, 16)
        settle(T, V, A)
        steps = tokens // CHUNK
        nc.sync.wait_ge(out, 32 * (steps + 1))
        nc.sync.wait_ge(out_v, 16 * (steps * TILES + 1))
        nc.sync.wait_ge(out_qk, 64 * (steps * TILES + 1))
        barrier(nc)


def final(nc, ps, const, ins, scr, result, tokens, hidden, kc):
    PER = {"T": 15, "V": 33, "A": 15}
    FC = hidden // P
    with ExitStack() as ctx:
        wp = sbuf(nc, ctx, "fwp", [P, kc, P])
        w1, w2 = sbuf(nc, ctx, "fw1", [P, hidden]), sbuf(nc, ctx, "fw2", [P, hidden])
        h1, h2 = sbuf(nc, ctx, "fh1", [P, FC, hidden]), sbuf(nc, ctx, "fh2", [P, FC, hidden])
        w3, s3 = sbuf(nc, ctx, "fw3", [P, FC, P]), sbuf(nc, ctx, "fs3", [P, P])
        sc = sbuf(nc, ctx, "fsc", [P, 4, FC])
        eps, spare = sbuf(nc, ctx, "feps", [P, 1]), sbuf(nc, ctx, "fspare", [P, 1])
        y, x = sbuf(nc, ctx, "fy", [P, kc, CHUNK]), sbuf(nc, ctx, "fx", [P, TILES, P])
        r, x3, res = (sbuf(nc, ctx, f"f{n}", [P, TILES, P]) for n in ("r", "x3", "res"))
        xT = sbuf(nc, ctx, "fxT", [P, CHUNK])
        ha, hb, hc, hd = (sbuf(nc, ctx, f"f{n}", [P, FC, CHUNK]) for n in ("ha", "hb", "hc", "hd"))
        stats, mv, rstd = sbuf(nc, ctx, "fst", [P, TILES, 6]), sbuf(nc, ctx, "fmv", [P, TILES, 2]), sbuf(nc, ctx, "frs", [P, TILES])
        w_in, c_in, out, s0 = (nc.alloc_semaphore(f"f_{n}") for n in ("w_in", "c_in", "out", "s0"))
        weights = [(wp[:, :, :], ins["wproj"]), (w1[:, :], ins["fw1"]), (w2[:, :], ins["fw2"]), (h1[:, :, :], ins["fh1"]),
                   (h2[:, :, :], ins["fh2"]), (w3[:, :, :], ins["fw3"]), (s3[:, :], ins["fs3"].partition_broadcast(P)),
                   (sc[:, :, :], ins["fsc"])]
        for d, s in weights:
            nc.sync.dma_start(d, s).then_inc(w_in, 16)
        nc.vector.memset(eps[:, :], EPS).then_inc(s0, 1)
        nc.scalar.wait_ge(s0, 1)
        for e in (nc.tensor, nc.vector, nc.scalar):
            e.wait_ge(w_in, 16 * len(weights))
        T, V, A = Lane(nc, nc.tensor, "f_T", PER["T"]), Lane(nc, nc.vector, "f_V", PER["V"]), Lane(nc, nc.scalar, "f_A", PER["A"])
        nc.sync.sem_inc(out, 16)
        ident = const["ident"][:, :]
        with nc.Fori(0, tokens // CHUNK) as it:
            for lane in (T, V, A):
                lane.begin(it)
            at = bass.ds(it * CHUNK, CHUNK)
            for e in (nc.sync, nc.tensor, nc.vector, nc.scalar):
                for lane in (T, V, A):
                    if lane.engine is not e:
                        lane.need(e, 0)
            nc.sync.dma_start(y[:, :, :], scr["y1"][:, at].rearrange("(k p) n -> p k n", p=P)).then_inc(c_in, 16)
            nc.sync.dma_start(x[:, :, :], scr["x2"][at, :].rearrange("(t p) d -> p t d", p=P)).then_inc(c_in, 16)
            nc.tensor.wait_ge(c_in, it * 32 + 32)
            nc.vector.wait_ge(c_in, it * 32 + 32)
            for t in range(TILES):
                for k in range(kc):
                    last = nc.tensor.matmul(ps[:, 0, t * P:(t + 1) * P], y[:, k, t * P:(t + 1) * P], wp[:, k, :],
                                            start=k == 0, stop=k == kc - 1)
            T.did(last)
            T.need(nc.vector, T.n)
            V.did(nc.vector.tensor_tensor(r[:, :, :], ps[:, 0, :].rearrange("p (t d) -> p t d", d=P), x[:, :, :], ALU.add))
            n3 = layernorm(nc, V, A, r, x3, stats, mv, rstd, eps, spare, V.n)
            V.need(nc.tensor, n3)
            a = turn(nc, T, A, x3, ps[:, 1, :], xT, ident)
            A.need(nc.tensor, a)
            for f in range(FC):
                nc.tensor.matmul(ps[:, f, :], w1[:, f * P:(f + 1) * P], xT[:, :], start=True, stop=True)
                n = T.did(nc.tensor.matmul(ps[:, 4 + f, :], w2[:, f * P:(f + 1) * P], xT[:, :], start=True, stop=True))
                T.need(nc.scalar, n)
                m = A.did(nc.scalar.activation(ha[:, f, :], ps[:, f, :], ACT.Silu, scale=sc[:, 0, f:f + 1]))
                A.need(nc.vector, m)
                V.did(nc.vector.scalar_tensor_tensor(hb[:, f, :], ps[:, 4 + f, :], sc[:, 1, f:f + 1], ha[:, f, :], ALU.mult, ALU.mult))
            V.need(nc.tensor, V.n)
            for w, src, dst, b0, row in ((h1, hb, hc, 0, 2), (h2, hc, hd, 4, 3)):
                for o in range(FC):
                    for k in range(FC):
                        last = nc.tensor.matmul(ps[:, b0 + o, :], w[:, k, o * P:(o + 1) * P], src[:, k, :], start=k == 0, stop=k == FC - 1)
                    T.did(last)
                    T.need(nc.scalar, T.n)
                    A.did(nc.scalar.activation(dst[:, o, :], ps[:, b0 + o, :], ACT.Gelu, scale=sc[:, row, o:o + 1]))
                A.need(nc.tensor, A.n)
            for t in range(TILES):
                for k in range(FC):
                    last = nc.tensor.matmul(ps[:, 0, t * P:(t + 1) * P], hd[:, k, t * P:(t + 1) * P], w3[:, k, :], start=k == 0, stop=k == FC - 1)
            T.did(last)
            T.need(nc.vector, T.n)
            V.did(nc.vector.tensor_tensor(r[:, :, :], ps[:, 0, :].rearrange("p (t d) -> p t d", d=P),
                                          s3[:, :].unsqueeze(1).to_broadcast([P, TILES, P]), ALU.mult))
            V.need(nc.vector, V.n)
            V.did(nc.vector.tensor_tensor(r[:, :, :], r[:, :, :], x3[:, :, :], ALU.add))
            nc.vector.wait_ge(out, it * 16 + 16)
            n4 = layernorm(nc, V, A, r, res, stats, mv, rstd, eps, spare, V.n)
            V.need(nc.sync, n4)
            nc.sync.dma_start(result[at, :].rearrange("(t p) d -> p t d", p=P), res[:, :, :]).then_inc(out, 16)
        settle(T, V, A)
        nc.sync.wait_ge(out, 16 * (tokens // CHUNK + 1))


def build(nc, ins, result, B, S, upto=5):
    tokens = B * S
    H0, H1, DIM1 = 16, 16, 64
    D0 = P // H0
    ps = nc.alloc_psum_tensor("ps", [P, 8, BANK], F32)

    def scratch(name, shape):
        return nc.dram_tensor(name, shape, F32, kind="Internal").ap()

    scr = {"q0": scratch("s_q0", [2, P, tokens]), "k0": scratch("s_k0", [2, P, tokens]), "v0": scratch("s_v0", [tokens, 512]),
           "y0": scratch("s_y0", [512, tokens]), "x2": scratch("s_x2", [tokens, P]), "ku": scratch("s_ku", [H1, DIM1]),
           "q1": scratch("s_q1", [2, H1 * DIM1, tokens]), "k1": scratch("s_k1", [2, H1 * DIM1, tokens]),
           "v1": scratch("s_v1", [tokens, H1 * DIM1]), "g1": scratch("s_g1", [4 * H1, tokens]),
           "y1": scratch("s_y1", [H1 * DIM1, tokens]), "zero": scratch("s_zero", [2 * S])}

    with ExitStack() as ctx:
        const = {n: sbuf(nc, ctx, f"c_{n}", s, d) for n, s, d in (
            ("ident", [P, P], F32), ("identb", [P, P], BF16), ("mask_ij", [P, P], BF16), ("mask_ji", [P, P], BF16),
            ("ones", [P, 32], F32), ("pick0", [P, 4], F32), ("pick1", [P, 4], F32), ("zero", [1, 2 * S], F32))}
        c_in, c_set = nc.alloc_semaphore("c_in"), nc.alloc_semaphore("c_set")
        with ExitStack() as tmp:
            mask = sbuf(nc, tmp, "c_mask", [P, 2, P])
            for d, s in ((const["ident"][:, :], ins["ident"]), (mask[:, :, :], ins["mask"]), (const["pick0"][:, :], ins["pick0"]),
                         (const["pick1"][:, :], ins["pick1"])):
                nc.sync.dma_start(d, s).then_inc(c_in, 16)
            nc.vector.wait_ge(c_in, 64)
            nc.vector.tensor_copy(const["identb"][:, :], const["ident"][:, :]).then_inc(c_set, 1)
            nc.vector.tensor_copy(const["mask_ij"][:, :], mask[:, 0, :]).then_inc(c_set, 1)
            nc.vector.tensor_copy(const["mask_ji"][:, :], mask[:, 1, :]).then_inc(c_set, 1)
            nc.vector.memset(const["ones"][:, :], 1.0).then_inc(c_set, 1)
            nc.vector.memset(const["zero"][:, :], 0.0).then_inc(c_set, 1)
            nc.sync.wait_ge(c_set, 5)
            nc.sync.dma_start(scr["zero"].rearrange("(a n) -> a n", a=1), const["zero"][:, :]).then_inc(c_in, 16)
            nc.sync.wait_ge(c_in, 80)
            barrier(nc)

        if upto >= 1:
            project0(nc, ps, const, ins, scr, tokens, H0)

        def batch(g, per):
            return g // per, g % per

        def head_rows(src, part, per, heads, dim):
            def of(g):
                b, m = batch(g, per)
                return src[part, bass.ds(m * (heads * dim), heads * dim), bass.ds(b * S, S)].rearrange("(h d) i -> d h i", d=dim)
            return of

        def values_of(src, per):
            def of(g):
                b, m = batch(g, per)
                return src[bass.ds(b * S, S), bass.ds(m * P, P)].rearrange("(t p) n -> p t n", p=P)
            return of

        def out_of(dst, per):
            def of(g, c):
                b, m = batch(g, per)
                return dst[bass.ds(m * P, P), bass.ds(b * S + c * BANK, BANK)]
            return of

        if upto >= 2:
            with ExitStack() as pos:
                p_in = nc.alloc_semaphore("a0_p_in")
                const["qpos"], const["kpos"] = sbuf(nc, pos, "c_qpos", [P, S]), sbuf(nc, pos, "c_kpos", [P, S])
                const["pick"] = const["pick0"]
                nc.sync.dma_start(const["qpos"][POS:P, :], ins["qpos"]).then_inc(p_in, 16)
                nc.sync.dma_start(const["kpos"][POS:P, :], ins["kpos0"]).then_inc(p_in, 16)
                nc.vector.wait_ge(p_in, 32)
                per = H0 // 4
                rows = [head_rows(scr["q0"], part, per, 4, D0) for part in range(2)]
                krows = [head_rows(scr["k0"], part, per, 4, D0) for part in range(2)]
                attention(nc, ps, const, "a0",
                          [((0, 8), rows[0]), ((8, 16), rows[0]), ((16, 24), rows[1])], None,
                          [((0, 8), krows[0]), ((8, 16), krows[1]), ((16, 24), krows[0])], None,
                          [], values_of(scr["v0"], per), out_of(scr["y0"], per), B * per, 4, S)

        if upto >= 3:
            middle(nc, ps, const, ins, scr, tokens, 8, 512, H1, DIM1)

        if upto >= 4:
            with ExitStack() as pos:
                p_in = nc.alloc_semaphore("a1_p_in")
                const["qpos"], const["kpos"] = sbuf(nc, pos, "c_qpos1", [P, S]), sbuf(nc, pos, "c_kpos1", [P, S])
                const["pick"] = const["pick1"]
                nc.sync.dma_start(const["qpos"][POS:P, :], ins["qpos"]).then_inc(p_in, 16)
                nc.sync.dma_start(const["kpos"][POS:P, :], ins["kpos1"]).then_inc(p_in, 16)
                nc.vector.wait_ge(p_in, 32)
                per = H1 // 2
                q = [head_rows(scr["q1"], part, per, 2, DIM1) for part in range(2)]
                k = [head_rows(scr["k1"], part, per, 2, DIM1) for part in range(2)]

                def slopes_of(g):
                    b, m = batch(g, per)
                    return scr["g1"].rearrange("(a h) n -> a h n", a=4)[:, bass.ds(m * 2, 2), bass.ds(b * S, S)]

                def zeros(g):
                    return scr["zero"].rearrange("(a h n) -> a h n", a=1, h=2)

                attention(nc, ps, const, "a1", [((0, 64), q[0])], [((0, 64), q[0]), ((64, 128), q[1])],
                          [((0, 64), k[0])], [((0, 64), k[1]), ((64, 128), k[0])],
                          [(True, (POS, POS + 4), slopes_of), (False, (MAXROW, MAXROW + 1), zeros)],
                          values_of(scr["v1"], per), out_of(scr["y1"], per), B * per, 2, S)

        if upto >= 5:
            final(nc, ps, const, ins, scr, result, tokens, 512, H1 * DIM1 // P)


def layout(a):
    f = np.float32
    x = a["L0_attn_x"]
    B, S, _ = x.shape
    E, _, F = a["L0_ffn_W1"].shape
    C = np.ascontiguousarray
    o = {"x": x.reshape(B * S, P)}
    o["wq0"], o["wk0"] = C(a["L0_attn_Wq"].T), C(a["L0_attn_Wk"].T)
    o["bq0"], o["bk0"] = a["L0_attn_bq"].reshape(P, 1), a["L0_attn_bk"].reshape(P, 1)
    wv = np.zeros((P, 16, 32), f)
    wv[:, :, 0:8] = a["L0_attn_Wv"].T.reshape(P, 16, 8)
    bv = np.zeros((16, 32), f)
    bv[:, 0:8] = a["L0_attn_bv"].reshape(16, 8)
    bv[:, 8] = 1.0
    o["wv0"], o["bv0"] = wv.reshape(P, 512), bv.reshape(512)
    wo = np.zeros((16, 32, P), f)
    wo[:, 0:8] = a["L0_attn_Wo"].T.reshape(16, 8, P)
    o["wo0"] = C(wo.reshape(4, P, P).transpose(1, 0, 2))
    o["bo0"] = a["L0_attn_bo"]
    o["cent"] = C(a["L0_ffn_centroids"].T)
    o["ln_g"], o["ln_b"] = C(a["L0_ffn_ln_g"].T), C(a["L0_ffn_ln_b"].T)
    o["w1"] = C(a["L0_ffn_W1"].transpose(1, 0, 2))
    o["b1"] = C(a["L0_ffn_b1"].reshape(E, F // P, P).transpose(2, 0, 1))
    o["w2"] = C(a["L0_ffn_W2"].reshape(E, F // P, P, P).transpose(2, 0, 1, 3))
    o["b2"] = a["L0_ffn_b2"]
    o["wq1"], o["wk1"], o["wv1"] = a["L1_attn_Wq"], a["L1_attn_Wk"], a["L1_attn_Wv"]
    o["wproj"] = C(a["L1_attn_Wproj"].reshape(8, P, P).transpose(1, 0, 2))
    o["qn"] = np.concatenate([a["L1_attn_q_rms_w"]] * 2).reshape(P, 1)
    o["kn"] = np.concatenate([a["L1_attn_k_rms_w"]] * 2).reshape(P, 1)
    o["kn_row"], o["u"], o["omega"] = a["L1_attn_k_rms_w"], a["L1_attn_u"], a["L1_attn_omega"]
    o["fw1"], o["fw2"] = C(a["L1_ffn_w1_w"].T), C(a["L1_ffn_w2_w"].T)
    o["fh1"] = C(a["L1_ffn_h1_w"].T.reshape(4, P, 512).transpose(1, 0, 2))
    o["fh2"] = C(a["L1_ffn_h2_w"].T.reshape(4, P, 512).transpose(1, 0, 2))
    o["fw3"] = C(a["L1_ffn_w3_w"].T.reshape(4, P, P).transpose(1, 0, 2))
    o["fs3"] = a["L1_ffn_w3_s"]
    o["fsc"] = C(np.stack([a[f"L1_ffn_{n}_s"].reshape(4, P) for n in ("w1", "w2", "h1", "h2")]).transpose(2, 0, 1))
    o["ident"] = np.eye(P, dtype=f)
    upper = np.triu(np.ones((P, P), f), 1)
    o["mask"] = C(np.stack([upper * f(MASKED), upper.T * f(MASKED)]).transpose(1, 0, 2))
    pos = np.arange(S, dtype=f) - f(S // 2)
    q = np.zeros((P - POS, S), f)
    q[0] = q[1] = -pos
    q[2] = q[3] = 1.0
    k0 = np.zeros((P - POS, S), f)
    k0[0], k0[2], k0[MAXROW - POS] = 1.0, pos, 1.0
    k1 = np.zeros((P - POS, S), f)
    k1[MAXROW - POS] = 1.0
    o["qpos"], o["kpos0"], o["kpos1"] = q, k0, k1
    o["jpos"] = C(np.tile(pos, B).reshape(B * S // CHUNK, TILES, P).transpose(0, 2, 1))
    o["slopes"] = np.array([2.0 ** (-(n + 1) / 2) for n in range(16)], f)
    o["iota"] = np.tile(np.arange(E, dtype=f) - E, (TILES, 1))
    p0, p1 = np.zeros((P, 4), f), np.zeros((P, 4), f)
    for n in range(4):
        p0[32 * n + 8, n] = 1.0
        p1[32 * n, n] = 1.0
    o["pick0"], o["pick1"] = p0, p1
    return o, B, S


def kernel(**inputs):
    import concourse.bacc as bacc
    from concourse.bass_utils import run_bass_kernel_spmd

    arrays, B, S = layout({k: np.asarray(v) for k, v in inputs.items()})
    nc = bacc.Bacc("TRN2", target_bir_lowering=False, num_devices=1)
    given, ins = {}, {}
    for name, a in arrays.items():
        given[f"in_{name}"] = np.ascontiguousarray(a)
        ins[name] = nc.dram_tensor(f"in_{name}", a.shape, mybir.dt.from_np(a.dtype), kind="ExternalInput").ap()
    result = nc.dram_tensor("out_0", (B * S, P), F32, kind="ExternalOutput").ap()
    build(nc, ins, result, B, S)
    r = run_bass_kernel_spmd(nc, [given], core_ids=[0])
    return r.results[0]["out_0"].reshape(B, S, P)
```

```python
from contextlib import ExitStack
from itertools import chain

import numpy as np

import concourse.bass as bass
from concourse import mybir
from concourse.alu_op_type import AluOpType as ALU

ACT = mybir.ActivationFunctionType
AX = mybir.AxisListType
F32 = mybir.dt.float32
F32R = mybir.dt.float32r
BF16 = mybir.dt.bfloat16

P = 128
BANK = 512
CHUNK = 512
TILES = CHUNK // P
EPS = 1e-5

POS = 64
MAXROW = 68
MASKED = -1e30
LOWEST = -3e38


class Lane:

    def __init__(self, nc, engine, name, per):
        self.sem, self.engine, self.per, self.base, self.n = nc.alloc_semaphore(name), engine, per, per, 0
        if per:
            engine.sem_inc(self.sem, per)

    def begin(self, it):
        self.base, self.n = it * self.per + self.per, 0

    def did(self, instruction, k=1):
        instruction.then_inc(self.sem, k)
        self.n += k
        return self.n

    def need(self, engine, number):
        if not (isinstance(self.base, int) and self.base + number == 0):
            engine.wait_ge(self.sem, self.base + number)



def settle(*lanes):
    found, said = [x.n for x in lanes], [x.per for x in lanes]
    assert found == said, (found, said)


def interleave(main, side, n_main, n_side):
    given, left = 0.0, 0
    for n, _ in enumerate(main):
        given += n_side / n_main
        while left < given and next(side, "end") != "end":
            left += 1
        if left < given:
            left = given
    for _ in side:
        pass


def barrier(nc):
    nc.all_engine_barrier()


def sbuf(nc, ctx, name, shape, dt=F32):
    return ctx.enter_context(nc.sbuf_tensor(name, shape, dt))


def attention(nc, ps, const, tag, qh, ql, kh, kl, extra, v_of, y_of, groups, heads, seq):
    NB = 4
    W = seq
    IT = seq // P
    HC = seq // BANK
    two = ql is not None and heads == 2
    wide = P // heads
    R = 4 * heads if heads > 2 else 12
    units = [(c, j) for c in range(HC) for j in range((c + 1) * BANK // P)]
    U = len(units) * heads
    assert U % R == 0 and HC == 2 and groups % NB == 0
    RING = 3
    rows = [(t, j0) for t in range(IT) for j0 in range(0, (t + 1) * P, BANK)]
    CH = len(rows) * heads
    assert CH % RING == 0 and U % RING == 0
    n_load = len(qh) + len(kh) + 1 + len(extra) + (len(ql) + len(kl) if two else 0)

    with ExitStack() as ctx:
        QA = [sbuf(nc, ctx, f"{tag}QA{b}", [P, heads, W], F32R) for b in range(NB)]
        KA = [sbuf(nc, ctx, f"{tag}KA{b}", [P, heads, W], F32R) for b in range(NB)]
        QB = [sbuf(nc, ctx, f"{tag}QB{b}", [P, heads, W], F32R) for b in range(NB)] if two else None
        KB = [sbuf(nc, ctx, f"{tag}KB{b}", [P, heads, W], F32R) for b in range(NB)] if two else None
        V = [sbuf(nc, ctx, f"{tag}V{b}", [P, IT, P]) for b in range(NB)]
        prob = sbuf(nc, ctx, f"{tag}prob", [P, R, BANK])
        mx = sbuf(nc, ctx, f"{tag}mx", [P, 2, heads, IT])
        mx2 = sbuf(nc, ctx, f"{tag}mx2", [P, 2, heads, IT // 2])
        negT = sbuf(nc, ctx, f"{tag}negT", [heads * IT, NB, P], F32R)
        spare = sbuf(nc, ctx, f"{tag}spare", [P, RING])
        if two:
            sums = sbuf(nc, ctx, f"{tag}sums", [P, HC, heads, BANK])
        else:
            den = sbuf(nc, ctx, f"{tag}den", [P, BANK])
        rec = sbuf(nc, ctx, f"{tag}rec", [P, TILES * heads])
        recw = sbuf(nc, ctx, f"{tag}recw", [P, TILES * heads, wide])
        recb = sbuf(nc, ctx, f"{tag}recb", [P, BANK])
        oT = sbuf(nc, ctx, f"{tag}oT", [P, HC, BANK])
        S1 = [ps[:, n, :] for n in range(RING)]
        S2 = [ps[:, RING + n, :] for n in range(RING)]
        O = ps[:, 6, :]
        D = ps[:, 7, :]

        ld = [nc.alloc_semaphore(f"{tag}_loaded{b}") for b in range(NB)]
        s1_full = nc.alloc_semaphore(f"{tag}_s1_full")
        s1_free = nc.alloc_semaphore(f"{tag}_s1_free")
        mx_done = nc.alloc_semaphore(f"{tag}_mx_done")
        t_full = nc.alloc_semaphore(f"{tag}_t_full")
        neg_full = nc.alloc_semaphore(f"{tag}_neg_full")
        row_full = [nc.alloc_semaphore(f"{tag}_row_full{b}") for b in range(NB)]
        s2_full = nc.alloc_semaphore(f"{tag}_s2_full")
        p_full = nc.alloc_semaphore(f"{tag}_p_full")
        p_free = nc.alloc_semaphore(f"{tag}_p_free")
        s2_masked = nc.alloc_semaphore(f"{tag}_s2_masked")
        summed = nc.alloc_semaphore(f"{tag}_summed")
        d_copied = nc.alloc_semaphore(f"{tag}_d_copied")
        d_turned = nc.alloc_semaphore(f"{tag}_d_turned")
        r_full = nc.alloc_semaphore(f"{tag}_r_full")
        rb_full = nc.alloc_semaphore(f"{tag}_rb_full")
        rb_copied = nc.alloc_semaphore(f"{tag}_rb_copied")
        o_done = nc.alloc_semaphore(f"{tag}_o_done")
        stored = [nc.alloc_semaphore(f"{tag}_stored{c}") for c in range(HC)]
        setup, zeroed = nc.alloc_semaphore(f"{tag}_setup"), nc.alloc_semaphore(f"{tag}_zeroed")

        nc.vector.sem_inc(s1_free, RING)
        nc.scalar.sem_inc(p_full, RING)
        nc.tensor.sem_inc(p_free, R)
        nc.vector.sem_inc(o_done, 1)
        DA = HC if two else 0
        if two:
            nc.gpsimd.sem_inc(summed, R)
            nc.tensor.sem_inc(d_turned, HC)
        for c in range(HC):
            nc.vector.sem_inc(stored[c], 16)
        def load(g, b, first=True, second=True):
            parts = []
            if first:
                parts += [(QA, r, s) for r, s in qh] + [(KA, r, s) for r, s in kh]
                if two:
                    parts += [(QB, r, s) for r, s in ql] + [(KB, r, s) for r, s in kl]
            if second:
                parts += [(KA if k else QA, r, s) for k, r, s in extra]
            for buf, (r0, r1), src in parts:
                nc.sync.dma_start(buf[b][r0:r1, :, :].bitcast(F32), src(g)).then_inc(ld[b], 16)
            if first:
                nc.sync.dma_start(V[b][:, :, :], v_of(g)).then_inc(ld[b], 16)

        def loaded(engine, r, b):
            engine.wait_ge(ld[b], (r + 1) * 16 * n_load)

        def maxima(g, r, b, h, t, j0):
            k = h * len(rows) + rows.index((t, j0))
            n = g * CH + k
            if k == 0:
                loaded(nc.tensor, r, b)
            if k == RING:
                nc.tensor.wait_ge(neg_full, g + 1)
            nc.tensor.wait_ge(s1_free, n + 1)
            j1 = min((t + 1) * P, j0 + BANK)
            s = S1[k % RING]
            diag = j1 == (t + 1) * P
            nc.tensor.matmul(s[:, 0:j1 - j0], QA[b][:, h, t * P:(t + 1) * P], KA[b][:, h, j0:j1], start=True, stop=True).then_inc(s1_full, 1)
            nc.vector.wait_ge(s1_full, n + 1)
            if diag:
                nc.vector.memset(spare[:, k % RING:k % RING + 1], 0.0)
                nc.vector.tensor_tensor_reduce(s[:, 0:j1 - j0], s[:, 0:j1 - j0], const["mask_ij"][:, BANK - (j1 - j0):BANK],
                                               1.0, LOWEST, ALU.add, ALU.max, mx[:, b % 2, h, t:t + 1]).then_inc(s1_free, 1)
            else:
                to = mx2[:, b % 2, h, t - IT // 2:t - IT // 2 + 1]
                nc.vector.tensor_reduce(to, s[:, 0:j1 - j0], axis=AX.X, op=ALU.max).then_inc(s1_free, 1)

        def turn_maxima(g, b, ahead):
            nc.vector.wait_ge(s1_free, (g + 1) * CH + RING)
            upper = mx[:, b % 2, :, IT // 2:IT]
            nc.vector.tensor_tensor(upper, upper, mx2[:, b % 2, :, :], ALU.max).then_inc(mx_done, 1)
            nc.tensor.wait_ge(mx_done, g + 1)
            if ahead:
                nc.tensor.wait_ge(s1_free, (g + 1) * CH + RING + 1)
            nc.tensor.transpose(S1[0][0:heads * IT, 0:P], mx[:, b % 2, :, :].rearrange("p h t -> p (h t)"), const["ident"][:, :]).then_inc(t_full, 1)
            nc.vector.wait_ge(t_full, g + 1)
            nc.vector.tensor_scalar(negT[:, b, :], S1[0][0:heads * IT, 0:P], -1.0, None, ALU.mult).then_inc(neg_full, 1)
            nc.sync.wait_ge(neg_full, g + 2)
            nc.sync.dma_start(QA[b][MAXROW:MAXROW + 1, :, :].bitcast(F32), negT[:, b, :].bitcast(F32)).then_inc(row_full[b], 16)

        def masks_before(g, u):
            before, all_of_them = (sum(1 for c, j in units[:n] if j * P >= c * BANK) for n in (u, len(units)))
            return (g * all_of_them + before) * heads

        def exponentials(g, r, b, u, h):
            c, j = units[u]
            k = u * heads + h
            n = g * U + k
            if k == 0:
                nc.tensor.wait_ge(row_full[b], (r + 1) * 16)
            off = max(0, j * P - c * BANK)
            i0, i1 = c * BANK + off, (c + 1) * BANK
            s = S2[k % RING][:, off:BANK]
            diag = j * P >= c * BANK
            nc.tensor.wait_ge(p_full, n + 1)
            added = diag and not two
            last = nc.tensor.matmul(s, KA[b][:, h, j * P:(j + 1) * P], QA[b][:, h, i0:i1], start=True, stop=not (two or added))
            if two:
                last = nc.tensor.matmul(s, KB[b][:, h, j * P:(j + 1) * P], QB[b][:, h, i0:i1], start=False, stop=True)
            if added:
                last = nc.tensor.matmul(S2[k % RING][:, off:off + P], const["identb"][:, :], const["mask_ji_add"][:, :],
                                        start=False, stop=True)
            last.then_inc(s2_full, 1)
            if diag and not added:
                nc.vector.wait_ge(s2_full, n + 1)
                tile = s[:, 0:P]
                nc.vector.tensor_tensor(tile, tile, const["mask_ji"][:, :], ALU.min).then_inc(s2_masked, 1)
                nc.scalar.wait_ge(s2_masked, masks_before(g, u) + h + 1)
            else:
                nc.scalar.wait_ge(s2_full, n + 1)
            nc.scalar.wait_ge(p_free, n + 1)
            if two:
                nc.scalar.wait_ge(summed, n + 1)
            nc.scalar.activation(prob[:, k % R, off:BANK], s, ACT.Exp).then_inc(p_full, 1)

        def add_up(g, u, h):
            c, j = units[u]
            k = u * heads + h
            off = max(0, j * P - c * BANK)
            pool, total = nc.gpsimd, sums[:, c, h, :]
            if j == 0:
                if h == 0:
                    pool.wait_ge(d_turned, g * HC + c + 1)
                pool.wait_ge(p_full, g * U + k + 1 + RING)
                pool.tensor_tensor(total, prob[:, k % R, :], const["zero"][:, :], ALU.add).then_inc(summed, 1)
                return
            pool.wait_ge(p_full, g * U + k + 1 + RING)
            pool.wait_ge(summed, g * U + k + R - heads + 1)
            pool.tensor_tensor(total[:, off:BANK], total[:, off:BANK], prob[:, k % R, off:BANK], ALU.add).then_inc(summed, 1)

        def values(g, b, u):
            c, j = units[u]
            off = max(0, j * P - c * BANK)
            first, final = j == 0, u + 1 == len(units) or units[u + 1][0] != c
            if first:
                nc.tensor.wait_ge(o_done, g * HC + c + 1)
            nc.tensor.wait_ge(p_full, g * U + (u + 1) * heads + RING)
            for h in range(heads):
                k = u * heads + h
                last = nc.tensor.matmul(O[h * wide:(h + 1) * wide, off:BANK], V[b][:, j, h * wide:(h + 1) * wide],
                                        prob[:, k % R, off:BANK], start=first, stop=final)
            last.then_inc(p_free, heads)

        def copy_den(g, c):
            if two:
                return
            done = sum(1 for x in units if x[0] <= c) * heads
            nc.scalar.wait_ge(p_free, g * U + done + R)
            nc.scalar.activation(den[:, :], O, ACT.Copy).then_inc(d_copied, 1)

        def turn_den(g, c):
            if two:
                nc.tensor.wait_ge(summed, g * U + sum(1 for x in units if x[0] <= c) * heads + R)
                nc.tensor.wait_ge(o_done, g * HC + c + 1)
                for t in range(TILES):
                    for h in range(heads):
                        n = t * heads + h
                        last = nc.tensor.matmul(D[:, n:n + 1], sums[:, c, h, t * P:(t + 1) * P], const["ones"][:, 0:1], start=True, stop=True)
            else:
                nc.tensor.wait_ge(d_copied, g * HC + c + 1)
                for t in range(TILES):
                    last = nc.tensor.matmul(D[:, t * heads:(t + 1) * heads], den[:, t * P:(t + 1) * P], const["pick"][:, 0:heads],
                                            start=True, stop=True)
            last.then_inc(d_turned, 1)
            nc.vector.wait_ge(d_turned, g * HC + c + 1 + DA)
            nc.vector.reciprocal(rec[:, :], D[:, 0:TILES * heads]).then_inc(r_full, 1)
            nc.vector.wait_ge(r_full, (g * HC + c) * 2 + 1)
            nc.vector.tensor_copy(recw[:, :, :], rec[:, :].unsqueeze(2).to_broadcast([P, TILES * heads, wide])).then_inc(r_full, 1)

        def spread(g, c):
            nc.tensor.wait_ge(r_full, (g * HC + c) * 2 + 2)
            for t in range(TILES):
                lhs = recw[:, t * heads:(t + 1) * heads, :].rearrange("p h w -> p (h w)")
                last = nc.tensor.matmul(D[:, t * P:(t + 1) * P], lhs, const["ident"][:, :], start=True, stop=True)
            last.then_inc(rb_full, 1)
            nc.scalar.wait_ge(rb_full, g * HC + c + 1)
            nc.scalar.activation(recb[:, :], D, ACT.Copy).then_inc(rb_copied, 1)

        def normalise(g, c):
            nc.vector.wait_ge(rb_copied, g * HC + c + 1)
            nc.vector.wait_ge(stored[c], (g + 1) * 16)
            nc.vector.tensor_tensor(oT[:, c, :], O, recb[:, :], ALU.mult).then_inc(o_done, 1)
            nc.sync.wait_ge(o_done, g * HC + c + 2)
            nc.sync.dma_start(y_of(g, c), oT[:, c, :]).then_inc(stored[c], 16)

        class Maxima:

            def __init__(self, g, r, b, there=True, turn=True):
                self.g, self.r, self.b, self.turn, self.there = g, r, b, turn, there
                self.todo = [(h, t, j0) for h in range(heads) for t, j0 in rows] if there else []
                self.total = len(self.todo)

            def give(self, share):
                while self.todo and self.total - len(self.todo) < self.total * share:
                    maxima(self.g, self.r, self.b, *self.todo.pop(0))
                    if self.total - len(self.todo) == RING:
                        self.give_turn()
                if not self.there:
                    self.give_turn()

            def give_turn(self):
                if self.turn:
                    turn_maxima(self.g - 1, (self.b - 1) % NB, self.there)
                    self.turn = False

        def finish(g, b, c, part):
            if part == 0:
                values(g, b, last_unit[c])
                copy_den(g, c)
            elif part == 1:
                turn_den(g, c)
            else:
                spread(g, c)
                normalise(g, c)

        def block(g, r, b, c, before, ahead, share0, share1):
            mine = [u for u, (cu, _) in enumerate(units) if cu == c]
            for n, u in enumerate(mine):
                for h in range(heads):
                    exponentials(g, r, b, u, h)
                    if two:
                        add_up(g, u, h)
                    ahead.give(share0 + (share1 - share0) * (n * heads + h + 1) / (len(mine) * heads))
                if n < 3:
                    if before:
                        finish(*before, n)
                else:
                    for x in (mine[0:3] if n == 3 else mine[n - 1:n]):
                        values(g, b, x)

        last_unit = [max(u for u, (cu, _) in enumerate(units) if cu == c) for c in range(HC)]

        def step(g, r, b, r1, r2, more, most):
            b1, b2 = (b + 1) % NB, (b + 2) % NB
            ahead = Maxima(g + 2, r2, b2, most, more)
            block(g, r, b, 1, (g, b, 0), ahead, 0, 2 / 3 if more else 1)
            if more:
                block(g + 1, r1, b1, 0, (g, b, 1), ahead, 2 / 3, 1)

        def load_when_free(g, b):
            nc.sync.wait_ge(p_free, (g - NB + 1) * U + R)
            load(g, b)

        for b in range(NB):
            load(b, b, second=False)
        n = n_zero = 0
        for b in range(NB):
            for buf, pos, engine, copy in ((QA, const["qpos"], nc.vector, nc.vector.tensor_copy), (KA, const["kpos"], nc.gpsimd, nc.scalar.copy)):
                for h in range(heads):
                    copy(buf[b][POS:P, h, :], pos[POS:P, :]).then_inc(setup, 1)
                    n += 1
                if not two:
                    engine.memset(buf[b][32:POS, :, :].bitcast(F32), 0.0).then_inc(setup, 1)
                    n += 1
                    for h in range(0, heads, 2):
                        nc.scalar.dma_start(buf[b][24:32, h:h + 2, :].bitcast(F32), const["zeros"].partition_broadcast(8)).then_inc(zeroed, 16)
                        n_zero += 16
        for engine in (nc.sync, nc.tensor):
            engine.wait_ge(setup, n)
            if n_zero:
                engine.wait_ge(zeroed, n_zero)
        for b in range(NB):
            load(b, b, first=False)
        nc.vector.sem_inc(neg_full, 1)
        Maxima(0, 0, 0, turn=False).give(1)
        ahead = Maxima(1, 0, 1)
        ahead.give(RING / CH)
        block(0, 0, 0, 0, None, ahead, RING / CH, 1)
        body = groups // NB
        with nc.Fori(0, body - 1) as it:
            nc.disable_value_cache = True
            for b in range(NB):
                g = it * NB + b
                step(g, it, b, it + (b + 1) // NB, it + (b + 2) // NB, True, True)
                load_when_free(g + NB, b)
        for b in range(NB):
            step((body - 1) * NB + b, body - 1, b, body - 1, body - 1, b < 3, b < 2)
        for part in range(3):
            finish(groups - 1, NB - 1, 1, part)
        for c in range(HC):
            nc.sync.wait_ge(stored[c], 16 * (groups + 1))
        barrier(nc)


def layernorm(nc, V, A, x, out, stats, mv, rstd, eps, spare, after):
    V.need(nc.vector, after)
    for t in range(TILES):
        V.did(nc.vector.bn_stats(stats[:, t, :], x[:, t, :]))
    V.need(nc.vector, V.n)
    nc.vector.memset(spare[:, 0:1], 0.0)
    for t in range(TILES):
        V.did(nc.vector.bn_aggr(mv[:, t, :], stats[:, t, :]))
    V.need(nc.scalar, V.n)
    A.did(nc.scalar.activation(rstd[:, :], mv[:, :, 1], ACT.Sqrt, bias=eps[:, 0:1]))
    A.need(nc.vector, A.n)
    V.did(nc.vector.reciprocal(rstd[:, :], rstd[:, :]))
    V.need(nc.vector, V.n)
    for t in range(TILES):
        V.did(nc.vector.tensor_scalar(out[:, t, :], x[:, t, :], mv[:, t, 0:1], rstd[:, t:t + 1],
                                      ALU.subtract, ALU.mult))
    return V.n


def turn(nc, T, A, src, bank, dst, ident):
    for t in range(TILES):
        last = nc.tensor.transpose(bank[:, t * P:(t + 1) * P], src[:, t, :], ident)
    n = T.did(last)
    T.need(nc.scalar, n)
    return A.did(nc.scalar.activation(dst[:, :], bank, ACT.Copy))


def project0(nc, ps, const, ins, scr, tokens, heads):
    scale = float(1.0 / np.sqrt(np.float32(P // heads)))
    PER = {"T": 7, "V": 8, "A": 3}
    with ExitStack() as ctx:
        wq, wk = sbuf(nc, ctx, "p0wq", [P, P]), sbuf(nc, ctx, "p0wk", [P, P])
        wv, bv = sbuf(nc, ctx, "p0wv", [P, BANK]), sbuf(nc, ctx, "p0bv", [P, BANK])
        bq, bk = sbuf(nc, ctx, "p0bq", [P, 1]), sbuf(nc, ctx, "p0bk", [P, 1])
        x = sbuf(nc, ctx, "p0x", [P, TILES, P])
        xT = sbuf(nc, ctx, "p0xT", [P, CHUNK])
        full = sbuf(nc, ctx, "p0full", [P, 2, CHUNK])
        high = sbuf(nc, ctx, "p0high", [P, 2, CHUNK], F32R)
        low = sbuf(nc, ctx, "p0low", [P, 2, CHUNK], F32R)
        v = sbuf(nc, ctx, "p0v", [P, TILES, BANK])
        w_in, x_in, out = (nc.alloc_semaphore(f"p0_{s}") for s in ("w_in", "x_in", "out"))
        T, V, A = Lane(nc, nc.tensor, "p0_T", PER["T"]), Lane(nc, nc.vector, "p0_V", PER["V"]), Lane(nc, nc.scalar, "p0_A", PER["A"])
        for d, s in ((wq, ins["wq0"]), (wk, ins["wk0"]), (wv, ins["wv0"]), (bq, ins["bq0"]), (bk, ins["bk0"]),
                     (bv, ins["bv0"].partition_broadcast(P))):
            nc.sync.dma_start(d[:, :], s).then_inc(w_in, 16)
        nc.tensor.wait_ge(w_in, 96)
        nc.vector.wait_ge(w_in, 96)
        nc.sync.sem_inc(out, 16 * 5)
        with nc.Fori(0, tokens // CHUNK) as it:
            for lane in (T, V, A):
                lane.begin(it)
            T.need(nc.sync, 0)
            nc.sync.dma_start(x[:, :, :], ins["x"][bass.ds(it * CHUNK, CHUNK), :].rearrange("(t p) d -> p t d", p=P)).then_inc(x_in, 16)
            nc.tensor.wait_ge(x_in, it * 16 + 16)
            V.need(nc.tensor, 0)
            A.need(nc.tensor, 0)
            xt = turn(nc, T, A, x, ps[:, 0, :], xT, const["ident"][:, :])
            A.need(nc.tensor, xt)
            T.did(nc.tensor.matmul(ps[:, 1, :], wq[:, :], xT[:, :], start=True, stop=True))
            k_at = T.did(nc.tensor.matmul(ps[:, 2, :], wk[:, :], xT[:, :], start=True, stop=True))
            v_at = [T.did(nc.tensor.matmul(ps[:, 3 + t, :], xT[:, t * P:(t + 1) * P], wv[:, :], start=True, stop=True))
                    for t in range(TILES)]
            nc.vector.wait_ge(out, it * 16 * 5 + 16 * 5)
            T.need(nc.vector, k_at)
            V.did(nc.vector.tensor_scalar(full[:, 0, :], ps[:, 1, :], bq[:, 0:1], scale, ALU.add, ALU.mult))
            f = V.did(nc.vector.tensor_scalar(full[:, 1, :], ps[:, 2, :], bk[:, 0:1], None, ALU.add))
            V.need(nc.scalar, f)
            A.did(nc.scalar.activation(high[:, 0, :], full[:, 0, :], ACT.Copy))
            hi = A.did(nc.scalar.activation(high[:, 1, :], full[:, 1, :], ACT.Copy))
            for t in range(TILES):
                T.need(nc.vector, v_at[t])
                V.did(nc.vector.tensor_tensor(v[:, t, :], ps[:, 3 + t, :], bv[:, :], ALU.add))
            A.need(nc.vector, hi)
            for n in range(2):
                V.did(nc.vector.tensor_tensor(low[:, n, :], full[:, n, :], high[:, n, :].bitcast(F32), ALU.subtract))
            V.need(nc.sync, V.n)
            A.need(nc.sync, hi)
            at = bass.ds(it * CHUNK, CHUNK)
            nc.sync.dma_start(scr["v0"][at, :].rearrange("(t p) n -> p t n", p=P), v[:, :, :]).then_inc(out, 16)
            for n, name in enumerate(("q0", "k0")):
                nc.sync.dma_start(scr[name][0, :, at], high[:, n, :].bitcast(F32)).then_inc(out, 16)
                nc.sync.dma_start(scr[name][1, :, at], low[:, n, :].bitcast(F32)).then_inc(out, 16)
        settle(T, V, A)
        nc.sync.wait_ge(out, 16 * 5 * (tokens // CHUNK + 1))
        barrier(nc)


def middle(nc, ps, const, ins, scr, tokens, experts, hidden, heads, dim):
    PER = {"T": 77, "V": 142, "A": 79}
    KC = 4
    FC = hidden // P
    HD = heads * dim
    PAIRS = HD // P
    with ExitStack() as ctx:
        wo = sbuf(nc, ctx, "mwo", [P, KC, P])
        bo = sbuf(nc, ctx, "mbo", [P, P])
        cent = sbuf(nc, ctx, "mcent", [P, experts])
        gT, bT = sbuf(nc, ctx, "mg", [P, experts]), sbuf(nc, ctx, "mb", [P, experts])
        w1 = sbuf(nc, ctx, "mw1", [P, experts, hidden])
        b1 = sbuf(nc, ctx, "mb1", [P, experts, FC])
        w2 = sbuf(nc, ctx, "mw2", [P, experts, FC, P])
        b2 = sbuf(nc, ctx, "mb2", [experts, P])
        wq, wk, wv = (sbuf(nc, ctx, f"m{n}", [P, HD]) for n in ("wq", "wk", "wv"))
        wqn, wkn = sbuf(nc, ctx, "mwqn", [P, 1]), sbuf(nc, ctx, "mwkn", [P, 1])
        u, kw = sbuf(nc, ctx, "mu", [heads, dim]), sbuf(nc, ctx, "mkw", [heads, dim])
        usq, us = sbuf(nc, ctx, "musq", [heads, dim]), sbuf(nc, ctx, "mus", [heads, 1])
        G = sbuf(nc, ctx, "mG", [P, heads])
        om, om1, slopes = (sbuf(nc, ctx, f"m{n}", [P, heads]) for n in ("om", "om1", "slopes"))
        iota = sbuf(nc, ctx, "miota", [P, TILES, experts])
        eps, spare = sbuf(nc, ctx, "meps", [P, 1]), sbuf(nc, ctx, "mspare", [P, 1])

        y, x = sbuf(nc, ctx, "my", [P, KC, CHUNK]), sbuf(nc, ctx, "mx0", [P, TILES, P])
        jpos = sbuf(nc, ctx, "mjpos", [P, TILES])
        r1 = sbuf(nc, ctx, "mr1", [P, TILES, P])
        x1n, xn, accn, acc, x2 = (sbuf(nc, ctx, f"m{n}", [P, TILES, P]) for n in ("x1", "xn", "accn", "acc", "x2"))
        xT, x1T, xnTn, xnT = (sbuf(nc, ctx, f"m{n}", [P, CHUNK]) for n in ("xT", "x1T", "xnTn", "xnT"))
        xe = sbuf(nc, ctx, "mxe", [P, 2, CHUNK])
        stats, mv, rstd = sbuf(nc, ctx, "mst", [P, TILES, 6]), sbuf(nc, ctx, "mmv", [P, TILES, 2]), sbuf(nc, ctx, "mrs", [P, TILES])
        top = sbuf(nc, ctx, "mtop", [P, TILES])
        eq, oh, ohn = (sbuf(nc, ctx, f"m{n}", [P, TILES, experts]) for n in ("eq", "oh", "ohn"))
        ohT = sbuf(nc, ctx, "mohT", [experts, CHUNK])
        h = sbuf(nc, ctx, "mh", [P, 2, FC, CHUNK])
        sq = sbuf(nc, ctx, "msq", [P, HD])
        ss = sbuf(nc, ctx, "mss", [P, 2 * heads])
        qk = sbuf(nc, ctx, "mqk", [P, 2, HD])
        v = sbuf(nc, ctx, "mval", [P, HD])
        high, low = sbuf(nc, ctx, "mhi", [P, 2, PAIRS, P], F32R), sbuf(nc, ctx, "mlo", [P, 2, PAIRS, P], F32R)
        z, zabs, g, gj = (sbuf(nc, ctx, f"m{n}", [P, TILES, heads]) for n in ("z", "zabs", "slope", "gj"))
        aug = sbuf(nc, ctx, "maug", [P, TILES, P // heads, heads], F32R)
        augT = sbuf(nc, ctx, "maugT", [4 * heads, CHUNK])

        sem = lambda n: nc.alloc_semaphore(f"m_{n}")
        w_in, c_in, j_in = sem("w_in"), sem("c_in"), sem("j_in")
        out_x, out_g, out_v, out_qk = sem("out_x"), sem("out_g"), sem("out_v"), sem("out_qk")
        s0, s1 = sem("setup_v"), sem("setup_a")
        weights = [(wo[:, :, :], ins["wo0"]), (bo[:, :], ins["bo0"].partition_broadcast(P)), (cent[:, :], ins["cent"]),
                   (gT[:, :], ins["ln_g"]), (bT[:, :], ins["ln_b"]), (w1[:, :, :], ins["w1"]), (b1[:, :, :], ins["b1"]),
                   (w2[:, :, :, :], ins["w2"]), (b2[:, :], ins["b2"]), (wq[:, :], ins["wq1"]), (wk[:, :], ins["wk1"]),
                   (wv[:, :], ins["wv1"]), (wqn[:, :], ins["qn"]), (wkn[:, :], ins["kn"]), (u[:, :], ins["u"]),
                   (kw[:, :], ins["kn_row"].partition_broadcast(heads)), (om[:, :], ins["omega"].partition_broadcast(P)),
                   (slopes[:, :], ins["slopes"].partition_broadcast(P)),
                   (iota[:, :, :], ins["iota"].partition_broadcast(P))]
        for d, s in weights:
            nc.sync.dma_start(d, s).then_inc(w_in, 16)
        n_w = 16 * len(weights)
        for e in (nc.tensor, nc.vector, nc.scalar):
            e.wait_ge(w_in, n_w)

        dv, ac = [0], [0]

        def dve(ins_):
            dv[0] += 1
            ins_.then_inc(s0, 1)
            nc.vector.wait_ge(s0, dv[0])

        def act(ins_):
            ac[0] += 1
            nc.vector.wait_ge(s1, ac[0])
            return ins_
        dve(nc.vector.memset(eps[:, :], EPS))
        dve(nc.vector.memset(aug[:, :, :, :].bitcast(F32), 0.0))
        dve(nc.vector.tensor_scalar(wqn[:, :], wqn[:, :], float(1.0 / np.sqrt(dim)), None, ALU.mult))
        dve(nc.vector.tensor_tensor(usq[:, :], u[:, :], u[:, :], ALU.mult))
        dve(nc.vector.tensor_reduce(us[:, :], usq[:, :], axis=AX.X, op=ALU.add))
        nc.scalar.wait_ge(s0, dv[0])
        nc.scalar.activation(us[:, :], us[:, :], ACT.Sqrt).then_inc(s1, 1)
        nc.vector.wait_ge(s1, 1)
        dve(nc.vector.tensor_scalar(us[:, :], us[:, :], 1e-6, None, ALU.max))
        dve(nc.vector.reciprocal(us[:, :], us[:, :]))
        dve(nc.vector.scalar_tensor_tensor(usq[:, :], u[:, :], us[:, 0:1], kw[:, :], ALU.mult, ALU.mult))
        nc.sync.wait_ge(s0, dv[0])
        nc.sync.dma_start(scr["ku"], usq[:, :]).then_inc(w_in, 16)
        nc.sync.wait_ge(w_in, n_w + 16)
        nc.sync.dma_start(sq[:, 0:HD], scr["ku"].rearrange("h d -> (h d)").partition_broadcast(P)).then_inc(w_in, 16)
        nc.vector.wait_ge(w_in, n_w + 32)
        dve(nc.vector.tensor_tensor(sq[:, 0:HD], sq[:, 0:HD], wk[:, :], ALU.mult))
        dve(nc.vector.tensor_reduce(G[:, :], sq[:, 0:HD].rearrange("p (h d) -> p h d", d=dim), axis=AX.X, op=ALU.add))
        dve(nc.vector.tensor_scalar(G[:, :], G[:, :], float(1.0 / np.sqrt(dim)), None, ALU.mult))
        dve(nc.vector.scalar_tensor_tensor(om1[:, :], om[:, :], -1.0, om[:, :], ALU.mult, ALU.max))
        nc.scalar.wait_ge(s0, dv[0])
        nc.scalar.activation(om1[:, :], om1[:, :], ACT.Exp, scale=-1.0).then_inc(s1, 1)
        nc.scalar.wait_ge(s1, 2)
        nc.scalar.activation(om1[:, :], om1[:, :], ACT.Ln, bias=1.0).then_inc(s1, 1)
        nc.vector.wait_ge(s1, 3)
        dve(nc.vector.scalar_tensor_tensor(om[:, :], om[:, :], 0.0, om1[:, :], ALU.max, ALU.add))
        dve(nc.vector.tensor_tensor(om[:, :], om[:, :], slopes[:, :], ALU.mult))
        nc.tensor.wait_ge(s0, dv[0])
        nc.scalar.wait_ge(s0, dv[0])

        ident = const["ident"][:, :]
        steps = tokens // CHUNK
        nc.sync.sem_inc(out_x, 16)
        nc.sync.sem_inc(out_g, 16)
        nc.sync.sem_inc(out_v, 16)
        nc.sync.sem_inc(out_qk, 64)

        def tiled(view):
            return view.rearrange("p (t d) -> p t d", d=P)

        def load(c, T, V, A):
            at = bass.ds(c * CHUNK, CHUNK)
            for lane in (T, V, A):
                lane.need(nc.sync, lane.n)
            nc.sync.dma_start(y[:, :, :], scr["y0"][:, at].rearrange("(k p) n -> p k n", p=P)).then_inc(c_in, 16)
            nc.sync.dma_start(x[:, :, :], ins["x"][at, :].rearrange("(t p) d -> p t d", p=P)).then_inc(c_in, 16)

        def before(c, T, V, A):
            V.need(nc.tensor, V.n)
            A.need(nc.tensor, A.n)
            nc.tensor.wait_ge(c_in, c * 32 + 32)
            nc.vector.wait_ge(c_in, c * 32 + 32)
            for t in range(TILES):
                for k in range(KC):
                    last = nc.tensor.matmul(ps[:, 4, t * P:(t + 1) * P], y[:, k, t * P:(t + 1) * P], wo[:, k, :],
                                            start=k == 0, stop=k == KC - 1)
                if t < TILES - 1:
                    yield
            pr = T.did(last)
            T.need(nc.vector, pr)
            V.did(nc.vector.tensor_tensor(r1[:, :, :], tiled(ps[:, 4, :]), x[:, :, :], ALU.add))
            V.need(nc.vector, V.n)
            V.did(nc.vector.tensor_tensor(r1[:, :, :], r1[:, :, :], bo[:, :].unsqueeze(1).to_broadcast([P, TILES, P]), ALU.add))
            n1 = layernorm(nc, V, A, r1, x1n, stats, mv, rstd, eps, spare, V.n)
            yield
            V.need(nc.tensor, n1)
            a = turn(nc, T, A, x1n, ps[:, 5, :], x1T, ident)
            n = layernorm(nc, V, A, x1n, xn, stats, mv, rstd, eps, spare, n1)
            yield
            A.need(nc.tensor, a)
            for t in range(TILES):
                last = nc.tensor.matmul(ps[:, 6, t * experts:(t + 1) * experts], x1T[:, t * P:(t + 1) * P], cent[:, :],
                                        start=True, stop=True)
            lg = T.did(last)
            V.need(nc.tensor, n)
            turn(nc, T, A, xn, ps[:, 7, :], xnTn, ident)
            T.need(nc.vector, lg)
            logits = ps[:, 6, 0:TILES * experts].rearrange("p (t e) -> p t e", e=experts)
            per_tile = [P, TILES, experts]
            V.did(nc.vector.tensor_reduce(top[:, :], logits, axis=AX.X, op=ALU.max))
            V.need(nc.vector, V.n)
            V.did(nc.vector.tensor_tensor(eq[:, :, :], logits, top[:, :].unsqueeze(2).to_broadcast(per_tile), ALU.is_equal))
            V.need(nc.vector, V.n)
            V.did(nc.vector.tensor_tensor(eq[:, :, :], eq[:, :, :], iota[:, :, :], ALU.mult))
            V.need(nc.vector, V.n)
            V.did(nc.vector.tensor_reduce(top[:, :], eq[:, :, :], axis=AX.X, op=ALU.min))
            V.need(nc.vector, V.n)
            o = V.did(nc.vector.tensor_tensor(ohn[:, :, :], iota[:, :, :], top[:, :].unsqueeze(2).to_broadcast(per_tile), ALU.is_equal))
            yield
            V.need(nc.tensor, o)
            for t in range(TILES):
                last = nc.tensor.transpose(ps[0:experts, 4, t * P:(t + 1) * P], ohn[:, t, :], ident)
            T.did(last)
            T.need(nc.scalar, T.n)
            oa = A.did(nc.scalar.activation(ohT[:, :], ps[0:experts, 4, :], ACT.Copy))
            yield
            A.need(nc.tensor, oa)
            for t in range(TILES):
                last = nc.tensor.matmul(ps[:, 5, t * P:(t + 1) * P], ohT[:, t * P:(t + 1) * P], b2[:, :], start=True, stop=True)
            T.did(last)
            T.need(nc.vector, T.n)
            V.did(nc.vector.scalar_tensor_tensor(accn[:, :, :], x1n[:, :, :], 2.0, tiled(ps[:, 5, :]), ALU.mult, ALU.add))
            yield

        def moe(T, V, A):
            xe_at, up_at, h_at, h_read, y_at = {}, {}, {}, {}, {}
            ring, acc_at = [], V.n

            def scaled(e):
                if e >= 2:
                    T.need(nc.vector, up_at[e - 2])
                xe_at[e] = V.did(nc.vector.tensor_scalar(xe[:, e % 2, :], xnT[:, :], gT[:, e:e + 1], bT[:, e:e + 1], ALU.mult, ALU.add))

            V.need(nc.vector, V.n)
            scaled(0)
            for e in range(experts + 1):
                if e < experts:
                    if e + 1 < experts:
                        scaled(e + 1)
                    V.need(nc.tensor, xe_at[e])
                    for f in range(FC):
                        if len(ring) >= 2:
                            A.need(nc.tensor, ring[-2])
                        m = T.did(nc.tensor.matmul(ps[:, len(ring) % 2, :], w1[:, e, f * P:(f + 1) * P], xe[:, e % 2, :], start=True, stop=True))
                        T.need(nc.scalar, m)
                        if f == 0 and e >= 2:
                            T.need(nc.scalar, y_at[e - 2])
                        ring.append(A.did(nc.scalar.activation(h[:, e % 2, f, :], ps[:, len(ring) % 2, :], ACT.Relu, bias=b1[:, e, f:f + 1])))
                        yield
                    up_at[e], h_at[e] = m, ring[-1]
                if e:
                    d = e - 1
                    A.need(nc.tensor, h_at[d])
                    V.need(nc.tensor, acc_at)
                    for t in range(TILES):
                        for f in range(FC):
                            last = nc.tensor.matmul(ps[:, 2, t * P:(t + 1) * P], h[:, d % 2, f, t * P:(t + 1) * P], w2[:, d, f, :],
                                                    start=f == 0, stop=f == FC - 1)
                        if t < TILES - 1:
                            yield
                    y_at[d] = T.did(last)
                    T.need(nc.vector, y_at[d])
                    V.need(nc.vector, acc_at)
                    for t in range(TILES):
                        acc_at = V.did(nc.vector.scalar_tensor_tensor(acc[:, t, :], ps[:, 2, t * P:(t + 1) * P], oh[:, t, d:d + 1],
                                                                      acc[:, t, :], ALU.mult, ALU.add))
                    yield

        def handover(T, V, A):
            A.need(nc.vector, A.n)
            T.need(nc.vector, T.n)
            V.need(nc.vector, V.n)
            V.did(nc.vector.tensor_copy(acc[:, :, :], accn[:, :, :]))
            V.did(nc.vector.tensor_copy(oh[:, :, :], ohn[:, :, :]))
            V.did(nc.vector.tensor_copy(xnT[:, :], xnTn[:, :]))

        def ending(c, T, V, A):
            nc.vector.wait_ge(out_x, c * 16 + 16)
            n2 = layernorm(nc, V, A, acc, x2, stats, mv, rstd, eps, spare, V.n)
            V.need(nc.sync, n2)
            nc.sync.dma_start(scr["x2"][bass.ds(c * CHUNK, CHUNK), :].rearrange("(t p) d -> p t d", p=P), x2[:, :, :]).then_inc(out_x, 16)
            V.need(nc.tensor, n2)
            A.need(nc.tensor, A.n)
            a = turn(nc, T, A, x2, ps[:, 2, :], xT, ident)
            A.need(nc.tensor, a)

        def after(c, T, V, A):
            at = bass.ds(c * CHUNK, CHUNK)
            V.need(nc.sync, V.n)
            nc.sync.dma_start(jpos[:, :], ins["jpos"][bass.ds(c, 1), :, :].rearrange("a p t -> (a p) t")).then_inc(j_in, 16)
            V.need(nc.tensor, V.n)
            A.need(nc.tensor, A.n)
            for t in range(TILES):
                last = nc.tensor.matmul(ps[:, 7, t * heads:(t + 1) * heads], xT[:, t * P:(t + 1) * P], G[:, :], start=True, stop=True)
            gm = T.did(last)
            T.need(nc.scalar, gm)
            zc = A.did(nc.scalar.activation(z[:, :, :].rearrange("p t h -> p (t h)"), ps[:, 7, 0:TILES * heads], ACT.Copy))
            items = [(t, kind) for t in range(TILES) for kind in range(3)]
            out_at, turned, evac = {}, {}, []

            def multiply(k):
                t, kind = items[k]
                if k >= 2:
                    lane, n = out_at[k - 2]
                    lane.need(nc.tensor, n)
                bank = 3 + k % 2 * 2
                pair = ps[:, bank:bank + 2, :].rearrange("p a n -> p (a n)")
                for m in range(2):
                    last = nc.tensor.matmul(ps[:, bank + m, :], xT[:, t * P:(t + 1) * P], (wq, wk, wv)[kind][:, m * BANK:(m + 1) * BANK],
                                            start=True, stop=True)
                pq = T.did(last)
                T.need(nc.scalar, pq)
                if kind == 2:
                    nc.scalar.wait_ge(out_v, c * 16 * TILES + (t + 1) * 16)
                    vc = A.did(nc.scalar.activation(v[:, :], pair, ACT.Copy))
                    A.need(nc.sync, vc)
                    nc.sync.dma_start(scr["v1"][at, :][t * P:(t + 1) * P, :], v[:, :]).then_inc(out_v, 16)
                    out_at[k] = A, vc
                    return
                if reduced:
                    V.need(nc.scalar, reduced[-1])
                sqd = A.did(nc.scalar.activation(sq[:, 0:HD], pair, ACT.Square))
                A.need(nc.vector, sqd)
                ssn = ss[:, kind * heads:(kind + 1) * heads]
                reduced.append(V.did(nc.vector.tensor_reduce(ssn, sq[:, 0:HD].rearrange("p (h d) -> p h d", d=dim), axis=AX.X, op=ALU.add)))
                V.need(nc.scalar, reduced[-1])
                sr = A.did(nc.scalar.activation(ssn, ssn, ACT.Sqrt, scale=1.0 / dim, bias=eps[:, 0:1]))
                A.need(nc.vector, sr)
                rc = V.did(nc.vector.reciprocal(ssn, ssn))
                if k >= 3:
                    T.need(nc.vector, turned[k - 3])
                V.need(nc.vector, rc)
                to = qk[:, kind, :].rearrange("p (h d) -> p h d", d=dim)
                out_at[k] = V, V.did(nc.vector.tensor_tensor(to, pair.rearrange("p (h d) -> p h d", d=dim),
                                                             ssn.unsqueeze(2).to_broadcast([P, heads, dim]), ALU.mult))
                if kind == 1:
                    A.need(nc.vector, zc)
                    V.need(nc.vector, out_at[k][1])
                    V.did(nc.vector.tensor_tensor(z[:, t, :], z[:, t, :], ssn, ALU.mult))

            def transpose(k, half):
                t, kind = items[k]
                if kind == 2:
                    return
                V.need(nc.tensor, out_at[k][1])
                if evac:
                    V.need(nc.tensor, evac[-1])
                else:
                    A.need(nc.tensor, zc)
                for m in range(4):
                    b = half * 4 + m
                    last = nc.tensor.transpose(ps[:, 7, m * P:(m + 1) * P], qk[:, kind, b * P:(b + 1) * P], ident)
                turned[k] = T.did(last)
                if kind == 0 and half == 0:
                    nc.vector.wait_ge(out_qk, c * 64 * TILES + (t + 1) * 64)
                    nc.scalar.wait_ge(out_qk, c * 64 * TILES + (t + 1) * 64)
                T.need(nc.scalar, turned[k])
                wn = (wqn, wkn)[kind]
                view = ps[:, 7, :].rearrange("p (m i) -> p m i", i=P)
                to = slice(half * 4, half * 4 + 4)
                hi = A.did(nc.scalar.activation(high[:, kind, to, :], view, ACT.Copy, scale=wn[:, 0:1]))
                A.need(nc.vector, hi)
                evac.append(V.did(nc.vector.scalar_tensor_tensor(low[:, kind, to, :], view, wn[:, 0:1],
                                                                 high[:, kind, to, :].bitcast(F32), ALU.mult, ALU.subtract)))
                if kind == 1 and half == 1:
                    V.need(nc.sync, evac[-1])
                    for n, name in enumerate(("q1", "k1")):
                        for part, buf in enumerate((high, low)):
                            nc.sync.dma_start(scr[name][part, :, at][:, t * P:(t + 1) * P].rearrange("(k p) i -> p k i", p=P),
                                              buf[:, n, :, :].bitcast(F32)).then_inc(out_qk, 16)

            reduced = []
            for k in range(len(items) + 1):
                if k < len(items):
                    multiply(k)
                yield
                if k:
                    transpose(k - 1, 0)
                    yield
                    transpose(k - 1, 1)
                    yield
            V.need(nc.vector, V.n)
            z1 = V.did(nc.vector.scalar_tensor_tensor(zabs[:, :, :], z[:, :, :], -1.0, z[:, :, :], ALU.mult, ALU.max))
            V.need(nc.scalar, z1)
            A.did(nc.scalar.activation(zabs[:, :, :], zabs[:, :, :], ACT.Exp, scale=-1.0))
            A.need(nc.scalar, A.n)
            A.did(nc.scalar.activation(zabs[:, :, :], zabs[:, :, :], ACT.Ln, bias=1.0))
            A.need(nc.vector, A.n)
            V.did(nc.vector.scalar_tensor_tensor(g[:, :, :], z[:, :, :], 0.0, zabs[:, :, :], ALU.max, ALU.add))
            V.need(nc.vector, V.n)
            V.did(nc.vector.tensor_tensor(g[:, :, :], g[:, :, :], om[:, :].unsqueeze(1).to_broadcast([P, TILES, heads]), ALU.mult))
            V.need(nc.vector, V.n)
            nc.vector.wait_ge(j_in, c * 16 + 16)
            V.did(nc.vector.tensor_tensor(gj[:, :, :], g[:, :, :], jpos[:, :].unsqueeze(2).to_broadcast([P, TILES, heads]), ALU.mult))
            V.did(nc.vector.tensor_copy(aug[:, :, 0, :], g[:, :, :]))
            V.need(nc.vector, V.n)
            V.did(nc.vector.tensor_copy(aug[:, :, 2, :], gj[:, :, :]))
            V.did(nc.vector.tensor_tensor(aug[:, :, 1, :], g[:, :, :], aug[:, :, 0, :].bitcast(F32), ALU.subtract))
            V.need(nc.vector, V.n)
            ag = V.did(nc.vector.tensor_tensor(aug[:, :, 3, :], gj[:, :, :], aug[:, :, 2, :].bitcast(F32), ALU.subtract))
            yield
            V.need(nc.tensor, ag)
            for t in range(TILES):
                last = nc.tensor.transpose(ps[:, 6, t * P:(t + 1) * P],
                                           aug[:, t, :, :].rearrange("p a h -> p (a h)").bitcast(F32), ident)
            tr = T.did(last)
            T.need(nc.scalar, tr)
            nc.scalar.wait_ge(out_g, c * 16 + 16)
            at_ = A.did(nc.scalar.activation(augT[:, :], ps[0:4 * heads, 6, :], ACT.Copy))
            A.need(nc.sync, at_)
            nc.sync.dma_start(scr["g1"][:, at], augT[:, :]).then_inc(out_g, 16)
            yield

        def step(c, T, V, A, last_post, next_pre):
            if next_pre:
                load(c + 1, T, V, A)
            side = chain(*([after(c - 1, T, V, A)] if last_post else []), *([before(c + 1, T, V, A)] if next_pre else []))
            interleave(moe(T, V, A), side, MOE_YIELDS, (AFTER_YIELDS if last_post else 0) + (BEFORE_YIELDS if next_pre else 0))
            ending(c, T, V, A)
            if next_pre:
                handover(T, V, A)

        MOE_YIELDS, AFTER_YIELDS, BEFORE_YIELDS = 8 * experts, 39, 8
        lanes = lambda tag, t, v, a: (Lane(nc, nc.tensor, f"m{tag}_T", t), Lane(nc, nc.vector, f"m{tag}_V", v), Lane(nc, nc.scalar, f"m{tag}_A", a))
        first = lanes("f", 0, 0, 0)
        load(0, *first)
        for _ in before(0, *first):
            pass
        handover(*first)
        step(0, *first, False, True)
        barrier(nc)
        T, V, A = lanes("l", PER["T"], PER["V"], PER["A"])
        with nc.Fori(1, steps - 1) as it:
            for lane in (T, V, A):
                lane.begin(it - 1)
            for e in (nc.sync, nc.tensor, nc.vector, nc.scalar):
                for lane in (T, V, A):
                    if lane.engine is not e:
                        lane.need(e, 0)
            step(it, T, V, A, True, True)
        settle(T, V, A)
        barrier(nc)
        final_lanes = lanes("e", 0, 0, 0)
        step(steps - 1, *final_lanes, True, False)
        for _ in after(steps - 1, *final_lanes):
            pass
        nc.sync.wait_ge(out_x, 16 * (steps + 1))
        nc.sync.wait_ge(out_g, 16 * (steps + 1))
        nc.sync.wait_ge(out_v, 16 * (steps * TILES + 1))
        nc.sync.wait_ge(out_qk, 64 * (steps * TILES + 1))
        barrier(nc)


def final(nc, ps, const, ins, scr, result, tokens, hidden, kc):
    PER = {"T": 19, "V": 36, "A": 15}
    FC = hidden // P
    with ExitStack() as ctx:
        wp = sbuf(nc, ctx, "fwp", [P, kc, P])
        w1, w2 = sbuf(nc, ctx, "fw1", [P, hidden]), sbuf(nc, ctx, "fw2", [P, hidden])
        h1, h2 = sbuf(nc, ctx, "fh1", [P, FC, hidden]), sbuf(nc, ctx, "fh2", [P, FC, hidden])
        w3, s3 = sbuf(nc, ctx, "fw3", [P, FC, P]), sbuf(nc, ctx, "fs3", [P, P])
        sc = sbuf(nc, ctx, "fsc", [P, 4, FC])
        eps, spare = sbuf(nc, ctx, "feps", [P, 1]), sbuf(nc, ctx, "fspare", [P, 1])
        y, x = sbuf(nc, ctx, "fy", [P, kc, CHUNK]), sbuf(nc, ctx, "fx", [P, TILES, P])
        r, x3n, x3, x3l, res = (sbuf(nc, ctx, f"f{n}", [P, TILES, P]) for n in ("r", "x3n", "x3", "x3l", "res"))
        xT, xTn = sbuf(nc, ctx, "fxT", [P, CHUNK]), sbuf(nc, ctx, "fxTn", [P, CHUNK])
        ha, hb, hc, hd = (sbuf(nc, ctx, f"f{n}", [P, FC, CHUNK]) for n in ("ha", "hb", "hc", "hd"))
        stats, mv, rstd = sbuf(nc, ctx, "fst", [P, TILES, 6]), sbuf(nc, ctx, "fmv", [P, TILES, 2]), sbuf(nc, ctx, "frs", [P, TILES])
        w_in, c_in, out, s0 = (nc.alloc_semaphore(f"f_{n}") for n in ("w_in", "c_in", "out", "s0"))
        weights = [(wp[:, :, :], ins["wproj"]), (w1[:, :], ins["fw1"]), (w2[:, :], ins["fw2"]), (h1[:, :, :], ins["fh1"]),
                   (h2[:, :, :], ins["fh2"]), (w3[:, :, :], ins["fw3"]), (s3[:, :], ins["fs3"].partition_broadcast(P)),
                   (sc[:, :, :], ins["fsc"])]
        for d, s in weights:
            nc.sync.dma_start(d, s).then_inc(w_in, 16)
        nc.vector.memset(eps[:, :], EPS).then_inc(s0, 1)
        nc.scalar.wait_ge(s0, 1)
        for e in (nc.tensor, nc.vector, nc.scalar):
            e.wait_ge(w_in, 16 * len(weights))
        nc.sync.sem_inc(out, 16)
        ident = const["ident"][:, :]
        steps = tokens // CHUNK

        def tiled(view):
            return view.rearrange("p (t d) -> p t d", d=P)

        def load(c, T, V, A):
            at = bass.ds(c * CHUNK, CHUNK)
            for lane in (T, V, A):
                lane.need(nc.sync, lane.n)
            nc.sync.dma_start(y[:, :, :], scr["y1"][:, at].rearrange("(k p) n -> p k n", p=P)).then_inc(c_in, 16)
            nc.sync.dma_start(x[:, :, :], scr["x2"][at, :].rearrange("(t p) d -> p t d", p=P)).then_inc(c_in, 16)

        def before(c, T, V, A):
            V.need(nc.tensor, V.n)
            A.need(nc.tensor, A.n)
            nc.tensor.wait_ge(c_in, c * 32 + 32)
            nc.vector.wait_ge(c_in, c * 32 + 32)
            for t in range(TILES):
                for k in range(kc):
                    last = nc.tensor.matmul(ps[:, 6, t * P:(t + 1) * P], y[:, k, t * P:(t + 1) * P], wp[:, k, :],
                                            start=k == 0, stop=k == kc - 1)
                if t < TILES - 1:
                    yield
            pr = T.did(last)
            T.need(nc.vector, pr)
            V.did(nc.vector.tensor_tensor(r[:, :, :], tiled(ps[:, 6, :]), x[:, :, :], ALU.add))
            n3 = layernorm(nc, V, A, r, x3n, stats, mv, rstd, eps, spare, V.n)
            yield
            yield
            V.need(nc.tensor, n3)
            turn(nc, T, A, x3n, ps[:, 7, :], xTn, ident)
            yield

        def network(T, V, A):
            ring = []

            def bank():
                if len(ring) >= 4:
                    lane, n = ring[-4]
                    lane.need(nc.tensor, n)
                return ps[:, len(ring) % 4, :]

            V.need(nc.tensor, V.n)
            A.need(nc.tensor, A.n)
            for f in range(FC):
                b = bank()
                n = T.did(nc.tensor.matmul(b, w1[:, f * P:(f + 1) * P], xT[:, :], start=True, stop=True))
                T.need(nc.scalar, n)
                m = A.did(nc.scalar.activation(ha[:, f, :], b, ACT.Silu, scale=sc[:, 0, f:f + 1]))
                ring.append((A, m))
                yield
                b = bank()
                n = T.did(nc.tensor.matmul(b, w2[:, f * P:(f + 1) * P], xT[:, :], start=True, stop=True))
                T.need(nc.vector, n)
                A.need(nc.vector, m)
                ring.append((V, V.did(nc.vector.scalar_tensor_tensor(hb[:, f, :], b, sc[:, 1, f:f + 1], ha[:, f, :], ALU.mult, ALU.mult))))
                yield
            for w, src, dst, row in ((h1, hb, hc, 2), (h2, hc, hd, 3)):
                made = ring[-1]
                for o in range(FC):
                    b = bank()
                    for k in range(FC):
                        if o == 0:
                            lane, n = ring[2 * k + 1] if row == 2 else ring[2 * FC + k]
                            lane.need(nc.tensor, n)
                        last = nc.tensor.matmul(b, w[:, k, o * P:(o + 1) * P], src[:, k, :], start=k == 0, stop=k == FC - 1)
                        if k % 2 and k < FC - 1:
                            yield
                    n = T.did(last)
                    T.need(nc.scalar, n)
                    ring.append((A, A.did(nc.scalar.activation(dst[:, o, :], b, ACT.Gelu, scale=sc[:, row, o:o + 1]))))
                    yield

        def handover(T, V, A):
            for lane in (A, T, V):
                lane.need(nc.vector, lane.n)
            V.did(nc.vector.tensor_copy(x3l[:, :, :], x3[:, :, :]))
            V.need(nc.vector, V.n)
            V.did(nc.vector.tensor_copy(x3[:, :, :], x3n[:, :, :]))
            V.did(nc.vector.tensor_copy(xT[:, :], xTn[:, :]))

        def after(c, T, V, A):
            V.need(nc.tensor, V.n)
            A.need(nc.tensor, A.n)
            for t in range(TILES):
                for k in range(FC):
                    last = nc.tensor.matmul(ps[:, 5, t * P:(t + 1) * P], hd[:, k, t * P:(t + 1) * P], w3[:, k, :], start=k == 0, stop=k == FC - 1)
                if t % 2 and t < TILES - 1:
                    yield
            pr = T.did(last)
            yield
            T.need(nc.vector, pr)
            V.need(nc.vector, V.n)
            V.did(nc.vector.tensor_tensor(r[:, :, :], tiled(ps[:, 5, :]), s3[:, :].unsqueeze(1).to_broadcast([P, TILES, P]), ALU.mult))
            V.need(nc.vector, V.n)
            V.did(nc.vector.tensor_tensor(r[:, :, :], r[:, :, :], x3l[:, :, :], ALU.add))
            nc.vector.wait_ge(out, c * 16 + 16)
            n4 = layernorm(nc, V, A, r, res, stats, mv, rstd, eps, spare, V.n)
            V.need(nc.sync, n4)
            nc.sync.dma_start(result[bass.ds(c * CHUNK, CHUNK), :].rearrange("(t p) d -> p t d", p=P), res[:, :, :]).then_inc(out, 16)
            yield

        def step(c, T, V, A, last_post, next_pre):
            if next_pre:
                load(c + 1, T, V, A)
            side = chain(*([after(c - 1, T, V, A)] if last_post else []), *([before(c + 1, T, V, A)] if next_pre else []))
            interleave(network(T, V, A), side, NETWORK_YIELDS, (AFTER_YIELDS if last_post else 0) + (BEFORE_YIELDS if next_pre else 0) + 1)
            handover(T, V, A)

        NETWORK_YIELDS, AFTER_YIELDS, BEFORE_YIELDS = 2 * FC + 4 * FC, 3, 6
        lanes = lambda tag, t, v, a: (Lane(nc, nc.tensor, f"f{tag}_T", t), Lane(nc, nc.vector, f"f{tag}_V", v), Lane(nc, nc.scalar, f"f{tag}_A", a))
        nc.vector.memset(x3[:, :, :], 0.0).then_inc(s0, 1)
        nc.vector.wait_ge(s0, 2)
        first = lanes("f", 0, 0, 0)
        load(0, *first)
        for _ in before(0, *first):
            pass
        handover(*first)
        step(0, *first, False, True)
        barrier(nc)
        T, V, A = lanes("l", PER["T"], PER["V"], PER["A"])
        with nc.Fori(1, steps - 1) as it:
            for lane in (T, V, A):
                lane.begin(it - 1)
            for e in (nc.sync, nc.tensor, nc.vector, nc.scalar):
                for lane in (T, V, A):
                    if lane.engine is not e:
                        lane.need(e, 0)
            step(it, T, V, A, True, True)
        settle(T, V, A)
        barrier(nc)
        final_lanes = lanes("e", 0, 0, 0)
        step(steps - 1, *final_lanes, True, False)
        for _ in after(steps - 1, *final_lanes):
            pass
        nc.sync.wait_ge(out, 16 * (steps + 1))


def build(nc, ins, result, B, S, upto=5):
    tokens = B * S
    H0, H1, DIM1 = 16, 16, 64
    D0 = P // H0
    ps = nc.alloc_psum_tensor("ps", [P, 8, BANK], F32)

    def scratch(name, shape):
        return nc.dram_tensor(name, shape, F32, kind="Internal").ap()

    scr = {"q0": scratch("s_q0", [2, P, tokens]), "k0": scratch("s_k0", [2, P, tokens]), "v0": scratch("s_v0", [tokens, 512]),
           "y0": scratch("s_y0", [512, tokens]), "x2": scratch("s_x2", [tokens, P]), "ku": scratch("s_ku", [H1, DIM1]),
           "q1": scratch("s_q1", [2, H1 * DIM1, tokens]), "k1": scratch("s_k1", [2, H1 * DIM1, tokens]),
           "v1": scratch("s_v1", [tokens, H1 * DIM1]), "g1": scratch("s_g1", [4 * H1, tokens]),
           "y1": scratch("s_y1", [H1 * DIM1, tokens]), "zero": scratch("s_zero", [4 * S])}

    with ExitStack() as ctx:
        const = {n: sbuf(nc, ctx, f"c_{n}", s, d) for n, s, d in (
            ("ident", [P, P], F32), ("identb", [P, P], BF16), ("mask_ji_add", [P, P], BF16), ("mask_ij", [P, BANK], BF16), ("mask_ji", [P, P], F32),
            ("ones", [P, 1], F32), ("zero", [P, BANK], F32), ("pick", [P, 4], F32))}
        c_in, c_set = nc.alloc_semaphore("c_in"), nc.alloc_semaphore("c_set")
        with ExitStack() as tmp:
            mask, mask_add, zero = sbuf(nc, tmp, "c_mask", [P, P]), sbuf(nc, tmp, "c_mask_add", [P, P]), sbuf(nc, tmp, "c_zero0", [1, 4 * S])
            for d, s in ((const["ident"], ins["ident"]), (mask, ins["mask_ij"]), (mask_add, ins["mask_ji_add"]), (const["mask_ji"], ins["mask_ji"]), (const["pick"], ins["pick"])):
                nc.sync.dma_start(d[:, :], s).then_inc(c_in, 16)
            nc.vector.memset(const["mask_ij"][:, :], 0.0).then_inc(c_set, 1)
            nc.vector.memset(const["zero"][:, :], 0.0).then_inc(c_set, 1)
            nc.vector.memset(const["ones"][:, :], 1.0).then_inc(c_set, 1)
            nc.vector.memset(zero[:, :], 0.0).then_inc(c_set, 1)
            nc.vector.wait_ge(c_in, 80)
            nc.vector.tensor_copy(const["identb"][:, :], const["ident"][:, :]).then_inc(c_set, 1)
            nc.vector.tensor_copy(const["mask_ji_add"][:, :], mask_add[:, :]).then_inc(c_set, 1)
            nc.vector.wait_ge(c_set, 1)
            nc.vector.tensor_copy(const["mask_ij"][:, BANK - P:BANK], mask[:, :]).then_inc(c_set, 1)
            nc.sync.wait_ge(c_set, 7)
            nc.sync.dma_start(scr["zero"].rearrange("(a n) -> a n", a=1), zero[:, :]).then_inc(c_in, 16)
            nc.sync.wait_ge(c_in, 96)
            barrier(nc)

        if upto >= 1:
            project0(nc, ps, const, ins, scr, tokens, H0)

        const["zeros"] = scr["zero"].rearrange("(h n) -> h n", n=S)[0:2, :]

        def batch(g, per):
            return g // per, g % per

        def head_rows(src, part, per, heads, dim):
            def of(g):
                b, m = batch(g, per)
                return src[part, bass.ds(m * (heads * dim), heads * dim), bass.ds(b * S, S)].rearrange("(h d) i -> d h i", d=dim)
            return of

        def values_of(src, per):
            def of(g):
                b, m = batch(g, per)
                return src[bass.ds(b * S, S), bass.ds(m * P, P)].rearrange("(t p) n -> p t n", p=P)
            return of

        def out_of(dst, per):
            def of(g, c):
                b, m = batch(g, per)
                return dst[bass.ds(m * P, P), bass.ds(b * S + c * BANK, BANK)]
            return of

        def zeros_for(heads):
            return lambda g: scr["zero"].rearrange("(a h n) -> a h n", a=1, n=S)[:, 0:heads, :]

        if upto >= 2:
            with ExitStack() as pos:
                p_in = nc.alloc_semaphore("a0_p_in")
                const["qpos"], const["kpos"] = sbuf(nc, pos, "c_qpos", [P, S]), sbuf(nc, pos, "c_kpos", [P, S])
                nc.sync.dma_start(const["qpos"][POS:P, :], ins["qpos"]).then_inc(p_in, 16)
                nc.sync.dma_start(const["kpos"][POS:P, :], ins["kpos0"]).then_inc(p_in, 16)
                nc.vector.wait_ge(p_in, 32)
                nc.scalar.wait_ge(p_in, 32)
                per = H0 // 4
                rows = [head_rows(scr["q0"], part, per, 4, D0) for part in range(2)]
                krows = [head_rows(scr["k0"], part, per, 4, D0) for part in range(2)]
                attention(nc, ps, const, "a0",
                          [((0, 8), rows[0]), ((8, 16), rows[0]), ((16, 24), rows[1])], None,
                          [((0, 8), krows[0]), ((8, 16), krows[1]), ((16, 24), krows[0])], None,
                          [(False, (MAXROW, MAXROW + 1), zeros_for(4))], values_of(scr["v0"], per), out_of(scr["y0"], per), B * per, 4, S)

        if upto >= 3:
            middle(nc, ps, const, ins, scr, tokens, 8, 512, H1, DIM1)

        if upto >= 4:
            with ExitStack() as pos:
                p_in = nc.alloc_semaphore("a1_p_in")
                const["qpos"], const["kpos"] = sbuf(nc, pos, "c_qpos1", [P, S]), sbuf(nc, pos, "c_kpos1", [P, S])
                nc.sync.dma_start(const["qpos"][POS:P, :], ins["qpos"]).then_inc(p_in, 16)
                nc.sync.dma_start(const["kpos"][POS:P, :], ins["kpos1"]).then_inc(p_in, 16)
                nc.vector.wait_ge(p_in, 32)
                nc.scalar.wait_ge(p_in, 32)
                per = H1 // 2
                q = [head_rows(scr["q1"], part, per, 2, DIM1) for part in range(2)]
                k = [head_rows(scr["k1"], part, per, 2, DIM1) for part in range(2)]

                def slopes_of(g):
                    b, m = batch(g, per)
                    return scr["g1"].rearrange("(a h) n -> a h n", a=4)[:, bass.ds(m * 2, 2), bass.ds(b * S, S)]

                attention(nc, ps, const, "a1", [((0, 64), q[0])], [((0, 64), q[0]), ((64, 128), q[1])],
                          [((0, 64), k[0])], [((0, 64), k[1]), ((64, 128), k[0])],
                          [(True, (POS, POS + 4), slopes_of), (False, (MAXROW, MAXROW + 1), zeros_for(2))],
                          values_of(scr["v1"], per), out_of(scr["y1"], per), B * per, 2, S)

        if upto >= 5:
            final(nc, ps, const, ins, scr, result, tokens, 512, H1 * DIM1 // P)


def layout(a):
    f = np.float32
    x = a["L0_attn_x"]
    B, S, _ = x.shape
    E, _, F = a["L0_ffn_W1"].shape
    C = np.ascontiguousarray
    o = {"x": x.reshape(B * S, P)}
    o["wq0"], o["wk0"] = C(a["L0_attn_Wq"].T), C(a["L0_attn_Wk"].T)
    o["bq0"], o["bk0"] = a["L0_attn_bq"].reshape(P, 1), a["L0_attn_bk"].reshape(P, 1)
    wv = np.zeros((P, 16, 32), f)
    wv[:, :, 0:8] = a["L0_attn_Wv"].T.reshape(P, 16, 8)
    bv = np.zeros((16, 32), f)
    bv[:, 0:8] = a["L0_attn_bv"].reshape(16, 8)
    bv[:, 8] = 1.0
    o["wv0"], o["bv0"] = wv.reshape(P, 512), bv.reshape(512)
    wo = np.zeros((16, 32, P), f)
    wo[:, 0:8] = a["L0_attn_Wo"].T.reshape(16, 8, P)
    o["wo0"] = C(wo.reshape(4, P, P).transpose(1, 0, 2))
    o["bo0"] = a["L0_attn_bo"]
    o["cent"] = C(a["L0_ffn_centroids"].T)
    o["ln_g"], o["ln_b"] = C(a["L0_ffn_ln_g"].T), C(a["L0_ffn_ln_b"].T)
    o["w1"] = C(a["L0_ffn_W1"].transpose(1, 0, 2))
    o["b1"] = C(a["L0_ffn_b1"].reshape(E, F // P, P).transpose(2, 0, 1))
    o["w2"] = C(a["L0_ffn_W2"].reshape(E, F // P, P, P).transpose(2, 0, 1, 3))
    o["b2"] = a["L0_ffn_b2"]
    o["wq1"], o["wk1"], o["wv1"] = a["L1_attn_Wq"], a["L1_attn_Wk"], a["L1_attn_Wv"]
    o["wproj"] = C(a["L1_attn_Wproj"].reshape(8, P, P).transpose(1, 0, 2))
    o["qn"] = np.concatenate([a["L1_attn_q_rms_w"]] * 2).reshape(P, 1)
    o["kn"] = np.concatenate([a["L1_attn_k_rms_w"]] * 2).reshape(P, 1)
    o["kn_row"], o["u"], o["omega"] = a["L1_attn_k_rms_w"], a["L1_attn_u"], a["L1_attn_omega"]
    o["fw1"], o["fw2"] = C(a["L1_ffn_w1_w"].T), C(a["L1_ffn_w2_w"].T)
    o["fh1"] = C(a["L1_ffn_h1_w"].T.reshape(4, P, 512).transpose(1, 0, 2))
    o["fh2"] = C(a["L1_ffn_h2_w"].T.reshape(4, P, 512).transpose(1, 0, 2))
    o["fw3"] = C(a["L1_ffn_w3_w"].T.reshape(4, P, P).transpose(1, 0, 2))
    o["fs3"] = a["L1_ffn_w3_s"]
    o["fsc"] = C(np.stack([a[f"L1_ffn_{n}_s"].reshape(4, P) for n in ("w1", "w2", "h1", "h2")]).transpose(2, 0, 1))
    o["ident"] = np.eye(P, dtype=f)
    upper = np.triu(np.ones((P, P), f), 1)
    o["mask_ij"] = upper * f(MASKED)
    o["mask_ji_add"] = upper.T * f(MASKED)
    o["mask_ji"] = np.where(upper.T > 0, f(MASKED), -f(LOWEST))
    pos = np.arange(S, dtype=f) - f(S // 2)
    q = np.zeros((P - POS, S), f)
    q[0] = q[1] = -pos
    q[2] = q[3] = 1.0
    k0 = np.zeros((P - POS, S), f)
    k0[0], k0[2], k0[MAXROW - POS] = 1.0, pos, 1.0
    k1 = np.zeros((P - POS, S), f)
    k1[MAXROW - POS] = 1.0
    o["qpos"], o["kpos0"], o["kpos1"] = q, k0, k1
    o["jpos"] = C(np.tile(pos, B).reshape(B * S // CHUNK, TILES, P).transpose(0, 2, 1))
    o["slopes"] = np.array([2.0 ** (-(n + 1) / 2) for n in range(16)], f)
    o["iota"] = np.tile(np.arange(E, dtype=f) - E, (TILES, 1))
    o["pick"] = np.zeros((P, 4), f)
    for n in range(4):
        o["pick"][32 * n + 8, n] = 1.0
    return o, B, S


def kernel(**inputs):
    import concourse.bacc as bacc
    from concourse.bass_utils import run_bass_kernel_spmd

    arrays, B, S = layout({k: np.asarray(v) for k, v in inputs.items()})
    nc = bacc.Bacc("TRN2", target_bir_lowering=False, num_devices=1)
    given, ins = {}, {}
    for name, a in arrays.items():
        given[f"in_{name}"] = np.ascontiguousarray(a)
        ins[name] = nc.dram_tensor(f"in_{name}", a.shape, mybir.dt.from_np(a.dtype), kind="ExternalInput").ap()
    result = nc.dram_tensor("out_0", (B * S, P), F32, kind="ExternalOutput").ap()
    build(nc, ins, result, B, S)
    r = run_bass_kernel_spmd(nc, [given], core_ids=[0])
    return r.results[0]["out_0"].reshape(B, S, P)
```

```python
from contextlib import ExitStack
from itertools import chain

import numpy as np

import concourse.bass as bass
from concourse import mybir
from concourse.alu_op_type import AluOpType as ALU

ACT = mybir.ActivationFunctionType
AX = mybir.AxisListType
F32 = mybir.dt.float32
F32R = mybir.dt.float32r
BF16 = mybir.dt.bfloat16

P = 128
BANK = 512
CHUNK = 512
TILES = CHUNK // P
EPS = 1e-5

POS = 64
MAXROW = 68
MASKED = -1e30
LOWEST = -3e38


class Lane:

    def __init__(self, nc, engine, name, per):
        self.sem, self.engine, self.per, self.base, self.n = nc.alloc_semaphore(name), engine, per, per, 0
        if per:
            engine.sem_inc(self.sem, per)

    def begin(self, it):
        self.base, self.n = it * self.per + self.per, 0

    def did(self, instruction, k=1):
        instruction.then_inc(self.sem, k)
        self.n += k
        return self.n

    def need(self, engine, number):
        if not (isinstance(self.base, int) and self.base + number == 0):
            engine.wait_ge(self.sem, self.base + number)



def settle(*lanes):
    found, said = [x.n for x in lanes], [x.per for x in lanes]
    assert found == said, (found, said)


def interleave(main, side, n_main, n_side):
    given, left = 0.0, 0
    for n, _ in enumerate(main):
        given += n_side / n_main
        while left < given and next(side, "end") != "end":
            left += 1
        if left < given:
            left = given
    for _ in side:
        pass


def barrier(nc):
    nc.all_engine_barrier()


def sbuf(nc, ctx, name, shape, dt=F32):
    return ctx.enter_context(nc.sbuf_tensor(name, shape, dt))


def attention(nc, ps, const, tag, qh, ql, kh, kl, extra, v_of, y_of, groups, heads, seq):
    NB = 4
    W = seq
    IT = seq // P
    HC = seq // BANK
    two = ql is not None and heads == 2
    wide = P // heads
    R = 4 * heads if heads > 2 else 12
    units = [(c, j) for c in range(HC) for j in range((c + 1) * BANK // P)]
    U = len(units) * heads
    assert U % R == 0 and HC == 2 and groups % NB == 0
    RING = 3
    rows = [(t, j0) for t in range(IT) for j0 in range(0, (t + 1) * P, BANK)]
    CH = len(rows) * heads
    assert CH % RING == 0 and U % RING == 0
    n_load = len(qh) + len(kh) + 1 + len(extra) + (len(ql) + len(kl) if two else 0)

    with ExitStack() as ctx:
        QA = [sbuf(nc, ctx, f"{tag}QA{b}", [P, heads, W], F32R) for b in range(NB)]
        KA = [sbuf(nc, ctx, f"{tag}KA{b}", [P, heads, W], F32R) for b in range(NB)]
        QB = [sbuf(nc, ctx, f"{tag}QB{b}", [P, heads, W], F32R) for b in range(NB)] if two else None
        KB = [sbuf(nc, ctx, f"{tag}KB{b}", [P, heads, W], F32R) for b in range(NB)] if two else None
        V = [sbuf(nc, ctx, f"{tag}V{b}", [P, IT, P]) for b in range(NB)]
        prob = sbuf(nc, ctx, f"{tag}prob", [P, R, BANK])
        mx = sbuf(nc, ctx, f"{tag}mx", [P, 2, heads, IT])
        mx2 = sbuf(nc, ctx, f"{tag}mx2", [P, 2, heads, IT // 2])
        negT = sbuf(nc, ctx, f"{tag}negT", [heads * IT, NB, P], F32R)
        spare = sbuf(nc, ctx, f"{tag}spare", [P, RING])
        if two:
            sums = sbuf(nc, ctx, f"{tag}sums", [P, HC, heads, BANK])
        else:
            den = sbuf(nc, ctx, f"{tag}den", [P, BANK])
        rec = sbuf(nc, ctx, f"{tag}rec", [P, TILES * heads])
        recw = sbuf(nc, ctx, f"{tag}recw", [P, TILES * heads, wide])
        recb = sbuf(nc, ctx, f"{tag}recb", [P, BANK])
        oT = sbuf(nc, ctx, f"{tag}oT", [P, HC, BANK])
        S1 = [ps[:, n, :] for n in range(RING)]
        S2 = [ps[:, RING + n, :] for n in range(RING)]
        O = ps[:, 6, :]
        D = ps[:, 7, :]

        ld = [nc.alloc_semaphore(f"{tag}_loaded{b}") for b in range(NB)]
        s1_full = nc.alloc_semaphore(f"{tag}_s1_full")
        s1_free = nc.alloc_semaphore(f"{tag}_s1_free")
        mx_done = nc.alloc_semaphore(f"{tag}_mx_done")
        t_full = nc.alloc_semaphore(f"{tag}_t_full")
        neg_full = nc.alloc_semaphore(f"{tag}_neg_full")
        row_full = [nc.alloc_semaphore(f"{tag}_row_full{b}") for b in range(NB)]
        s2_full = nc.alloc_semaphore(f"{tag}_s2_full")
        p_full = nc.alloc_semaphore(f"{tag}_p_full")
        p_free = nc.alloc_semaphore(f"{tag}_p_free")
        s2_masked = nc.alloc_semaphore(f"{tag}_s2_masked")
        summed = nc.alloc_semaphore(f"{tag}_summed")
        d_copied = nc.alloc_semaphore(f"{tag}_d_copied")
        d_turned = nc.alloc_semaphore(f"{tag}_d_turned")
        r_full = nc.alloc_semaphore(f"{tag}_r_full")
        rb_full = nc.alloc_semaphore(f"{tag}_rb_full")
        rb_copied = nc.alloc_semaphore(f"{tag}_rb_copied")
        o_done = nc.alloc_semaphore(f"{tag}_o_done")
        stored = [nc.alloc_semaphore(f"{tag}_stored{c}") for c in range(HC)]
        setup = [nc.alloc_semaphore(f"{tag}_setup{b}") for b in range(NB)]
        zeroed = [nc.alloc_semaphore(f"{tag}_zeroed{b}") for b in range(NB)]

        nc.vector.sem_inc(s1_free, RING)
        nc.scalar.sem_inc(p_full, RING)
        nc.tensor.sem_inc(p_free, R)
        nc.vector.sem_inc(o_done, 1)
        DA = HC if two else 0
        if two:
            nc.gpsimd.sem_inc(summed, R)
            nc.tensor.sem_inc(d_turned, HC)
        for c in range(HC):
            nc.vector.sem_inc(stored[c], 16)
        def load(g, b, first=True, second=True):
            parts = []
            if first:
                parts += [(QA, r, s) for r, s in qh] + [(KA, r, s) for r, s in kh]
                if two:
                    parts += [(QB, r, s) for r, s in ql] + [(KB, r, s) for r, s in kl]
            if second:
                parts += [(KA if k else QA, r, s) for k, r, s in extra]
            for buf, (r0, r1), src in parts:
                nc.sync.dma_start(buf[b][r0:r1, :, :].bitcast(F32), src(g)).then_inc(ld[b], 16)
            if first:
                nc.sync.dma_start(V[b][:, :, :], v_of(g)).then_inc(ld[b], 16)

        def loaded(engine, r, b):
            engine.wait_ge(ld[b], (r + 1) * 16 * n_load)

        def maxima(g, r, b, h, t, j0):
            k = h * len(rows) + rows.index((t, j0))
            n = g * CH + k
            if k == 0:
                loaded(nc.tensor, r, b)
            if k == RING:
                nc.tensor.wait_ge(neg_full, g + 1)
            nc.tensor.wait_ge(s1_free, n + 1)
            j1 = min((t + 1) * P, j0 + BANK)
            s = S1[k % RING]
            diag = j1 == (t + 1) * P
            nc.tensor.matmul(s[:, 0:j1 - j0], QA[b][:, h, t * P:(t + 1) * P], KA[b][:, h, j0:j1], start=True, stop=True).then_inc(s1_full, 1)
            nc.vector.wait_ge(s1_full, n + 1)
            if diag:
                nc.vector.memset(spare[:, k % RING:k % RING + 1], 0.0)
                nc.vector.tensor_tensor_reduce(s[:, 0:j1 - j0], s[:, 0:j1 - j0], const["mask_ij"][:, BANK - (j1 - j0):BANK],
                                               1.0, LOWEST, ALU.add, ALU.max, mx[:, b % 2, h, t:t + 1]).then_inc(s1_free, 1)
            else:
                to = mx2[:, b % 2, h, t - IT // 2:t - IT // 2 + 1]
                nc.vector.tensor_reduce(to, s[:, 0:j1 - j0], axis=AX.X, op=ALU.max).then_inc(s1_free, 1)

        def turn_maxima(g, b, ahead):
            nc.vector.wait_ge(s1_free, (g + 1) * CH + RING)
            upper = mx[:, b % 2, :, IT // 2:IT]
            nc.vector.tensor_tensor(upper, upper, mx2[:, b % 2, :, :], ALU.max).then_inc(mx_done, 1)
            nc.tensor.wait_ge(mx_done, g + 1)
            if ahead:
                nc.tensor.wait_ge(s1_free, (g + 1) * CH + RING + 1)
            nc.tensor.transpose(S1[0][0:heads * IT, 0:P], mx[:, b % 2, :, :].rearrange("p h t -> p (h t)"), const["ident"][:, :]).then_inc(t_full, 1)
            nc.vector.wait_ge(t_full, g + 1)
            nc.vector.tensor_scalar(negT[:, b, :], S1[0][0:heads * IT, 0:P], -1.0, None, ALU.mult).then_inc(neg_full, 1)
            nc.sync.wait_ge(neg_full, g + 2)
            nc.sync.dma_start(QA[b][MAXROW:MAXROW + 1, :, :].bitcast(F32), negT[:, b, :].bitcast(F32)).then_inc(row_full[b], 16)

        def masks_before(g, u):
            before, all_of_them = (sum(1 for c, j in units[:n] if j * P >= c * BANK) for n in (u, len(units)))
            return (g * all_of_them + before) * heads

        def exponentials(g, r, b, u, h):
            c, j = units[u]
            k = u * heads + h
            n = g * U + k
            if k == 0:
                nc.tensor.wait_ge(row_full[b], (r + 1) * 16)
            off = max(0, j * P - c * BANK)
            i0, i1 = c * BANK + off, (c + 1) * BANK
            s = S2[k % RING][:, off:BANK]
            diag = j * P >= c * BANK
            nc.tensor.wait_ge(p_full, n + 1)
            added = diag and not two
            last = nc.tensor.matmul(s, KA[b][:, h, j * P:(j + 1) * P], QA[b][:, h, i0:i1], start=True, stop=not (two or added))
            if two:
                last = nc.tensor.matmul(s, KB[b][:, h, j * P:(j + 1) * P], QB[b][:, h, i0:i1], start=False, stop=True)
            if added:
                last = nc.tensor.matmul(S2[k % RING][:, off:off + P], const["identb"][:, :], const["mask_ji_add"][:, :],
                                        start=False, stop=True)
            last.then_inc(s2_full, 1)
            if diag and not added:
                nc.vector.wait_ge(s2_full, n + 1)
                tile = s[:, 0:P]
                nc.vector.tensor_tensor(tile, tile, const["mask_ji"][:, :], ALU.min).then_inc(s2_masked, 1)
                nc.scalar.wait_ge(s2_masked, masks_before(g, u) + h + 1)
            else:
                nc.scalar.wait_ge(s2_full, n + 1)
            nc.scalar.wait_ge(p_free, n + 1)
            if two:
                nc.scalar.wait_ge(summed, n + 1)
            nc.scalar.activation(prob[:, k % R, off:BANK], s, ACT.Exp).then_inc(p_full, 1)

        def add_up(g, u, h):
            c, j = units[u]
            k = u * heads + h
            off = max(0, j * P - c * BANK)
            pool, total = nc.gpsimd, sums[:, c, h, :]
            if j == 0:
                if h == 0:
                    pool.wait_ge(d_turned, g * HC + c + 1)
                pool.wait_ge(p_full, g * U + k + 1 + RING)
                pool.tensor_tensor(total, prob[:, k % R, :], const["zero"][:, :], ALU.add).then_inc(summed, 1)
                return
            pool.wait_ge(p_full, g * U + k + 1 + RING)
            pool.wait_ge(summed, g * U + k + R - heads + 1)
            pool.tensor_tensor(total[:, off:BANK], total[:, off:BANK], prob[:, k % R, off:BANK], ALU.add).then_inc(summed, 1)

        def values(g, b, u):
            c, j = units[u]
            off = max(0, j * P - c * BANK)
            first, final = j == 0, u + 1 == len(units) or units[u + 1][0] != c
            if first:
                nc.tensor.wait_ge(o_done, g * HC + c + 1)
            nc.tensor.wait_ge(p_full, g * U + (u + 1) * heads + RING)
            for h in range(heads):
                k = u * heads + h
                last = nc.tensor.matmul(O[h * wide:(h + 1) * wide, off:BANK], V[b][:, j, h * wide:(h + 1) * wide],
                                        prob[:, k % R, off:BANK], start=first, stop=final)
            last.then_inc(p_free, heads)

        def copy_den(g, c):
            if two:
                return
            done = sum(1 for x in units if x[0] <= c) * heads
            nc.scalar.wait_ge(p_free, g * U + done + R)
            nc.scalar.activation(den[:, :], O, ACT.Copy).then_inc(d_copied, 1)

        def turn_den(g, c):
            if two:
                nc.tensor.wait_ge(summed, g * U + sum(1 for x in units if x[0] <= c) * heads + R)
                nc.tensor.wait_ge(o_done, g * HC + c + 1)
                for t in range(TILES):
                    for h in range(heads):
                        n = t * heads + h
                        last = nc.tensor.matmul(D[:, n:n + 1], sums[:, c, h, t * P:(t + 1) * P], const["ones"][:, 0:1], start=True, stop=True)
            else:
                nc.tensor.wait_ge(d_copied, g * HC + c + 1)
                for t in range(TILES):
                    last = nc.tensor.matmul(D[:, t * heads:(t + 1) * heads], den[:, t * P:(t + 1) * P], const["pick"][:, 0:heads],
                                            start=True, stop=True)
            last.then_inc(d_turned, 1)
            nc.vector.wait_ge(d_turned, g * HC + c + 1 + DA)
            nc.vector.reciprocal(rec[:, :], D[:, 0:TILES * heads]).then_inc(r_full, 1)
            nc.vector.wait_ge(r_full, (g * HC + c) * 2 + 1)
            nc.vector.tensor_copy(recw[:, :, :], rec[:, :].unsqueeze(2).to_broadcast([P, TILES * heads, wide])).then_inc(r_full, 1)

        def spread(g, c):
            nc.tensor.wait_ge(r_full, (g * HC + c) * 2 + 2)
            for t in range(TILES):
                lhs = recw[:, t * heads:(t + 1) * heads, :].rearrange("p h w -> p (h w)")
                last = nc.tensor.matmul(D[:, t * P:(t + 1) * P], lhs, const["ident"][:, :], start=True, stop=True)
            last.then_inc(rb_full, 1)
            nc.scalar.wait_ge(rb_full, g * HC + c + 1)
            nc.scalar.activation(recb[:, :], D, ACT.Copy).then_inc(rb_copied, 1)

        def normalise(g, c):
            nc.vector.wait_ge(rb_copied, g * HC + c + 1)
            nc.vector.wait_ge(stored[c], (g + 1) * 16)
            nc.vector.tensor_tensor(oT[:, c, :], O, recb[:, :], ALU.mult).then_inc(o_done, 1)
            nc.sync.wait_ge(o_done, g * HC + c + 2)
            nc.sync.dma_start(y_of(g, c), oT[:, c, :]).then_inc(stored[c], 16)

        class Maxima:

            def __init__(self, g, r, b, there=True, turn=True):
                self.g, self.r, self.b, self.turn, self.there = g, r, b, turn, there
                self.todo = [(h, t, j0) for h in range(heads) for t, j0 in rows] if there else []
                self.total = len(self.todo)

            def give(self, share):
                while self.todo and self.total - len(self.todo) < self.total * share:
                    maxima(self.g, self.r, self.b, *self.todo.pop(0))
                    if self.total - len(self.todo) == RING:
                        self.give_turn()
                if not self.there:
                    self.give_turn()

            def give_turn(self):
                if self.turn:
                    turn_maxima(self.g - 1, (self.b - 1) % NB, self.there)
                    self.turn = False

        def plan(c, n):
            count = blocks[c]
            other = blocks[1 - c]
            before = [("values", True, other - lag + n)] if n < lag else []
            if n == lag - 1:
                before.append(("copy", True, 0))
            if n == lag:
                before.append(("turn", True, 0))
            if n == lag + 1:
                before.append(("divide", True, 0))
            start = min(lag + 2, count - 1)
            if n == start:
                before += [("values", False, x) for x in range(n - lag + 1)]
            elif n > start:
                before.append(("values", False, n - lag))
            return before

        def do(action, g, b, c, x):
            if action == "values":
                values(g, b, x + (blocks[0] if c else 0))
            elif action == "copy":
                copy_den(g, c)
            elif action == "turn":
                turn_den(g, c)
            else:
                spread(g, c)
                normalise(g, c)

        def block(g, r, b, c, before, ahead, share0, share1):
            mine = [u for u, (cu, _) in enumerate(units) if cu == c]
            for n, u in enumerate(mine):
                for h in range(heads):
                    exponentials(g, r, b, u, h)
                    if two:
                        add_up(g, u, h)
                    ahead.give(share0 + (share1 - share0) * (n * heads + h + 1) / (len(mine) * heads))
                for action, of_before, x in plan(c, n):
                    if not of_before:
                        do(action, g, b, c, x)
                    elif before:
                        do(action, *before, x)

        blocks = [sum(1 for cu, _ in units if cu == c) for c in range(HC)]
        lag = 2 if two else 1

        def step(g, r, b, r1, r2, more, most):
            b1, b2 = (b + 1) % NB, (b + 2) % NB
            ahead = Maxima(g + 2, r2, b2, most, more)
            block(g, r, b, 1, (g, b, 0), ahead, 0, 2 / 3 if more else 1)
            if more:
                block(g + 1, r1, b1, 0, (g, b, 1), ahead, 2 / 3, 1)

        def load_when_free(g, b):
            nc.sync.wait_ge(p_free, (g - NB + 1) * U + R)
            load(g, b)

        for b in range(NB):
            n = n_zero = 0
            load(b, b, second=False)
            for buf, pos, engine, copy in ((QA, const["qpos"], nc.vector, nc.vector.tensor_copy), (KA, const["kpos"], nc.gpsimd, nc.scalar.copy)):
                for h in range(heads):
                    copy(buf[b][POS:P, h, :], pos[POS:P, :]).then_inc(setup[b], 1)
                    n += 1
                if not two:
                    engine.memset(buf[b][32:POS, :, :].bitcast(F32), 0.0).then_inc(setup[b], 1)
                    n += 1
                    for h in range(0, heads, 2):
                        nc.scalar.dma_start(buf[b][24:32, h:h + 2, :].bitcast(F32), const["zeros"].partition_broadcast(8)).then_inc(zeroed[b], 16)
                        n_zero += 16
            nc.sync.wait_ge(setup[b], n)
            if n_zero:
                nc.sync.wait_ge(zeroed[b], n_zero)
            load(b, b, first=False)
        nc.vector.sem_inc(neg_full, 1)
        Maxima(0, 0, 0, turn=False).give(1)
        ahead = Maxima(1, 0, 1)
        ahead.give(RING / CH)
        block(0, 0, 0, 0, None, ahead, RING / CH, 1)
        body = groups // NB
        with nc.Fori(0, body - 1) as it:
            nc.disable_value_cache = True
            for b in range(NB):
                g = it * NB + b
                step(g, it, b, it + (b + 1) // NB, it + (b + 2) // NB, True, True)
                load_when_free(g + NB, b)
        for b in range(NB):
            step((body - 1) * NB + b, body - 1, b, body - 1, body - 1, b < 3, b < 2)
        for n in range(lag + 2):
            for action, of_before, x in plan(0, n):
                if of_before:
                    do(action, groups - 1, NB - 1, 1, x)
        for c in range(HC):
            nc.sync.wait_ge(stored[c], 16 * (groups + 1))
        barrier(nc)


def layernorm(nc, V, A, x, out, stats, mv, rstd, eps, spare, after):
    V.need(nc.vector, after)
    for t in range(TILES):
        V.did(nc.vector.bn_stats(stats[:, t, :], x[:, t, :]))
    V.need(nc.vector, V.n)
    nc.vector.memset(spare[:, 0:1], 0.0)
    for t in range(TILES):
        V.did(nc.vector.bn_aggr(mv[:, t, :], stats[:, t, :]))
    varied = V.n
    yield
    V.need(nc.scalar, varied)
    root = A.did(nc.scalar.activation(rstd[:, :], mv[:, :, 1], ACT.Sqrt, bias=eps[:, 0:1]))
    yield
    A.need(nc.vector, root)
    V.did(nc.vector.reciprocal(rstd[:, :], rstd[:, :]))
    V.need(nc.vector, V.n)
    for t in range(TILES):
        V.did(nc.vector.tensor_scalar(out[:, t, :], x[:, t, :], mv[:, t, 0:1], rstd[:, t:t + 1],
                                      ALU.subtract, ALU.mult))
    return V.n


def at_once(steps):
    while True:
        try:
            next(steps)
        except StopIteration as end:
            return end.value


def turn(nc, T, A, src, bank, dst, ident):
    for t in range(TILES):
        last = nc.tensor.transpose(bank[:, t * P:(t + 1) * P], src[:, t, :], ident)
    n = T.did(last)
    T.need(nc.scalar, n)
    return A.did(nc.scalar.activation(dst[:, :], bank, ACT.Copy))


def project0(nc, ps, const, ins, scr, tokens, heads):
    scale = float(1.0 / np.sqrt(np.float32(P // heads)))
    chunks = tokens // CHUNK
    STORES = 5
    with ExitStack() as ctx:
        wq, wk = sbuf(nc, ctx, "p0wq", [P, P]), sbuf(nc, ctx, "p0wk", [P, P])
        wv, bv = sbuf(nc, ctx, "p0wv", [P, BANK]), sbuf(nc, ctx, "p0bv", [P, BANK])
        bq, bk = sbuf(nc, ctx, "p0bq", [P, 1]), sbuf(nc, ctx, "p0bk", [P, 1])
        x = sbuf(nc, ctx, "p0x", [P, 2, TILES, P])
        xT = sbuf(nc, ctx, "p0xT", [P, 2, CHUNK])
        full = sbuf(nc, ctx, "p0full", [P, 2, 2, CHUNK])
        high = sbuf(nc, ctx, "p0high", [P, 2, 2, CHUNK], F32R)
        low = sbuf(nc, ctx, "p0low", [P, 2, 2, CHUNK], F32R)
        v = sbuf(nc, ctx, "p0v", [P, 2, TILES, BANK])
        sem = lambda n: nc.alloc_semaphore(f"p0_{n}")
        w_in, x_in, stored = sem("w_in"), [sem("x_in0"), sem("x_in1")], [sem("stored0"), sem("stored1")]
        turned = sem("turned")
        xT_full = sem("xT_full")
        product = sem("product")
        qk_full = sem("qk_full")
        high_full = sem("high_full")
        v_full = sem("v_full")
        low_full = sem("low_full")
        scaled = sem("scaled")
        for engine, s, n in ((nc.tensor, turned, 2), (nc.scalar, xT_full, 2), (nc.tensor, product, 12), (nc.scalar, qk_full, 2),
                             (nc.vector, v_full, 4), (nc.vector, low_full, 4), (nc.sync, stored[0], 16 * STORES),
                             (nc.sync, stored[1], 16 * STORES)):
            engine.sem_inc(s, n)

        def load(c, r, p):
            nc.sync.wait_ge(turned, c + 1)
            nc.sync.dma_start(x[:, p, :, :], ins["x"][bass.ds(c * CHUNK, CHUNK), :].rearrange("(t p) d -> p t d", p=P)).then_inc(x_in[p], 16)

        def transpose(c, r, p):
            nc.tensor.wait_ge(x_in[p], r * 16 + 16)
            nc.tensor.wait_ge(xT_full, c + 1)
            for t in range(TILES):
                last = nc.tensor.transpose(ps[:, p, t * P:(t + 1) * P], x[:, p, t, :], const["ident"][:, :])
            last.then_inc(turned, 1)
            nc.scalar.wait_ge(turned, c + 3)
            nc.scalar.wait_ge(product, c * 6 + 6)
            nc.scalar.activation(xT[:, p, :], ps[:, p, :], ACT.Copy).then_inc(xT_full, 1)

        def project(c, r, p):
            nc.tensor.wait_ge(xT_full, c + 3)
            for n, w in enumerate((wq, wk)):
                nc.tensor.wait_ge(qk_full, c * 2 + n + 1)
                nc.tensor.matmul(ps[:, 2 + n, :], w[:, :], xT[:, p, :], start=True, stop=True).then_inc(product, 1)
            for t in range(TILES):
                nc.tensor.wait_ge(v_full, c * 4 + t + 1)
                nc.tensor.matmul(ps[:, 4 + t, :], xT[:, p, t * P:(t + 1) * P], wv[:, :], start=True, stop=True).then_inc(product, 1)
            nc.scalar.wait_ge(stored[p], (r + 1) * 16 * STORES)
            nc.scalar.wait_ge(low_full, c * 2 + 2)
            for n, (bias, factor) in enumerate(((bq, scale), (bk, 1.0))):
                nc.scalar.wait_ge(product, c * 6 + n + 13)
                nc.scalar.activation(full[:, p, n, :], ps[:, 2 + n, :], ACT.Identity, bias=bias[:, 0:1], scale=factor).then_inc(qk_full, 1)
            for n in range(2):
                nc.scalar.wait_ge(qk_full, c * 2 + n + 3)
                nc.scalar.activation(high[:, p, n, :], full[:, p, n, :], ACT.Copy).then_inc(high_full, 1)
            nc.vector.wait_ge(stored[p], (r + 1) * 16 * STORES)
            for t in range(TILES):
                nc.vector.wait_ge(product, c * 6 + t + 15)
                nc.vector.tensor_tensor(v[:, p, t, :], ps[:, 4 + t, :], bv[:, :], ALU.add).then_inc(v_full, 1)
            for n in range(2):
                nc.vector.wait_ge(high_full, c * 2 + n + 1)
                nc.vector.tensor_tensor(low[:, p, n, :], full[:, p, n, :], high[:, p, n, :].bitcast(F32), ALU.subtract).then_inc(low_full, 1)

        def store(c, r, p):
            at = bass.ds(c * CHUNK, CHUNK)
            nc.sync.wait_ge(v_full, c * 4 + 8)
            nc.sync.wait_ge(low_full, c * 2 + 6)
            nc.sync.dma_start(scr["v0"][at, :].rearrange("(t p) n -> p t n", p=P), v[:, p, :, :]).then_inc(stored[p], 16)
            for n, name in enumerate(("q0", "k0")):
                nc.sync.dma_start(scr[name][0, :, at], high[:, p, n, :].bitcast(F32)).then_inc(stored[p], 16)
                nc.sync.dma_start(scr[name][1, :, at], low[:, p, n, :].bitcast(F32)).then_inc(stored[p], 16)

        load(0, 0, 0)
        load(1, 0, 1)
        for d, s in ((wq, ins["wq0"]), (wk, ins["wk0"]), (wv, ins["wv0"]), (bq, ins["bq0"]), (bk, ins["bk0"]),
                     (bv, ins["bv0"].partition_broadcast(P))):
            nc.sync.dma_start(d[:, :], s).then_inc(w_in, 16)
        transpose(0, 0, 0)
        nc.tensor.wait_ge(w_in, 96)
        nc.vector.wait_ge(w_in, 96)
        nc.vector.tensor_scalar(bq[:, :], bq[:, :], scale, None, ALU.mult).then_inc(scaled, 1)
        nc.scalar.wait_ge(scaled, 1)

        def pair(i, more):
            for p in range(2):
                c = i * 2 + p
                if p == 0 or more:
                    transpose(c + 1, i + p, 1 - p)
                if more:
                    load(c + 2, i + 1, p)
                project(c, i, p)
                store(c, i, p)

        with nc.Fori(0, chunks // 2 - 1) as it:
            pair(it, True)
        pair(chunks // 2 - 1, False)
        for p in range(2):
            nc.sync.wait_ge(stored[p], 16 * STORES * (chunks // 2 + 1))
        barrier(nc)


def middle(nc, ps, const, ins, scr, tokens, experts, hidden, heads, dim):
    PER = {"T": 77, "V": 143, "A": 79}
    KC = 4
    FC = hidden // P
    HD = heads * dim
    PAIRS = HD // P
    with ExitStack() as ctx:
        wo = sbuf(nc, ctx, "mwo", [P, KC, P])
        bo = sbuf(nc, ctx, "mbo", [P, P])
        cent = sbuf(nc, ctx, "mcent", [P, experts])
        gT, bT = sbuf(nc, ctx, "mg", [P, experts]), sbuf(nc, ctx, "mb", [P, experts])
        w1 = sbuf(nc, ctx, "mw1", [P, experts, hidden])
        b1 = sbuf(nc, ctx, "mb1", [P, experts, FC])
        w2 = sbuf(nc, ctx, "mw2", [P, experts, FC, P])
        b2 = sbuf(nc, ctx, "mb2", [experts, P])
        wq, wk, wv = (sbuf(nc, ctx, f"m{n}", [P, HD]) for n in ("wq", "wk", "wv"))
        wqn, wkn = sbuf(nc, ctx, "mwqn", [P, 1]), sbuf(nc, ctx, "mwkn", [P, 1])
        u, kw = sbuf(nc, ctx, "mu", [heads, dim]), sbuf(nc, ctx, "mkw", [heads, dim])
        usq, us = sbuf(nc, ctx, "musq", [heads, dim]), sbuf(nc, ctx, "mus", [heads, 1])
        G = sbuf(nc, ctx, "mG", [P, heads])
        om, om1, slopes = (sbuf(nc, ctx, f"m{n}", [P, heads]) for n in ("om", "om1", "slopes"))
        iota = sbuf(nc, ctx, "miota", [P, TILES, experts])
        eps, spare = sbuf(nc, ctx, "meps", [P, 1]), sbuf(nc, ctx, "mspare", [P, 1])

        y, x = sbuf(nc, ctx, "my", [P, KC, CHUNK]), sbuf(nc, ctx, "mx0", [P, TILES, P])
        jpos = sbuf(nc, ctx, "mjpos", [P, TILES])
        r1 = sbuf(nc, ctx, "mr1", [P, TILES, P])
        x1n, xn, accn, acc, accl, x2 = (sbuf(nc, ctx, f"m{n}", [P, TILES, P]) for n in ("x1", "xn", "accn", "acc", "accl", "x2"))
        xT, x1T, xnTn, xnT = (sbuf(nc, ctx, f"m{n}", [P, CHUNK]) for n in ("xT", "x1T", "xnTn", "xnT"))
        xe = sbuf(nc, ctx, "mxe", [P, 2, CHUNK])
        stats, mv, rstd = sbuf(nc, ctx, "mst", [P, TILES, 6]), sbuf(nc, ctx, "mmv", [P, TILES, 2]), sbuf(nc, ctx, "mrs", [P, TILES])
        top = sbuf(nc, ctx, "mtop", [P, TILES])
        eq, oh, ohn = (sbuf(nc, ctx, f"m{n}", [P, TILES, experts]) for n in ("eq", "oh", "ohn"))
        ohT = sbuf(nc, ctx, "mohT", [experts, CHUNK])
        h = sbuf(nc, ctx, "mh", [P, 2, FC, CHUNK])
        sq = sbuf(nc, ctx, "msq", [P, HD])
        ss = sbuf(nc, ctx, "mss", [P, 2 * heads])
        qk = sbuf(nc, ctx, "mqk", [P, 2, HD])
        v = sbuf(nc, ctx, "mval", [P, HD])
        high, low = sbuf(nc, ctx, "mhi", [P, 2, PAIRS, P], F32R), sbuf(nc, ctx, "mlo", [P, 2, PAIRS, P], F32R)
        z, zabs, g, gj = (sbuf(nc, ctx, f"m{n}", [P, TILES, heads]) for n in ("z", "zabs", "slope", "gj"))
        aug = sbuf(nc, ctx, "maug", [P, TILES, P // heads, heads], F32R)
        augT = sbuf(nc, ctx, "maugT", [4 * heads, CHUNK])

        sem = lambda n: nc.alloc_semaphore(f"m_{n}")
        w_first, w_expert, w_rest, c_in, j_in = sem("w_first"), sem("w_expert"), sem("w_rest"), sem("c_in"), sem("j_in")
        out_x, out_g, out_v, out_qk = sem("out_x"), sem("out_g"), sem("out_v"), sem("out_qk")
        s0, s1 = sem("setup_v"), sem("setup_a")
        first_weights = [(wo[:, :, :], ins["wo0"]), (bo[:, :], ins["bo0"].partition_broadcast(P)), (cent[:, :], ins["cent"]),
                         (b2[:, :], ins["b2"]), (iota[:, :, :], ins["iota"].partition_broadcast(P))]
        expert_weights = [(gT[:, :], ins["ln_g"]), (bT[:, :], ins["ln_b"]), (w1[:, :, :], ins["w1"]), (b1[:, :, :], ins["b1"]),
                          (w2[:, :, :, :], ins["w2"])]
        other_weights = [(u[:, :], ins["u"]), (kw[:, :], ins["kn_row"].partition_broadcast(heads)), (wk[:, :], ins["wk1"]),
                         (om[:, :], ins["omega"].partition_broadcast(P)), (slopes[:, :], ins["slopes"].partition_broadcast(P)),
                         (wqn[:, :], ins["qn"]), (wkn[:, :], ins["kn"]), (wq[:, :], ins["wq1"]), (wv[:, :], ins["wv1"])]
        n_rest = 16 * len(other_weights)

        def fetch(weights, semaphore):
            for d, s in weights:
                nc.sync.dma_start(d, s).then_inc(semaphore, 16)

        dv = [0]

        def dve(ins_):
            dv[0] += 1
            ins_.then_inc(s0, 1)
            nc.vector.wait_ge(s0, dv[0])

        def prepare():
            nc.vector.wait_ge(w_rest, n_rest)
            nc.scalar.wait_ge(w_rest, n_rest)
            dve(nc.vector.memset(aug[:, :, :, :].bitcast(F32), 0.0))
            dve(nc.vector.tensor_scalar(wqn[:, :], wqn[:, :], float(1.0 / np.sqrt(dim)), None, ALU.mult))
            dve(nc.vector.tensor_tensor(usq[:, :], u[:, :], u[:, :], ALU.mult))
            dve(nc.vector.tensor_reduce(us[:, :], usq[:, :], axis=AX.X, op=ALU.add))
            yield
            nc.scalar.wait_ge(s0, dv[0])
            nc.scalar.activation(us[:, :], us[:, :], ACT.Sqrt).then_inc(s1, 1)
            yield
            nc.vector.wait_ge(s1, 1)
            dve(nc.vector.tensor_scalar(us[:, :], us[:, :], 1e-6, None, ALU.max))
            dve(nc.vector.reciprocal(us[:, :], us[:, :]))
            dve(nc.vector.scalar_tensor_tensor(usq[:, :], u[:, :], us[:, 0:1], kw[:, :], ALU.mult, ALU.mult))
            yield
            nc.sync.wait_ge(s0, dv[0])
            nc.sync.dma_start(scr["ku"], usq[:, :]).then_inc(w_rest, 16)
            nc.sync.wait_ge(w_rest, n_rest + 16)
            nc.sync.dma_start(sq[:, 0:HD], scr["ku"].rearrange("h d -> (h d)").partition_broadcast(P)).then_inc(w_rest, 16)
            yield
            yield
            nc.vector.wait_ge(w_rest, n_rest + 32)
            dve(nc.vector.tensor_tensor(sq[:, 0:HD], sq[:, 0:HD], wk[:, :], ALU.mult))
            dve(nc.vector.tensor_reduce(G[:, :], sq[:, 0:HD].rearrange("p (h d) -> p h d", d=dim), axis=AX.X, op=ALU.add))
            dve(nc.vector.tensor_scalar(G[:, :], G[:, :], float(1.0 / np.sqrt(dim)), None, ALU.mult))
            dve(nc.vector.scalar_tensor_tensor(om1[:, :], om[:, :], -1.0, om[:, :], ALU.mult, ALU.max))
            nc.scalar.wait_ge(s0, dv[0])
            nc.scalar.activation(om1[:, :], om1[:, :], ACT.Exp, scale=-1.0).then_inc(s1, 1)
            yield
            nc.scalar.wait_ge(s1, 2)
            nc.scalar.activation(om1[:, :], om1[:, :], ACT.Ln, bias=1.0).then_inc(s1, 1)
            yield
            nc.vector.wait_ge(s1, 3)
            dve(nc.vector.scalar_tensor_tensor(om[:, :], om[:, :], 0.0, om1[:, :], ALU.max, ALU.add))
            dve(nc.vector.tensor_tensor(om[:, :], om[:, :], slopes[:, :], ALU.mult))

        ident = const["ident"][:, :]
        steps = tokens // CHUNK
        nc.sync.sem_inc(out_x, 16)
        nc.sync.sem_inc(out_g, 16)
        nc.sync.sem_inc(out_v, 16)
        nc.sync.sem_inc(out_qk, 64)

        def tiled(view):
            return view.rearrange("p (t d) -> p t d", d=P)

        def load(c, T, V, A):
            at = bass.ds(c * CHUNK, CHUNK)
            for lane in (T, V, A):
                lane.need(nc.sync, lane.n)
            nc.sync.dma_start(y[:, :, :], scr["y0"][:, at].rearrange("(k p) n -> p k n", p=P)).then_inc(c_in, 16)
            nc.sync.dma_start(x[:, :, :], ins["x"][at, :].rearrange("(t p) d -> p t d", p=P)).then_inc(c_in, 16)

        def before(c, T, V, A):
            V.need(nc.tensor, V.n)
            A.need(nc.tensor, A.n)
            nc.tensor.wait_ge(c_in, c * 32 + 32)
            nc.vector.wait_ge(c_in, c * 32 + 32)
            for t in range(TILES):
                for k in range(KC):
                    last = nc.tensor.matmul(ps[:, 4, t * P:(t + 1) * P], y[:, k, t * P:(t + 1) * P], wo[:, k, :],
                                            start=k == 0, stop=k == KC - 1)
                if t < TILES - 1:
                    yield
            pr = T.did(last)
            T.need(nc.vector, pr)
            V.did(nc.vector.tensor_tensor(r1[:, :, :], tiled(ps[:, 4, :]), x[:, :, :], ALU.add))
            V.need(nc.vector, V.n)
            V.did(nc.vector.tensor_tensor(r1[:, :, :], r1[:, :, :], bo[:, :].unsqueeze(1).to_broadcast([P, TILES, P]), ALU.add))
            n1 = yield from layernorm(nc, V, A, r1, x1n, stats, mv, rstd, eps, spare, V.n)
            yield
            V.need(nc.tensor, n1)
            a = turn(nc, T, A, x1n, ps[:, 5, :], x1T, ident)
            n = yield from layernorm(nc, V, A, x1n, xn, stats, mv, rstd, eps, spare, n1)
            yield
            A.need(nc.tensor, a)
            for t in range(TILES):
                last = nc.tensor.matmul(ps[:, 6, t * experts:(t + 1) * experts], x1T[:, t * P:(t + 1) * P], cent[:, :],
                                        start=True, stop=True)
            lg = T.did(last)
            V.need(nc.tensor, n)
            turn(nc, T, A, xn, ps[:, 7, :], xnTn, ident)
            T.need(nc.vector, lg)
            logits = ps[:, 6, 0:TILES * experts].rearrange("p (t e) -> p t e", e=experts)
            per_tile = [P, TILES, experts]
            V.did(nc.vector.tensor_reduce(top[:, :], logits, axis=AX.X, op=ALU.max))
            V.need(nc.vector, V.n)
            V.did(nc.vector.tensor_tensor(eq[:, :, :], logits, top[:, :].unsqueeze(2).to_broadcast(per_tile), ALU.is_equal))
            V.need(nc.vector, V.n)
            V.did(nc.vector.tensor_tensor(eq[:, :, :], eq[:, :, :], iota[:, :, :], ALU.mult))
            V.need(nc.vector, V.n)
            V.did(nc.vector.tensor_reduce(top[:, :], eq[:, :, :], axis=AX.X, op=ALU.min))
            V.need(nc.vector, V.n)
            o = V.did(nc.vector.tensor_tensor(ohn[:, :, :], iota[:, :, :], top[:, :].unsqueeze(2).to_broadcast(per_tile), ALU.is_equal))
            yield
            V.need(nc.tensor, o)
            for t in range(TILES):
                last = nc.tensor.transpose(ps[0:experts, 4, t * P:(t + 1) * P], ohn[:, t, :], ident)
            T.did(last)
            T.need(nc.scalar, T.n)
            oa = A.did(nc.scalar.activation(ohT[:, :], ps[0:experts, 4, :], ACT.Copy))
            yield
            A.need(nc.tensor, oa)
            for t in range(TILES):
                last = nc.tensor.matmul(ps[:, 5, t * P:(t + 1) * P], ohT[:, t * P:(t + 1) * P], b2[:, :], start=True, stop=True)
            T.did(last)
            T.need(nc.vector, T.n)
            V.did(nc.vector.scalar_tensor_tensor(accn[:, :, :], x1n[:, :, :], 2.0, tiled(ps[:, 5, :]), ALU.mult, ALU.add))
            yield

        def moe(T, V, A):
            xe_at, up_at, h_at, h_read, y_at = {}, {}, {}, {}, {}
            ring, acc_at = [], V.n

            def scaled(e):
                if e >= 2:
                    T.need(nc.vector, up_at[e - 2])
                xe_at[e] = V.did(nc.vector.tensor_scalar(xe[:, e % 2, :], xnT[:, :], gT[:, e:e + 1], bT[:, e:e + 1], ALU.mult, ALU.add))

            V.need(nc.vector, V.n)
            scaled(0)
            for e in range(experts + 1):
                if e < experts:
                    if e + 1 < experts:
                        scaled(e + 1)
                    V.need(nc.tensor, xe_at[e])
                    for f in range(FC):
                        if len(ring) >= 2:
                            A.need(nc.tensor, ring[-2])
                        m = T.did(nc.tensor.matmul(ps[:, len(ring) % 2, :], w1[:, e, f * P:(f + 1) * P], xe[:, e % 2, :], start=True, stop=True))
                        T.need(nc.scalar, m)
                        if f == 0 and e >= 2:
                            T.need(nc.scalar, y_at[e - 2])
                        ring.append(A.did(nc.scalar.activation(h[:, e % 2, f, :], ps[:, len(ring) % 2, :], ACT.Relu, bias=b1[:, e, f:f + 1])))
                        yield
                    up_at[e], h_at[e] = m, ring[-1]
                if e:
                    d = e - 1
                    A.need(nc.tensor, h_at[d])
                    V.need(nc.tensor, acc_at)
                    for t in range(TILES):
                        for f in range(FC):
                            last = nc.tensor.matmul(ps[:, 2, t * P:(t + 1) * P], h[:, d % 2, f, t * P:(t + 1) * P], w2[:, d, f, :],
                                                    start=f == 0, stop=f == FC - 1)
                        if t < TILES - 1:
                            yield
                    y_at[d] = T.did(last)
                    T.need(nc.vector, y_at[d])
                    V.need(nc.vector, acc_at)
                    for t in range(TILES):
                        acc_at = V.did(nc.vector.scalar_tensor_tensor(acc[:, t, :], ps[:, 2, t * P:(t + 1) * P], oh[:, t, d:d + 1],
                                                                      acc[:, t, :], ALU.mult, ALU.add))
                    yield

        def handover(T, V, A):
            A.need(nc.vector, A.n)
            T.need(nc.vector, T.n)
            V.need(nc.vector, V.n)
            V.did(nc.vector.tensor_copy(accl[:, :, :], acc[:, :, :]))
            V.need(nc.vector, V.n)
            V.did(nc.vector.tensor_copy(acc[:, :, :], accn[:, :, :]))
            V.did(nc.vector.tensor_copy(oh[:, :, :], ohn[:, :, :]))
            V.did(nc.vector.tensor_copy(xnT[:, :], xnTn[:, :]))

        def ending(c, T, V, A):
            nc.vector.wait_ge(out_x, c * 16 + 16)
            n2 = yield from layernorm(nc, V, A, accl, x2, stats, mv, rstd, eps, spare, V.n)
            V.need(nc.sync, n2)
            nc.sync.dma_start(scr["x2"][bass.ds(c * CHUNK, CHUNK), :].rearrange("(t p) d -> p t d", p=P), x2[:, :, :]).then_inc(out_x, 16)
            V.need(nc.tensor, n2)
            A.need(nc.tensor, A.n)
            yield
            turn(nc, T, A, x2, ps[:, 7, :], xT, ident)
            yield

        def after(c, T, V, A):
            at = bass.ds(c * CHUNK, CHUNK)
            V.need(nc.sync, V.n)
            nc.sync.dma_start(jpos[:, :], ins["jpos"][bass.ds(c, 1), :, :].rearrange("a p t -> (a p) t")).then_inc(j_in, 16)
            V.need(nc.tensor, V.n)
            A.need(nc.tensor, A.n)
            for t in range(TILES):
                last = nc.tensor.matmul(ps[:, 7, t * heads:(t + 1) * heads], xT[:, t * P:(t + 1) * P], G[:, :], start=True, stop=True)
            gm = T.did(last)
            T.need(nc.scalar, gm)
            zc = A.did(nc.scalar.activation(z[:, :, :].rearrange("p t h -> p (t h)"), ps[:, 7, 0:TILES * heads], ACT.Copy))
            items = [(t, kind) for t in range(TILES) for kind in range(3)]
            out_at, turned, squared, rooted, evac = {}, {}, {}, {}, []

            def multiply(k):
                t, kind = items[k]
                if k >= 2:
                    lane, n = out_at[k - 2]
                    lane.need(nc.tensor, n)
                bank = 3 + k % 2 * 2
                pair = ps[:, bank:bank + 2, :].rearrange("p a n -> p (a n)")
                for m in range(2):
                    last = nc.tensor.matmul(ps[:, bank + m, :], xT[:, t * P:(t + 1) * P], (wq, wk, wv)[kind][:, m * BANK:(m + 1) * BANK],
                                            start=True, stop=True)
                pq = T.did(last)
                T.need(nc.scalar, pq)
                if kind == 2:
                    nc.scalar.wait_ge(out_v, c * 16 * TILES + (t + 1) * 16)
                    vc = A.did(nc.scalar.activation(v[:, :], pair, ACT.Copy))
                    A.need(nc.sync, vc)
                    nc.sync.dma_start(scr["v1"][at, :][t * P:(t + 1) * P, :], v[:, :]).then_inc(out_v, 16)
                    out_at[k] = A, vc
                    return
                if reduced:
                    V.need(nc.scalar, reduced[-1])
                squared[k] = A.did(nc.scalar.activation(sq[:, 0:HD], pair, ACT.Square))

            def reduce(k):
                t, kind = items[k]
                A.need(nc.vector, squared[k])
                ssn = ss[:, kind * heads:(kind + 1) * heads]
                reduced.append(V.did(nc.vector.tensor_reduce(ssn, sq[:, 0:HD].rearrange("p (h d) -> p h d", d=dim), axis=AX.X, op=ALU.add)))

            def root(k):
                ssn = ss[:, items[k][1] * heads:(items[k][1] + 1) * heads]
                V.need(nc.scalar, reduced[-1])
                rooted[k] = A.did(nc.scalar.activation(ssn, ssn, ACT.Sqrt, scale=1.0 / dim, bias=eps[:, 0:1]))

            def scale(k):
                t, kind = items[k]
                pair = ps[:, 3 + k % 2 * 2:5 + k % 2 * 2, :].rearrange("p a n -> p (a n)")
                ssn = ss[:, kind * heads:(kind + 1) * heads]
                A.need(nc.vector, rooted[k])
                rc = V.did(nc.vector.reciprocal(ssn, ssn))
                if k >= 3:
                    T.need(nc.vector, turned[k - 3])
                V.need(nc.vector, rc)
                to = qk[:, kind, :].rearrange("p (h d) -> p h d", d=dim)
                out_at[k] = V, V.did(nc.vector.tensor_tensor(to, pair.rearrange("p (h d) -> p h d", d=dim),
                                                             ssn.unsqueeze(2).to_broadcast([P, heads, dim]), ALU.mult))
                if kind == 1:
                    A.need(nc.vector, zc)
                    V.need(nc.vector, out_at[k][1])
                    V.did(nc.vector.tensor_tensor(z[:, t, :], z[:, t, :], ssn, ALU.mult))

            def transpose(k, half):
                t, kind = items[k]
                if kind == 2:
                    return
                V.need(nc.tensor, out_at[k][1])
                if evac:
                    V.need(nc.tensor, evac[-1])
                else:
                    A.need(nc.tensor, zc)
                for m in range(4):
                    b = half * 4 + m
                    last = nc.tensor.transpose(ps[:, 7, m * P:(m + 1) * P], qk[:, kind, b * P:(b + 1) * P], ident)
                turned[k] = T.did(last)
                if kind == 0 and half == 0:
                    nc.vector.wait_ge(out_qk, c * 64 * TILES + (t + 1) * 64)
                    nc.scalar.wait_ge(out_qk, c * 64 * TILES + (t + 1) * 64)
                T.need(nc.scalar, turned[k])
                wn = (wqn, wkn)[kind]
                view = ps[:, 7, :].rearrange("p (m i) -> p m i", i=P)
                to = slice(half * 4, half * 4 + 4)
                hi = A.did(nc.scalar.activation(high[:, kind, to, :], view, ACT.Copy, scale=wn[:, 0:1]))
                A.need(nc.vector, hi)
                evac.append(V.did(nc.vector.scalar_tensor_tensor(low[:, kind, to, :], view, wn[:, 0:1],
                                                                 high[:, kind, to, :].bitcast(F32), ALU.mult, ALU.subtract)))
                if kind == 1 and half == 1:
                    V.need(nc.sync, evac[-1])
                    for n, name in enumerate(("q1", "k1")):
                        for part, buf in enumerate((high, low)):
                            nc.sync.dma_start(scr[name][part, :, at][:, t * P:(t + 1) * P].rearrange("(k p) i -> p k i", p=P),
                                              buf[:, n, :, :].bitcast(F32)).then_inc(out_qk, 16)

            reduced = []
            for k in range(len(items) + 1):
                normed = k < len(items) and items[k][1] < 2
                if k < len(items):
                    multiply(k)
                yield
                if k:
                    transpose(k - 1, 0)
                if normed:
                    reduce(k)
                yield
                if normed:
                    root(k)
                yield
                if k:
                    transpose(k - 1, 1)
                if normed:
                    scale(k)
                yield

        def gates(c, T, V, A):
            at = bass.ds(c * CHUNK, CHUNK)
            V.need(nc.vector, V.n)
            z1 = V.did(nc.vector.scalar_tensor_tensor(zabs[:, :, :], z[:, :, :], -1.0, z[:, :, :], ALU.mult, ALU.max))
            V.need(nc.scalar, z1)
            A.did(nc.scalar.activation(zabs[:, :, :], zabs[:, :, :], ACT.Exp, scale=-1.0))
            A.need(nc.scalar, A.n)
            ln = A.did(nc.scalar.activation(zabs[:, :, :], zabs[:, :, :], ACT.Ln, bias=1.0))
            yield
            A.need(nc.vector, ln)
            V.did(nc.vector.scalar_tensor_tensor(g[:, :, :], z[:, :, :], 0.0, zabs[:, :, :], ALU.max, ALU.add))
            V.need(nc.vector, V.n)
            V.did(nc.vector.tensor_tensor(g[:, :, :], g[:, :, :], om[:, :].unsqueeze(1).to_broadcast([P, TILES, heads]), ALU.mult))
            V.need(nc.vector, V.n)
            nc.vector.wait_ge(j_in, c * 16 + 16)
            V.did(nc.vector.tensor_tensor(gj[:, :, :], g[:, :, :], jpos[:, :].unsqueeze(2).to_broadcast([P, TILES, heads]), ALU.mult))
            V.did(nc.vector.tensor_copy(aug[:, :, 0, :], g[:, :, :]))
            V.need(nc.vector, V.n)
            V.did(nc.vector.tensor_copy(aug[:, :, 2, :], gj[:, :, :]))
            V.did(nc.vector.tensor_tensor(aug[:, :, 1, :], g[:, :, :], aug[:, :, 0, :].bitcast(F32), ALU.subtract))
            V.need(nc.vector, V.n)
            ag = V.did(nc.vector.tensor_tensor(aug[:, :, 3, :], gj[:, :, :], aug[:, :, 2, :].bitcast(F32), ALU.subtract))
            yield
            V.need(nc.tensor, ag)
            for t in range(TILES):
                last = nc.tensor.transpose(ps[:, 3, t * P:(t + 1) * P],
                                           aug[:, t, :, :].rearrange("p a h -> p (a h)").bitcast(F32), ident)
            tr = T.did(last)
            T.need(nc.scalar, tr)
            nc.scalar.wait_ge(out_g, c * 16 + 16)
            at_ = A.did(nc.scalar.activation(augT[:, :], ps[0:4 * heads, 3, :], ACT.Copy))
            A.need(nc.sync, at_)
            nc.sync.dma_start(scr["g1"][:, at], augT[:, :]).then_inc(out_g, 16)
            yield

        def beside(c, T, V, A, more):
            yield from ending(c - 1, T, V, A)
            yield from after(c - 1, T, V, A)
            last = [gates(c - 1, T, V, A)] + ([before(c + 1, T, V, A)] if more else [])
            while last:
                last = [stream for stream in last if next(stream, "end") != "end"]
                yield

        def step(c, T, V, A, side, n_side, more):
            if more:
                load(c + 1, T, V, A)
            interleave(moe(T, V, A), side, MOE_YIELDS, n_side)
            handover(T, V, A)

        MOE_YIELDS, SIDE_YIELDS, PREPARE_YIELDS = 8 * experts, 60, 20
        lanes = lambda tag, t, v, a: (Lane(nc, nc.tensor, f"m{tag}_T", t), Lane(nc, nc.vector, f"m{tag}_V", v), Lane(nc, nc.scalar, f"m{tag}_A", a))
        first = lanes("f", 0, 0, 0)
        fetch(first_weights, w_first)
        load(0, *first)
        fetch(expert_weights, w_expert)
        fetch(other_weights, w_rest)
        dve(nc.vector.memset(eps[:, :], EPS))
        dve(nc.vector.memset(acc[:, :, :], 0.0))
        nc.scalar.wait_ge(s0, dv[0])
        for engine in (nc.tensor, nc.vector):
            engine.wait_ge(w_first, 16 * len(first_weights))
        at_once(before(0, *first))
        for engine in (nc.tensor, nc.vector, nc.scalar):
            engine.wait_ge(w_expert, 16 * len(expert_weights))
        handover(*first)
        step(0, *first, chain(prepare(), before(1, *first)), PREPARE_YIELDS, True)
        barrier(nc)
        T, V, A = lanes("l", PER["T"], PER["V"], PER["A"])
        with nc.Fori(1, steps - 1) as it:
            for lane in (T, V, A):
                lane.begin(it - 1)
            for e in (nc.sync, nc.tensor, nc.vector, nc.scalar):
                for lane in (T, V, A):
                    if lane.engine is not e:
                        lane.need(e, 0)
            step(it, T, V, A, beside(it, T, V, A, True), SIDE_YIELDS, True)
        settle(T, V, A)
        barrier(nc)
        final_lanes = lanes("e", 0, 0, 0)
        step(steps - 1, *final_lanes, beside(steps - 1, *final_lanes, False), SIDE_YIELDS, False)
        for part in (ending, after, gates):
            at_once(part(steps - 1, *final_lanes))
        nc.sync.wait_ge(out_x, 16 * (steps + 1))
        nc.sync.wait_ge(out_g, 16 * (steps + 1))
        nc.sync.wait_ge(out_v, 16 * (steps * TILES + 1))
        nc.sync.wait_ge(out_qk, 64 * (steps * TILES + 1))
        barrier(nc)


def final(nc, ps, const, ins, scr, result, tokens, hidden, kc):
    PER = {"T": 19, "V": 36, "A": 15}
    FC = hidden // P
    with ExitStack() as ctx:
        wp = sbuf(nc, ctx, "fwp", [P, kc, P])
        w1, w2 = sbuf(nc, ctx, "fw1", [P, hidden]), sbuf(nc, ctx, "fw2", [P, hidden])
        h1, h2 = sbuf(nc, ctx, "fh1", [P, FC, hidden]), sbuf(nc, ctx, "fh2", [P, FC, hidden])
        w3, s3 = sbuf(nc, ctx, "fw3", [P, FC, P]), sbuf(nc, ctx, "fs3", [P, P])
        sc = sbuf(nc, ctx, "fsc", [P, 4, FC])
        eps, spare = sbuf(nc, ctx, "feps", [P, 1]), sbuf(nc, ctx, "fspare", [P, 1])
        y, x = sbuf(nc, ctx, "fy", [P, kc, CHUNK]), sbuf(nc, ctx, "fx", [P, TILES, P])
        r, x3n, x3, x3l, res = (sbuf(nc, ctx, f"f{n}", [P, TILES, P]) for n in ("r", "x3n", "x3", "x3l", "res"))
        xT, xTn = sbuf(nc, ctx, "fxT", [P, CHUNK]), sbuf(nc, ctx, "fxTn", [P, CHUNK])
        ha, hb, hc, hd = (sbuf(nc, ctx, f"f{n}", [P, FC, CHUNK]) for n in ("ha", "hb", "hc", "hd"))
        stats, mv, rstd = sbuf(nc, ctx, "fst", [P, TILES, 6]), sbuf(nc, ctx, "fmv", [P, TILES, 2]), sbuf(nc, ctx, "frs", [P, TILES])
        wp_in, w_in, c_in, out, s0 = (nc.alloc_semaphore(f"f_{n}") for n in ("wp_in", "w_in", "c_in", "out", "s0"))
        weights = [(w1[:, :], ins["fw1"]), (w2[:, :], ins["fw2"]), (sc[:, :, :], ins["fsc"]), (h1[:, :, :], ins["fh1"]),
                   (h2[:, :, :], ins["fh2"]), (w3[:, :, :], ins["fw3"]), (s3[:, :], ins["fs3"].partition_broadcast(P))]
        nc.sync.dma_start(wp[:, :, :], ins["wproj"]).then_inc(wp_in, 16)
        nc.tensor.wait_ge(wp_in, 16)
        nc.vector.memset(eps[:, :], EPS).then_inc(s0, 1)
        nc.scalar.wait_ge(s0, 1)
        nc.sync.sem_inc(out, 16)
        ident = const["ident"][:, :]
        steps = tokens // CHUNK

        def tiled(view):
            return view.rearrange("p (t d) -> p t d", d=P)

        def load(c, T, V, A):
            at = bass.ds(c * CHUNK, CHUNK)
            for lane in (T, V, A):
                lane.need(nc.sync, lane.n)
            nc.sync.dma_start(y[:, :, :], scr["y1"][:, at].rearrange("(k p) n -> p k n", p=P)).then_inc(c_in, 16)
            nc.sync.dma_start(x[:, :, :], scr["x2"][at, :].rearrange("(t p) d -> p t d", p=P)).then_inc(c_in, 16)

        def before(c, T, V, A):
            V.need(nc.tensor, V.n)
            A.need(nc.tensor, A.n)
            nc.tensor.wait_ge(c_in, c * 32 + 32)
            nc.vector.wait_ge(c_in, c * 32 + 32)
            for t in range(TILES):
                for k in range(kc):
                    last = nc.tensor.matmul(ps[:, 6, t * P:(t + 1) * P], y[:, k, t * P:(t + 1) * P], wp[:, k, :],
                                            start=k == 0, stop=k == kc - 1)
                if t < TILES - 1:
                    yield
            pr = T.did(last)
            T.need(nc.vector, pr)
            V.did(nc.vector.tensor_tensor(r[:, :, :], tiled(ps[:, 6, :]), x[:, :, :], ALU.add))
            n3 = yield from layernorm(nc, V, A, r, x3n, stats, mv, rstd, eps, spare, V.n)
            yield
            yield
            V.need(nc.tensor, n3)
            turn(nc, T, A, x3n, ps[:, 7, :], xTn, ident)
            yield

        def network(T, V, A):
            ring = []

            def bank():
                if len(ring) >= 4:
                    lane, n = ring[-4]
                    lane.need(nc.tensor, n)
                return ps[:, len(ring) % 4, :]

            V.need(nc.tensor, V.n)
            A.need(nc.tensor, A.n)
            for f in range(FC):
                b = bank()
                n = T.did(nc.tensor.matmul(b, w1[:, f * P:(f + 1) * P], xT[:, :], start=True, stop=True))
                T.need(nc.scalar, n)
                m = A.did(nc.scalar.activation(ha[:, f, :], b, ACT.Silu, scale=sc[:, 0, f:f + 1]))
                ring.append((A, m))
                yield
                b = bank()
                n = T.did(nc.tensor.matmul(b, w2[:, f * P:(f + 1) * P], xT[:, :], start=True, stop=True))
                T.need(nc.vector, n)
                A.need(nc.vector, m)
                ring.append((V, V.did(nc.vector.scalar_tensor_tensor(hb[:, f, :], b, sc[:, 1, f:f + 1], ha[:, f, :], ALU.mult, ALU.mult))))
                yield
            for w, src, dst, row in ((h1, hb, hc, 2), (h2, hc, hd, 3)):
                for o in range(FC):
                    b = bank()
                    for k in range(FC):
                        if o == 0:
                            lane, n = ring[2 * k + 1] if row == 2 else ring[2 * FC + k]
                            lane.need(nc.tensor, n)
                        last = nc.tensor.matmul(b, w[:, k, o * P:(o + 1) * P], src[:, k, :], start=k == 0, stop=k == FC - 1)
                        if k % 2 and k < FC - 1:
                            yield
                    n = T.did(last)
                    T.need(nc.scalar, n)
                    ring.append((A, A.did(nc.scalar.activation(dst[:, o, :], b, ACT.Gelu, scale=sc[:, row, o:o + 1]))))
                    yield

        def handover(T, V, A):
            for lane in (A, T, V):
                lane.need(nc.vector, lane.n)
            V.did(nc.vector.tensor_copy(x3l[:, :, :], x3[:, :, :]))
            V.need(nc.vector, V.n)
            V.did(nc.vector.tensor_copy(x3[:, :, :], x3n[:, :, :]))
            V.did(nc.vector.tensor_copy(xT[:, :], xTn[:, :]))

        def after(c, T, V, A):
            V.need(nc.tensor, V.n)
            A.need(nc.tensor, A.n)
            for t in range(TILES):
                for k in range(FC):
                    last = nc.tensor.matmul(ps[:, 5, t * P:(t + 1) * P], hd[:, k, t * P:(t + 1) * P], w3[:, k, :], start=k == 0, stop=k == FC - 1)
                if t % 2 and t < TILES - 1:
                    yield
            pr = T.did(last)
            yield
            T.need(nc.vector, pr)
            V.need(nc.vector, V.n)
            V.did(nc.vector.tensor_tensor(r[:, :, :], tiled(ps[:, 5, :]), s3[:, :].unsqueeze(1).to_broadcast([P, TILES, P]), ALU.mult))
            V.need(nc.vector, V.n)
            V.did(nc.vector.tensor_tensor(r[:, :, :], r[:, :, :], x3l[:, :, :], ALU.add))
            nc.vector.wait_ge(out, c * 16 + 16)
            n4 = yield from layernorm(nc, V, A, r, res, stats, mv, rstd, eps, spare, V.n)
            V.need(nc.sync, n4)
            nc.sync.dma_start(result[bass.ds(c * CHUNK, CHUNK), :].rearrange("(t p) d -> p t d", p=P), res[:, :, :]).then_inc(out, 16)
            yield

        def step(c, T, V, A, last_post, next_pre):
            if next_pre:
                load(c + 1, T, V, A)
            side = chain(*([after(c - 1, T, V, A)] if last_post else []), *([before(c + 1, T, V, A)] if next_pre else []))
            interleave(network(T, V, A), side, NETWORK_YIELDS, (AFTER_YIELDS if last_post else 0) + (BEFORE_YIELDS if next_pre else 0) + 1)
            handover(T, V, A)

        NETWORK_YIELDS, AFTER_YIELDS, BEFORE_YIELDS = 2 * FC + 4 * FC, 5, 8
        lanes = lambda tag, t, v, a: (Lane(nc, nc.tensor, f"f{tag}_T", t), Lane(nc, nc.vector, f"f{tag}_V", v), Lane(nc, nc.scalar, f"f{tag}_A", a))
        nc.vector.memset(x3[:, :, :], 0.0).then_inc(s0, 1)
        nc.vector.wait_ge(s0, 2)
        first = lanes("f", 0, 0, 0)
        load(0, *first)
        for d, source in weights:
            nc.sync.dma_start(d, source).then_inc(w_in, 16)
        for _ in before(0, *first):
            pass
        for engine in (nc.tensor, nc.vector, nc.scalar):
            engine.wait_ge(w_in, 16 * len(weights))
        handover(*first)
        step(0, *first, False, True)
        barrier(nc)
        T, V, A = lanes("l", PER["T"], PER["V"], PER["A"])
        with nc.Fori(1, steps - 1) as it:
            for lane in (T, V, A):
                lane.begin(it - 1)
            for e in (nc.sync, nc.tensor, nc.vector, nc.scalar):
                for lane in (T, V, A):
                    if lane.engine is not e:
                        lane.need(e, 0)
            step(it, T, V, A, True, True)
        settle(T, V, A)
        barrier(nc)
        final_lanes = lanes("e", 0, 0, 0)
        step(steps - 1, *final_lanes, True, False)
        for _ in after(steps - 1, *final_lanes):
            pass
        nc.sync.wait_ge(out, 16 * (steps + 1))


def build(nc, ins, result, B, S, upto=5):
    tokens = B * S
    H0, H1, DIM1 = 16, 16, 64
    D0 = P // H0
    ps = nc.alloc_psum_tensor("ps", [P, 8, BANK], F32)

    def scratch(name, shape):
        return nc.dram_tensor(name, shape, F32, kind="Internal").ap()

    scr = {"q0": scratch("s_q0", [2, P, tokens]), "k0": scratch("s_k0", [2, P, tokens]), "v0": scratch("s_v0", [tokens, 512]),
           "y0": scratch("s_y0", [512, tokens]), "x2": scratch("s_x2", [tokens, P]), "ku": scratch("s_ku", [H1, DIM1]),
           "q1": scratch("s_q1", [2, H1 * DIM1, tokens]), "k1": scratch("s_k1", [2, H1 * DIM1, tokens]),
           "v1": scratch("s_v1", [tokens, H1 * DIM1]), "g1": scratch("s_g1", [4 * H1, tokens]),
           "y1": scratch("s_y1", [H1 * DIM1, tokens]), "zero": scratch("s_zero", [4 * S])}

    with ExitStack() as ctx:
        const = {n: sbuf(nc, ctx, f"c_{n}", s, d) for n, s, d in (
            ("ident", [P, P], F32), ("identb", [P, P], BF16), ("mask_ji_add", [P, P], BF16), ("mask_ij", [P, BANK], BF16), ("mask_ji", [P, P], F32),
            ("ones", [P, 1], F32), ("zero", [P, BANK], F32), ("pick", [P, 4], F32))}
        c_in, c_set = nc.alloc_semaphore("c_in"), nc.alloc_semaphore("c_set")
        with ExitStack() as tmp:
            mask, mask_add, zero = sbuf(nc, tmp, "c_mask", [P, P]), sbuf(nc, tmp, "c_mask_add", [P, P]), sbuf(nc, tmp, "c_zero0", [1, 4 * S])
            for d, s in ((const["ident"], ins["ident"]), (mask, ins["mask_ij"]), (mask_add, ins["mask_ji_add"]), (const["mask_ji"], ins["mask_ji"]), (const["pick"], ins["pick"])):
                nc.sync.dma_start(d[:, :], s).then_inc(c_in, 16)
            nc.vector.memset(const["mask_ij"][:, :], 0.0).then_inc(c_set, 1)
            nc.vector.memset(const["zero"][:, :], 0.0).then_inc(c_set, 1)
            nc.vector.memset(const["ones"][:, :], 1.0).then_inc(c_set, 1)
            nc.vector.memset(zero[:, :], 0.0).then_inc(c_set, 1)
            nc.vector.wait_ge(c_in, 80)
            nc.vector.tensor_copy(const["identb"][:, :], const["ident"][:, :]).then_inc(c_set, 1)
            nc.vector.tensor_copy(const["mask_ji_add"][:, :], mask_add[:, :]).then_inc(c_set, 1)
            nc.vector.wait_ge(c_set, 1)
            nc.vector.tensor_copy(const["mask_ij"][:, BANK - P:BANK], mask[:, :]).then_inc(c_set, 1)
            nc.sync.wait_ge(c_set, 7)
            nc.sync.dma_start(scr["zero"].rearrange("(a n) -> a n", a=1), zero[:, :]).then_inc(c_in, 16)
            nc.sync.wait_ge(c_in, 96)
            barrier(nc)

        if upto >= 1:
            project0(nc, ps, const, ins, scr, tokens, H0)

        const["zeros"] = scr["zero"].rearrange("(h n) -> h n", n=S)[0:2, :]

        def batch(g, per):
            return g // per, g % per

        def head_rows(src, part, per, heads, dim):
            def of(g):
                b, m = batch(g, per)
                return src[part, bass.ds(m * (heads * dim), heads * dim), bass.ds(b * S, S)].rearrange("(h d) i -> d h i", d=dim)
            return of

        def values_of(src, per):
            def of(g):
                b, m = batch(g, per)
                return src[bass.ds(b * S, S), bass.ds(m * P, P)].rearrange("(t p) n -> p t n", p=P)
            return of

        def out_of(dst, per):
            def of(g, c):
                b, m = batch(g, per)
                return dst[bass.ds(m * P, P), bass.ds(b * S + c * BANK, BANK)]
            return of

        def zeros_for(heads):
            return lambda g: scr["zero"].rearrange("(a h n) -> a h n", a=1, n=S)[:, 0:heads, :]

        if upto >= 2:
            with ExitStack() as pos:
                p_in = nc.alloc_semaphore("a0_p_in")
                const["qpos"], const["kpos"] = sbuf(nc, pos, "c_qpos", [P, S]), sbuf(nc, pos, "c_kpos", [P, S])
                nc.sync.dma_start(const["qpos"][POS:P, :], ins["qpos"]).then_inc(p_in, 16)
                nc.sync.dma_start(const["kpos"][POS:P, :], ins["kpos0"]).then_inc(p_in, 16)
                nc.vector.wait_ge(p_in, 32)
                nc.scalar.wait_ge(p_in, 32)
                per = H0 // 4
                rows = [head_rows(scr["q0"], part, per, 4, D0) for part in range(2)]
                krows = [head_rows(scr["k0"], part, per, 4, D0) for part in range(2)]
                attention(nc, ps, const, "a0",
                          [((0, 8), rows[0]), ((8, 16), rows[0]), ((16, 24), rows[1])], None,
                          [((0, 8), krows[0]), ((8, 16), krows[1]), ((16, 24), krows[0])], None,
                          [(False, (MAXROW, MAXROW + 1), zeros_for(4))], values_of(scr["v0"], per), out_of(scr["y0"], per), B * per, 4, S)

        if upto >= 3:
            middle(nc, ps, const, ins, scr, tokens, 8, 512, H1, DIM1)

        if upto >= 4:
            with ExitStack() as pos:
                p_in = nc.alloc_semaphore("a1_p_in")
                const["qpos"], const["kpos"] = sbuf(nc, pos, "c_qpos1", [P, S]), sbuf(nc, pos, "c_kpos1", [P, S])
                nc.sync.dma_start(const["qpos"][POS:P, :], ins["qpos"]).then_inc(p_in, 16)
                nc.sync.dma_start(const["kpos"][POS:P, :], ins["kpos1"]).then_inc(p_in, 16)
                nc.vector.wait_ge(p_in, 32)
                nc.scalar.wait_ge(p_in, 32)
                per = H1 // 2
                q = [head_rows(scr["q1"], part, per, 2, DIM1) for part in range(2)]
                k = [head_rows(scr["k1"], part, per, 2, DIM1) for part in range(2)]

                def slopes_of(g):
                    b, m = batch(g, per)
                    return scr["g1"].rearrange("(a h) n -> a h n", a=4)[:, bass.ds(m * 2, 2), bass.ds(b * S, S)]

                attention(nc, ps, const, "a1", [((0, 64), q[0])], [((0, 64), q[0]), ((64, 128), q[1])],
                          [((0, 64), k[0])], [((0, 64), k[1]), ((64, 128), k[0])],
                          [(True, (POS, POS + 4), slopes_of), (False, (MAXROW, MAXROW + 1), zeros_for(2))],
                          values_of(scr["v1"], per), out_of(scr["y1"], per), B * per, 2, S)

        if upto >= 5:
            final(nc, ps, const, ins, scr, result, tokens, 512, H1 * DIM1 // P)


def layout(a):
    f = np.float32
    x = a["L0_attn_x"]
    B, S, _ = x.shape
    E, _, F = a["L0_ffn_W1"].shape
    C = np.ascontiguousarray
    o = {"x": x.reshape(B * S, P)}
    o["wq0"], o["wk0"] = C(a["L0_attn_Wq"].T), C(a["L0_attn_Wk"].T)
    o["bq0"], o["bk0"] = a["L0_attn_bq"].reshape(P, 1), a["L0_attn_bk"].reshape(P, 1)
    wv = np.zeros((P, 16, 32), f)
    wv[:, :, 0:8] = a["L0_attn_Wv"].T.reshape(P, 16, 8)
    bv = np.zeros((16, 32), f)
    bv[:, 0:8] = a["L0_attn_bv"].reshape(16, 8)
    bv[:, 8] = 1.0
    o["wv0"], o["bv0"] = wv.reshape(P, 512), bv.reshape(512)
    wo = np.zeros((16, 32, P), f)
    wo[:, 0:8] = a["L0_attn_Wo"].T.reshape(16, 8, P)
    o["wo0"] = C(wo.reshape(4, P, P).transpose(1, 0, 2))
    o["bo0"] = a["L0_attn_bo"]
    o["cent"] = C(a["L0_ffn_centroids"].T)
    o["ln_g"], o["ln_b"] = C(a["L0_ffn_ln_g"].T), C(a["L0_ffn_ln_b"].T)
    o["w1"] = C(a["L0_ffn_W1"].transpose(1, 0, 2))
    o["b1"] = C(a["L0_ffn_b1"].reshape(E, F // P, P).transpose(2, 0, 1))
    o["w2"] = C(a["L0_ffn_W2"].reshape(E, F // P, P, P).transpose(2, 0, 1, 3))
    o["b2"] = a["L0_ffn_b2"]
    o["wq1"], o["wk1"], o["wv1"] = a["L1_attn_Wq"], a["L1_attn_Wk"], a["L1_attn_Wv"]
    o["wproj"] = C(a["L1_attn_Wproj"].reshape(8, P, P).transpose(1, 0, 2))
    o["qn"] = np.concatenate([a["L1_attn_q_rms_w"]] * 2).reshape(P, 1)
    o["kn"] = np.concatenate([a["L1_attn_k_rms_w"]] * 2).reshape(P, 1)
    o["kn_row"], o["u"], o["omega"] = a["L1_attn_k_rms_w"], a["L1_attn_u"], a["L1_attn_omega"]
    o["fw1"], o["fw2"] = C(a["L1_ffn_w1_w"].T), C(a["L1_ffn_w2_w"].T)
    o["fh1"] = C(a["L1_ffn_h1_w"].T.reshape(4, P, 512).transpose(1, 0, 2))
    o["fh2"] = C(a["L1_ffn_h2_w"].T.reshape(4, P, 512).transpose(1, 0, 2))
    o["fw3"] = C(a["L1_ffn_w3_w"].T.reshape(4, P, P).transpose(1, 0, 2))
    o["fs3"] = a["L1_ffn_w3_s"]
    o["fsc"] = C(np.stack([a[f"L1_ffn_{n}_s"].reshape(4, P) for n in ("w1", "w2", "h1", "h2")]).transpose(2, 0, 1))
    o["ident"] = np.eye(P, dtype=f)
    upper = np.triu(np.ones((P, P), f), 1)
    o["mask_ij"] = upper * f(MASKED)
    o["mask_ji_add"] = upper.T * f(MASKED)
    o["mask_ji"] = np.where(upper.T > 0, f(MASKED), -f(LOWEST))
    pos = np.arange(S, dtype=f) - f(S // 2)
    q = np.zeros((P - POS, S), f)
    q[0] = q[1] = -pos
    q[2] = q[3] = 1.0
    k0 = np.zeros((P - POS, S), f)
    k0[0], k0[2], k0[MAXROW - POS] = 1.0, pos, 1.0
    k1 = np.zeros((P - POS, S), f)
    k1[MAXROW - POS] = 1.0
    o["qpos"], o["kpos0"], o["kpos1"] = q, k0, k1
    o["jpos"] = C(np.tile(pos, B).reshape(B * S // CHUNK, TILES, P).transpose(0, 2, 1))
    o["slopes"] = np.array([2.0 ** (-(n + 1) / 2) for n in range(16)], f)
    o["iota"] = np.tile(np.arange(E, dtype=f) - E, (TILES, 1))
    o["pick"] = np.zeros((P, 4), f)
    for n in range(4):
        o["pick"][32 * n + 8, n] = 1.0
    return o, B, S


def kernel(**inputs):
    import concourse.bacc as bacc
    from concourse.bass_utils import run_bass_kernel_spmd

    arrays, B, S = layout({k: np.asarray(v) for k, v in inputs.items()})
    nc = bacc.Bacc("TRN2", target_bir_lowering=False, num_devices=1)
    given, ins = {}, {}
    for name, a in arrays.items():
        given[f"in_{name}"] = np.ascontiguousarray(a)
        ins[name] = nc.dram_tensor(f"in_{name}", a.shape, mybir.dt.from_np(a.dtype), kind="ExternalInput").ap()
    result = nc.dram_tensor("out_0", (B * S, P), F32, kind="ExternalOutput").ap()
    build(nc, ins, result, B, S)
    r = run_bass_kernel_spmd(nc, [given], core_ids=[0])
    return r.results[0]["out_0"].reshape(B, S, P)
```
